# Optimizing a Trainium2 kernel written in Bass

```python
import numpy as np
import jax
import jax.numpy as jnp

def _softmax(x, axis=-1):
    return jax.nn.softmax(x, axis=axis)

def _gelu(x):
    return jax.nn.gelu(x, approximate=True)

def _silu(x):
    return jax.nn.silu(x)

def _sigmoid(x):
    return jax.nn.sigmoid(x)

def _layernorm(x, axis=-1, eps=1e-05):
    m = jnp.mean(x, axis=axis, keepdims=True)
    v = jnp.var(x, axis=axis, keepdims=True)
    return (x - m) / jnp.sqrt(v + eps)

def _scatter_add(tgt, idx, src, axis=0):
    return tgt.at[idx].add(src)

def _segment_sum(src, seg, n):
    return jax.ops.segment_sum(src, seg, n)
kernel_name = 'mk_vit_tower_postln_d2_tok_img1024_r4_68bce4'

def setup_inputs(seed: int=0):
    np.random.seed(seed)
    _w = jnp.asarray

    def _rec_inputs():
        import jax
        import jax.numpy as jnp
        _rk = jax.random.key(seed)
        x = -4.65018e-05 + 0.999886 * jax.random.normal(jax.random.fold_in(_rk, 1), (16, 3, 96, 96), jnp.float32)
        return x
    x = _rec_inputs()

    def _L0_tok_setup():
        import jax, jax.numpy as jnp
        import numpy as np
        P = 16
        key = jax.random.key(seed)
        k1, k2, k3 = jax.random.split(key, 3)
        B, C, H, W_ = (64, 3, 128, 128)
        D = 256
        x = jax.random.normal(k1, (B, C, H, W_), dtype=jnp.float32)
        W = jax.random.normal(k2, (C * P * P, D), dtype=jnp.float32) * (1.0 / np.sqrt(C * P * P))
        b = jax.random.normal(k3, (D,), dtype=jnp.float32) * 0.01
        return {'x': x, 'W': W, 'b': b}
    _L0_tok_all = _L0_tok_setup()
    _L0_tok_in = {k: v for k, v in _L0_tok_all.items() if k in ('W', 'b')}
    del _L0_tok_all

    def _L0_attn_setup():
        import jax, jax.numpy as jnp
        import numpy as np
        import math
        NUM_BUCKETS = 32
        MAX_DISTANCE = 128
        HEADS = 16
        D_MODEL = 256

        def _relative_position_bucket(rel_pos, num_buckets=NUM_BUCKETS, max_distance=MAX_DISTANCE):
            n = jnp.maximum(-rel_pos, 0)
            max_exact = num_buckets // 2
            is_small = n < max_exact
            val_large = max_exact + (jnp.log(jnp.maximum(n, 1).astype(jnp.float32) / max_exact) / math.log(max_distance / max_exact) * (num_buckets - max_exact)).astype(jnp.int32)
            val_large = jnp.minimum(val_large, num_buckets - 1)
            return jnp.where(is_small, n, val_large)
        key = jax.random.key(seed)
        ks = jax.random.split(key, 7)
        d = D_MODEL
        s = 1.0 / math.sqrt(d)
        x = jax.random.normal(ks[0], (2, 512, d), dtype=jnp.float32)
        Wq = jax.random.normal(ks[1], (d, d), dtype=jnp.float32) * s
        Wk = jax.random.normal(ks[2], (d, d), dtype=jnp.float32) * s
        Wv = jax.random.normal(ks[3], (d, d), dtype=jnp.float32) * s
        Wo = jax.random.normal(ks[4], (d, d), dtype=jnp.float32) * s
        bo = jnp.zeros((d,), dtype=jnp.float32)
        rel_emb = jax.random.normal(ks[5], (NUM_BUCKETS, HEADS), dtype=jnp.float32) * 0.02
        return {'x': x, 'Wq': Wq, 'Wk': Wk, 'Wv': Wv, 'Wo': Wo, 'bo': bo, 'rel_emb': rel_emb}
    _L0_attn_all = _L0_attn_setup()
    _L0_attn_in = {k: v for k, v in _L0_attn_all.items() if k in ('Wq', 'Wk', 'Wv', 'Wo', 'bo', 'rel_emb')}
    del _L0_attn_all

    def _L0_ffn_setup():
        import jax, jax.numpy as jnp
        import numpy as np
        D = 256
        I = 128
        E = 32
        K = 4
        T = 2 * 512
        C = 2 * T * K // E
        key = jax.random.key(seed)
        ks = jax.random.split(key, 9)
        bf = jnp.bfloat16
        std = 0.02
        x = jax.random.normal(ks[0], (2, 512, D), dtype=jnp.float32).astype(bf)
        gate_w = (std * jax.random.normal(ks[1], (E, D), dtype=jnp.float32)).astype(bf)
        bias = jnp.zeros((E,), jnp.float32)
        W1 = (std * jax.random.normal(ks[2], (E, D, I), dtype=jnp.float32)).astype(bf)
        W3 = (std * jax.random.normal(ks[3], (E, D, I), dtype=jnp.float32)).astype(bf)
        W2 = (std * jax.random.normal(ks[4], (E, I, D), dtype=jnp.float32)).astype(bf)
        sw1 = (std * jax.random.normal(ks[5], (I, D), dtype=jnp.float32)).astype(bf)
        sw3 = (std * jax.random.normal(ks[6], (I, D), dtype=jnp.float32)).astype(bf)
        sw2 = (std * jax.random.normal(ks[7], (D, I), dtype=jnp.float32)).astype(bf)
        return {'x': x, 'gate_w': gate_w, 'bias': bias, 'W1': W1, 'W3': W3, 'W2': W2, 'sw1': sw1, 'sw3': sw3, 'sw2': sw2}
    _L0_ffn_all = _L0_ffn_setup()
    _L0_ffn_in = {k: v for k, v in _L0_ffn_all.items() if k in ('gate_w', 'bias', 'W1', 'W3', 'W2', 'sw1', 'sw3', 'sw2')}
    del _L0_ffn_all

    def _L1_attn_setup():
        import jax, jax.numpy as jnp
        import numpy as np
        B, C, D_MODEL, N_HEADS = (2, 512, 256, 16)

        def rotary_matrix(context_length: int, d: int) -> jnp.ndarray:
            half = d // 2
            i = jnp.arange(half, dtype=jnp.float32)
            theta = 10000.0 ** (-2.0 * (i - 1.0) / d)
            m = jnp.arange(context_length, dtype=jnp.float32)
            ang = m[:, None] * theta
            c, s = (jnp.cos(ang), jnp.sin(ang))
            ev = 2 * jnp.arange(half)
            od = ev + 1
            R = jnp.zeros((context_length, d, d), jnp.float32)
            R = R.at[:, ev, ev].set(c)
            R = R.at[:, ev, od].set(-s)
            R = R.at[:, od, ev].set(s)
            R = R.at[:, od, od].set(c)
            return R
        key = jax.random.key(seed)
        k1, k2, k3, k4 = jax.random.split(key, 4)
        x = jax.random.normal(k1, (B, C, D_MODEL), dtype=jnp.float32)
        w_qkv = jax.random.normal(k2, (3 * D_MODEL, D_MODEL), dtype=jnp.float32) * 0.02
        w_out = jax.random.normal(k3, (D_MODEL, D_MODEL), dtype=jnp.float32) * 0.02
        b_out = jax.random.normal(k4, (D_MODEL,), dtype=jnp.float32) * 0.02
        return {'x': x, 'w_qkv': w_qkv, 'w_out': w_out, 'b_out': b_out}
    _L1_attn_all = _L1_attn_setup()
    _L1_attn_in = {k: v for k, v in _L1_attn_all.items() if k in ('w_qkv', 'w_out', 'b_out')}
    del _L1_attn_all

    def _L1_ffn_setup():
        import jax, jax.numpy as jnp
        import numpy as np
        T, Z, D_DIM = (8, 512, 256)
        N_EXP, P_SLOT, H = (64, 32, 256)
        LN_EPS = 1e-05
        key = jax.random.key(seed)
        k = jax.random.split(key, 5)
        s = 0.02
        return {'x': jax.random.normal(k[0], (T, Z, D_DIM), dtype=jnp.float32), 'phi_w': jax.random.normal(k[1], (N_EXP * P_SLOT, D_DIM), dtype=jnp.float32) * s, 'phi_b': jax.random.normal(k[2], (N_EXP * P_SLOT,), dtype=jnp.float32) * s, 'expert_w': jax.random.normal(k[3], (N_EXP, D_DIM, H), dtype=jnp.float32) * s, 'expert_b': jax.random.normal(k[4], (N_EXP, H), dtype=jnp.float32) * s}
    _L1_ffn_all = _L1_ffn_setup()
    _L1_ffn_in = {k: v for k, v in _L1_ffn_all.items() if k in ('phi_w', 'phi_b', 'expert_w', 'expert_b')}
    del _L1_ffn_all
    return {'x': x, 'L0_tok_W': _L0_tok_in['W'], 'L0_tok_b': _L0_tok_in['b'], 'L0_attn_Wq': _L0_attn_in['Wq'], 'L0_attn_Wk': _L0_attn_in['Wk'], 'L0_attn_Wv': _L0_attn_in['Wv'], 'L0_attn_Wo': _L0_attn_in['Wo'], 'L0_attn_bo': _L0_attn_in['bo'], 'L0_attn_rel_emb': _L0_attn_in['rel_emb'], 'L0_ffn_gate_w': _L0_ffn_in['gate_w'], 'L0_ffn_bias': _L0_ffn_in['bias'], 'L0_ffn_W1': _L0_ffn_in['W1'], 'L0_ffn_W3': _L0_ffn_in['W3'], 'L0_ffn_W2': _L0_ffn_in['W2'], 'L0_ffn_sw1': _L0_ffn_in['sw1'], 'L0_ffn_sw3': _L0_ffn_in['sw3'], 'L0_ffn_sw2': _L0_ffn_in['sw2'], 'L1_attn_w_qkv': _L1_attn_in['w_qkv'], 'L1_attn_w_out': _L1_attn_in['w_out'], 'L1_attn_b_out': _L1_attn_in['b_out'], 'L1_ffn_phi_w': _L1_ffn_in['phi_w'], 'L1_ffn_phi_b': _L1_ffn_in['phi_b'], 'L1_ffn_expert_w': _L1_ffn_in['expert_w'], 'L1_ffn_expert_b': _L1_ffn_in['expert_b']}

def reference(x, L0_tok_W, L0_tok_b, L0_attn_Wq, L0_attn_Wk, L0_attn_Wv, L0_attn_Wo, L0_attn_bo, L0_attn_rel_emb, L0_ffn_gate_w, L0_ffn_bias, L0_ffn_W1, L0_ffn_W3, L0_ffn_W2, L0_ffn_sw1, L0_ffn_sw3, L0_ffn_sw2, L1_attn_w_qkv, L1_attn_w_out, L1_attn_b_out, L1_ffn_phi_w, L1_ffn_phi_b, L1_ffn_expert_w, L1_ffn_expert_b):
    import jax
    import jax.numpy as jnp

    def _L0_tok_ref(x, W, b):
        import jax, jax.numpy as jnp
        import numpy as np
        P = 16
        B, C, H, W_ = x.shape
        nh, nw = (H // P, W_ // P)
        patches = x.reshape(B, C, nh, P, nw, P)
        patches = patches.transpose(0, 2, 4, 1, 3, 5)
        patches = patches.reshape(B, nh * nw, C * P * P)
        return jnp.einsum('bnk,kd->bnd', patches, W) + b

    def _L0_attn_ref(x, Wq, Wk, Wv, Wo, bo, rel_emb):
        import jax, jax.numpy as jnp
        import numpy as np
        import math
        NUM_BUCKETS = 32
        MAX_DISTANCE = 128
        HEADS = 16
        D_MODEL = 256

        def _relative_position_bucket(rel_pos, num_buckets=NUM_BUCKETS, max_distance=MAX_DISTANCE):
            n = jnp.maximum(-rel_pos, 0)
            max_exact = num_buckets // 2
            is_small = n < max_exact
            val_large = max_exact + (jnp.log(jnp.maximum(n, 1).astype(jnp.float32) / max_exact) / math.log(max_distance / max_exact) * (num_buckets - max_exact)).astype(jnp.int32)
            val_large = jnp.minimum(val_large, num_buckets - 1)
            return jnp.where(is_small, n, val_large)
        b, n, d = x.shape
        h = HEADS
        dh = d // h
        scale = dh ** (-0.5)
        q = (x @ Wq).reshape(b, n, h, dh).transpose(0, 2, 1, 3)
        k = (x @ Wk).reshape(b, n, h, dh).transpose(0, 2, 1, 3)
        v = (x @ Wv).reshape(b, n, h, dh).transpose(0, 2, 1, 3)
        sim = jnp.einsum('bhid,bhjd->bhij', q, k) * scale
        pos = jnp.arange(n, dtype=jnp.int32)
        rel_pos = pos[None, :] - pos[:, None]
        buckets = _relative_position_bucket(rel_pos)
        bias = rel_emb[buckets]
        sim = sim + jnp.transpose(bias, (2, 0, 1))[None]
        mask_value = -jnp.finfo(sim.dtype).max
        causal_mask = jnp.triu(jnp.ones((n, n), dtype=bool), k=1)
        sim = jnp.where(causal_mask[None, None], mask_value, sim)
        attn = jax.nn.softmax(sim, axis=-1)
        out = jnp.einsum('bhij,bhjd->bhid', attn, v)
        out = out.transpose(0, 2, 1, 3).reshape(b, n, d)
        return out @ Wo + bo

    def _L0_ffn_ref(x, gate_w, bias, W1, W3, W2, sw1, sw3, sw2):
        import jax, jax.numpy as jnp
        import numpy as np
        D = 256
        I = 128
        E = 32
        K = 4
        T = 2 * 512
        C = 2 * T * K // E
        X = x.reshape(-1, D)
        logits = (X @ gate_w.T).astype(jnp.float32)
        scores = jax.nn.sigmoid(logits)
        _, idx = jax.lax.top_k(scores + bias[None, :], K)
        w = jnp.take_along_axis(scores, idx, axis=-1)
        w = w / jnp.clip(jnp.sum(w, axis=-1, keepdims=True), 1e-12, None)
        w = w.astype(x.dtype)
        eid = idx.reshape(-1)
        onehot = (eid[:, None] == jnp.arange(E)[None, :]).astype(jnp.int32)
        pos = jnp.take_along_axis(jnp.cumsum(onehot, axis=0) - 1, eid[:, None], axis=1)[:, 0]
        valid = pos < C
        posc = jnp.minimum(pos, C - 1)
        Xrep = jnp.repeat(X, K, axis=0)
        xe = jnp.zeros((E, C, D), x.dtype).at[eid, posc].add(jnp.where(valid[:, None], Xrep, jnp.zeros((), x.dtype)))
        h = jax.nn.silu(jnp.einsum('ecd,edi->eci', xe, W1)) * jnp.einsum('ecd,edi->eci', xe, W3)
        ye = jnp.einsum('eci,eid->ecd', h, W2)
        gflat = jnp.where(valid, w.reshape(-1), jnp.zeros((), x.dtype))
        yrows = ye[eid, posc] * gflat[:, None]
        out = yrows.reshape(-1, K, D).sum(axis=1)
        out = out + jax.nn.silu(X @ sw1.T) * (X @ sw3.T) @ sw2.T
        return out.reshape(x.shape)

    def _L1_attn_ref(x, w_qkv, w_out, b_out):
        import jax, jax.numpy as jnp
        import numpy as np
        B, C, D_MODEL, N_HEADS = (2, 512, 256, 16)

        def rotary_matrix(context_length: int, d: int) -> jnp.ndarray:
            half = d // 2
            i = jnp.arange(half, dtype=jnp.float32)
            theta = 10000.0 ** (-2.0 * (i - 1.0) / d)
            m = jnp.arange(context_length, dtype=jnp.float32)
            ang = m[:, None] * theta
            c, s = (jnp.cos(ang), jnp.sin(ang))
            ev = 2 * jnp.arange(half)
            od = ev + 1
            R = jnp.zeros((context_length, d, d), jnp.float32)
            R = R.at[:, ev, ev].set(c)
            R = R.at[:, ev, od].set(-s)
            R = R.at[:, od, ev].set(s)
            R = R.at[:, od, od].set(c)
            return R
        b, c, d = x.shape
        h = N_HEADS
        dh = d // h
        qkv = x @ w_qkv.T
        q, k, v = jnp.split(qkv, 3, axis=-1)
        q = q.reshape(b, c, h, dh).transpose(0, 2, 1, 3)
        k = k.reshape(b, c, h, dh).transpose(0, 2, 1, 3)
        v = v.reshape(b, c, h, dh).transpose(0, 2, 1, 3)
        R = rotary_matrix(c, dh)
        q_rot = jnp.einsum('bhci,cij->bhcj', q, R)
        k_rot = jnp.einsum('bhci,cij->bhcj', k, R)
        scale = jnp.sqrt(jnp.float32(dh))
        attn_num = jnp.exp(jnp.einsum('bhqd,bhkd->bhqk', q_rot, k_rot) / scale)
        attn_den = jnp.exp(jnp.einsum('bhqd,bhkd->bhqk', q, k) / scale)
        attn_den = jnp.sum(attn_den, axis=-1, keepdims=True)
        attn = attn_num / attn_den
        causal = jnp.tril(jnp.ones((c, c), jnp.float32))[None, None]
        attn = jnp.where(causal == 0, 0.0, attn)
        y = jnp.einsum('bhqk,bhkd->bhqd', attn, v)
        y = y.transpose(0, 2, 1, 3).reshape(b, c, d)
        return y @ w_out.T + b_out

    def _L1_ffn_ref(x, phi_w, phi_b, expert_w, expert_b):
        import jax, jax.numpy as jnp
        import numpy as np
        T, Z, D_DIM = (8, 512, 256)
        N_EXP, P_SLOT, H = (64, 32, 256)
        LN_EPS = 1e-05
        t, z, d = x.shape
        n = expert_w.shape[0]
        p = phi_w.shape[0] // n
        logits = (jnp.einsum('tzd,ed->tze', x, phi_w) + phi_b).reshape(t, z, n, p)
        D = jax.nn.softmax(logits, axis=3)
        C = jax.nn.softmax(logits, axis=2)
        X_tilde = jnp.einsum('tznp,tzd->npd', D, x)
        X_tilde = jnp.clip(X_tilde, -33000.0, 65000.0)
        mu = jnp.mean(X_tilde, axis=-1, keepdims=True)
        var = jnp.mean(jnp.square(X_tilde - mu), axis=-1, keepdims=True)
        X_tilde = (X_tilde - mu) * jax.lax.rsqrt(var + LN_EPS)
        X_tilde = jnp.tanh(X_tilde)
        Y_tilde = jnp.einsum('npd,ndH->npH', X_tilde, expert_w) + expert_b[:, None, :]
        Y = jnp.einsum('tznp,npH->tzH', C, Y_tilde)
        return Y
    h = _L0_tok_ref(x, L0_tok_W, L0_tok_b)
    h = _layernorm(h + _L0_attn_ref(h, L0_attn_Wq, L0_attn_Wk, L0_attn_Wv, L0_attn_Wo, L0_attn_bo, L0_attn_rel_emb), axis=-1)
    h = _layernorm(h + _L0_ffn_ref(h, L0_ffn_gate_w, L0_ffn_bias, L0_ffn_W1, L0_ffn_W3, L0_ffn_W2, L0_ffn_sw1, L0_ffn_sw3, L0_ffn_sw2), axis=-1)
    h = _layernorm(h + _L1_attn_ref(h, L1_attn_w_qkv, L1_attn_w_out, L1_attn_b_out), axis=-1)
    h = _layernorm(h + _L1_ffn_ref(h, L1_ffn_phi_w, L1_ffn_phi_b, L1_ffn_expert_w, L1_ffn_expert_b), axis=-1)
    return h

_drawn_inputs = setup_inputs


def setup_inputs(seed=0):
    import zlib

    import numpy as np

    out = dict(_drawn_inputs(seed))
    spreads = {'L0_attn_bo': (0.0, 0.1), 'L0_ffn_bias': (0.0, 0.8)}
    factors = {'L0_attn_rel_emb': 8.0,
     'L0_ffn_gate_w': 8.0,
     'L0_ffn_W1': 8.0,
     'L0_ffn_W3': 8.0,
     'L0_ffn_W2': 8.0,
     'L0_ffn_sw1': 5.369,
     'L0_ffn_sw3': 5.194,
     'L0_ffn_sw2': 5.195,
     'L1_ffn_phi_b': 25.664}
    for name, (base, spread) in spreads.items():
        noise = np.random.default_rng([zlib.crc32(name.encode()), seed]).standard_normal(out[name].shape)
        drawn = base * np.exp(spread * noise) if base else spread * noise
        out[name] = jnp.asarray(drawn.astype(out[name].dtype))
    for name, factor in factors.items():
        out[name] = (out[name] * factor).astype(out[name].dtype)
    return out
```

```python
from contextlib import ExitStack

import concourse.bass as bass
from concourse import mybir

ALU = mybir.AluOpType
ACT = mybir.ActivationFunctionType
AX = mybir.AxisListType
F32 = mybir.dt.float32
F16 = mybir.dt.float16
BF16 = mybir.dt.bfloat16
U32 = mybir.dt.uint32

P = 128
NIMG, SEQ = 16, 36
TOK = NIMG * SEQ
D = 256
KD = D // P
TILES = -(-TOK // P)
TPAD = TILES * P
LAST = TOK - (TILES - 1) * P
HEADS, DH = 16, 16
HH = HEADS // KD
GROUP = NIMG // 2
GT = GROUP * SEQ
SLOT = 64
PAIRS = NIMG // 2
PATCH_K = 768 // P
NEXP, TOPK, CAP = 32, 4, 256
CHUNKS = [(0, 256), (256, TOK - 256)]
SE, SP = 64, 32
NP_ = SE * SP
NPT = NP_ // P
HALF = NP_ // 2
EPS = 1e-5
SCALE = DH ** -0.5
MOE_W = 2 * KD * P + D
MOE_CHUNK = 3
EW_SLOTS = 32
EW_DMA = 2
BUCKETS = 32

CF = {}
CB = {}
_at = 0
for _n, _w in (("ident", P), ("head", HH), ("cmask", SEQ), ("keep", SEQ), ("ones32", 32), ("iota", NEXP),
               ("cos", SEQ), ("sin", SEQ)):
    CF[_n] = (_at, _w)
    _at += _w
CF_W = _at
_at = 0
for _n, _w in (("before", P), ("ones", P), ("bucket", SEQ + SLOT - 1)):
    CB[_n] = (_at, _w)
    _at += _w
CB_W = _at + _at % 2


class Chain:

    def __init__(self, eng, sem):
        self.eng, self.sem, self.n = eng, sem, 0

    def mark(self, ins):
        ins.then_inc(self.sem, 1)
        self.n += 1
        return self.n

    def need(self, n):
        self.eng.wait_ge(self.sem, n)

    def link(self, ins):
        self.need(self.mark(ins))


def build(nc, a, out):
    ctx = ExitStack()
    with ctx:
        def sb(name, shape, dt=F32):
            return ctx.enter_context(nc.sbuf_tensor("sb_" + name, shape, dt))

        def sem(name):
            return ctx.enter_context(nc.semaphore(name))

        bank = [ctx.enter_context(nc.psum_tensor(f"bank{i}", [P, 512], F32)) for i in range(8)]

        cf = sb("cf", [P, CF_W])
        cb = sb("cb", [P, CB_W], BF16)
        c = {n: cf[:, o:o + w] for n, (o, w) in CF.items()}
        cbv = {n: cb[:, o:o + w] for n, (o, w) in CB.items()}
        ident = c["ident"]
        tokb = sb("tokb", [P, KD])
        attn_b = sb("attn_b", [P, D])
        route_b = sb("route_b", [P, NEXP])
        relp = sb("relp", [96, HEADS], BF16)
        relf = sb("relf", [BUCKETS, 2, HEADS])
        gate_w = sb("gate_w", [P, KD, NEXP], BF16)
        aw = sb("aw", [P, 6, KD, D])
        phi = sb("phi", [P, KD, NP_])
        h = sb("h", [P, TILES, D])
        hT = sb("hT", [P, KD, TPAD])
        xhi = sb("xhi", [P, KD, TPAD], F16)
        xlo = sb("xlo", [P, KD, TPAD], F16)
        stats = sb("stats", [P, 8, 6])
        mv = sb("mv", [P, 8, 2])
        ln = sb("ln", [P, 5, 8])
        ew = sb("ew", [P, EW_SLOTS, KD, D])
        moe_slots = -(-(NEXP + 1) * MOE_W // (2 * KD * D))
        ew_first = EW_SLOTS - moe_slots
        moe_w = ew[:, ew_first:, :, :].rearrange("p a b c -> p (a b c)").bitcast(BF16)[:, 0:(NEXP + 1) * MOE_W]
        moe_w = moe_w.rearrange("p (e w) -> p e w", w=MOE_W)

        R1 = 24800
        r1 = sb("r1", [P, R1])

        def carve(at, *shape):
            n = 1
            for s in shape:
                n *= s
            v = r1[:, at:at + n]
            assert at + n <= R1, (at, shape)
            if len(shape) > 1:
                names = "abcdef"[:len(shape)]
                v = v.rearrange("p (" + " ".join(names) + ") -> p " + " ".join(names),
                                **{x: s for x, s in zip(names[1:], shape[1:])})
            return v

        patches = carve(0, PATCH_K, TOK)
        tokw = carve(PATCH_K * TOK, PATCH_K, D)
        BD = carve(0, 4, GROUP, HH, SEQ)
        at = 4 * GROUP * HH * SEQ
        Vbd = carve(at, NIMG, HEADS // 2, 32); at += NIMG * HEADS // 2 * 32
        xTi = carve(at, KD, NIMG, SLOT); at += KD * NIMG * SLOT
        pads = carve(at, 2, KD, NIMG, SLOT); at += 2 * KD * NIMG * SLOT
        oT = carve(at, KD, TPAD); at += KD * TPAD
        low = at
        pad1 = at - KD * TPAD - KD * NIMG * SLOT
        S0 = carve(pad1, 2, HEADS, SEQ)
        bias0 = carve(pad1 + 2 * HEADS * SEQ, HEADS, SEQ)
        Pb = carve(at, 2, HEADS // 2, 2, SLOT); at += 2 * HEADS * SLOT
        PT = carve(at, 2, HEADS // 2, 2, SEQ); at += 2 * HEADS * SEQ
        sm0 = carve(at, 2, 3, HEADS); at += 6 * HEADS
        at = low
        Qs = carve(at, 2, 4, GT); at += 8 * GT
        rt = carve(at, 2, 2, GT)
        E1 = carve(at, 2, 2, 2, 4, SEQ); at += 8 * 4 * SEQ
        dn1 = carve(at, 2, 2 * SEQ); at += 4 * SEQ
        at = 0
        act_s = carve(at, 2, 320); at += 640
        act_m = carve(at, 2, 320); at += 640
        w2f = carve(at, 2, D); at += 2 * D
        gbc = carve(at, 3, TOK); at += 3 * TOK
        gT = carve(at, TPAD); at += TPAD
        rsc = carve(at, 8, TILES, NEXP); at += 8 * TILES * NEXP
        rmask = carve(at, TILES * NEXP // 2); at += TILES * NEXP // 2
        rmax = carve(at, TILES, 8); at += 8 * TILES
        ridx = carve(at, TILES, 8); at += 8 * TILES
        req = carve(at, NEXP, TOPK); at += NEXP * TOPK
        rsum = carve(at, 2, TILES); at += 2 * TILES
        maskb = rmask.bitcast(BF16).rearrange("p (t e) -> p t e", t=TILES)
        at = 0
        L = carve(at, TILES, NP_); at += TILES * NP_
        Eb = carve(at, 2, HALF); at += 2 * HALF
        phib = carve(at, NP_); at += NP_
        ebr = carve(at, 2, D); at += 2 * D
        CT = carve(at, 2, NPT, P); at += 2 * NPT * P
        XTt = carve(at, 2, KD, P); at += 2 * KD * P
        Yt = carve(at, NPT, D); at += NPT * D
        smD = carve(at, 2, 2, HALF // SP); at += 4 * HALF // SP
        smC = carve(at, 2, 2, SP); at += 4 * SP
        Xs = Yt

        gT_dram = nc.dram_tensor("gT_scratch", [NEXP, TOK], F32, kind="Internal").ap()

        S = {}

        def s(name):
            if name not in S:
                S[name] = sem(name)
            return S[name]

        for n in ("ld_bo1 ld_const ld_patch ld_attn0 ld_attn1 ld_phi ld_phib ld_gate ld_out "
                  "dve_chain").split():
            s(n)
        ld_moe = [sem(f"ld_moe{i}") for i in range(-(-(NEXP + 1) // MOE_CHUNK))]
        ld_ew = [sem(f"ld_ew{i}") for i in range(EW_SLOTS // EW_DMA)]
        ld_g = [sem(f"ld_g{i}") for i in range(3)]
        ld_eb = [sem(f"ld_eb{i}") for i in range(2)]
        for n in ("hT_mm hT_sb h_tr h_res xTi_ok zero_ok bias_mm bias_ok relp_ok "
                  "q_mm q_sb k_mm kbd_ok kbd_act v_mm v_sb_a v_sb_d sc_mm sc_free mx_ok sub_ok exp_ok rs_ok p_ok "
                  "tr_mm pt_ok av_mm oT_ok wo_mm r_ok var_ok std_ok ln_ok lnT_mm lnT_sb "
                  "route_mm route_exp mask_ok pos_mm g_ok gT_mm gT_sb g_st ab_mm silu_ok m_ok w2_ok "
                  "w2_used "
                  "x1T qk_mm qk_act qk_dve rope_ok rope_free x1i q1d_ok q1p_ok v1_mm v1_a v1_d s1_mm e1_ok e1m_ok av1_mm o1_ok "
                  "wo1_mm l_mm l_sb mD sD eD rD nD xt_mm xt_sb mC sC eC rC nC xvar xstd xln xtan xtT_mm xtT_sb "
                  "yt_mm yt_sb ct_mm ct_sb y_mm y_sb fin_ok hT_zero xhi_ok").split():
            s(n)

        block = ctx.enter_context(nc.Block())

        def tiles(t):
            return P if t < TILES - 1 else LAST

        def rows(b, t):
            return bank[b + t // 2][:, (t % 2) * D:(t % 2 + 1) * D]

        def piece(g, dh):
            return dh * 2 + g

        @block.sync
        def _(sp):
            sp.dma_start(tokw, a["tok_w"].rearrange("(k p) n -> p k n", p=P)).then_inc(s("ld_patch"), 16)
            sp.dma_start(patches, a["patches"].rearrange("(k p) n -> p k n", p=P)).then_inc(s("ld_patch"), 16)
            sp.dma_start(cf[:, :], a["cf"]).then_inc(s("ld_const"), 16)
            sp.dma_start(cb[:, :], a["cb"]).then_inc(s("ld_const"), 16)
            sp.dma_start(tokb[:, :], a["tok_b"]).then_inc(s("ld_const"), 16)
            sp.dma_start(attn_b[:, :], a["bo0"].partition_broadcast(P)).then_inc(s("ld_const"), 16)
            sp.dma_start(route_b[:, :], a["route_b"].partition_broadcast(P)).then_inc(s("ld_const"), 16)
            sp.dma_start(relf[:, 0, :], a["rel_emb"]).then_inc(s("ld_const"), 16)
            for i, n in enumerate(("wq0", "wk0", "wv0", "wo0")):
                sp.dma_start(aw[:, i], a[n].rearrange("(k p) n -> p k n", p=P)).then_inc(s("ld_attn0"), 16)
            sp.dma_start(gate_w[:, :, :], a["gate_w"].rearrange("(k p) n -> p k n", p=P)).then_inc(s("ld_gate"), 16)
            for i, q in enumerate(ld_moe):
                e0 = i * MOE_CHUNK
                e1 = min(e0 + MOE_CHUNK, NEXP + 1)
                sp.dma_start(moe_w[:, e0:e1, :], a["moe_w"][e0:e1].rearrange("e p w -> p e w")).then_inc(q, 16)
            for k in range(KD):
                sp.dma_start(phi[:, k, :], a["phi_w"][k * P:(k + 1) * P, :]).then_inc(s("ld_phi"), 16)
            sp.wait_ge(s("wo_mm"), TILES)
            sp.wait_ge(s("h_res"), 3)
            for i, n in enumerate(("wq1", "wqs1", "wk1", "wks1", "wv1", "wo1")):
                sp.dma_start(aw[:, i], a[n].rearrange("(k p) n -> p k n", p=P)).then_inc(s("ld_attn1"), 16)
            sp.wait_ge(s("gT_sb"), 2)
            sp.dma_start(gT_dram, gT[0:NEXP, 0:TOK]).then_inc(s("g_st"), 16)
            sp.wait_ge(s("g_st"), 16)
            for e in range(NEXP):
                if e >= 3:
                    sp.wait_ge(s("m_ok"), 2 * (e - 1))
                sp.dma_start(gbc[:, e % 3, :], gT_dram[e].partition_broadcast(P)).then_inc(ld_g[e % 3], 16)
            sp.wait_ge(s("w2_used"), 2 * (NEXP + 1))
            sp.dma_start(attn_b[:, :], a["bo1"].partition_broadcast(P)).then_inc(s("ld_bo1"), 16)
            ewd = a["expert_w"].rearrange("n (k p) h -> p n k h", p=P)
            for i in range(EW_SLOTS // EW_DMA):
                n0 = i * EW_DMA
                sp.dma_start(ew[:, n0:n0 + EW_DMA].rearrange("p n k h -> p (n k) h"),
                             ewd[:, n0:n0 + EW_DMA].rearrange("p n k h -> p (n k) h")).then_inc(ld_ew[i], 16)
            sp.wait_ge(s("wo1_mm"), TILES)
            sp.dma_start(phib, a["phi_b"].partition_broadcast(P)).then_inc(s("ld_phib"), 16)

            def slot_bias(n):
                if n >= 2:
                    sp.wait_ge(s("yt_sb"), n - 1)
                for j in range(4):
                    sp.dma_start(ebr[32 * j:32 * j + 32, n % 2, :],
                                 a["expert_b"][4 * n + j].partition_broadcast(32)).then_inc(ld_eb[n % 2], 16)

            for n in range(NPT):
                slot_bias(n)
                if n >= 1 and 4 * (n - 1) + EW_SLOTS < SE:
                    sp.wait_ge(s("yt_mm"), n)
                    for q in range(4 // EW_DMA):
                        e0 = 4 * (n - 1) + q * EW_DMA
                        sp.dma_start(ew[:, e0:e0 + EW_DMA].rearrange("p n k h -> p (n k) h"),
                                     ewd[:, e0 + EW_SLOTS:e0 + EW_SLOTS + EW_DMA].rearrange("p n k h -> p (n k) h")
                                     ).then_inc(ld_ew[e0 // EW_DMA], 16)
            outs = 0
            for t in range(TILES):
                sp.wait_ge(s("fin_ok"), t + 1)
                n = tiles(t)
                sp.dma_start(out[t * P:t * P + n, :], h[0:n, t, :]).then_inc(s("ld_out"), 16)
                outs += 16
            sp.wait_ge(s("ld_out"), outs)

        @block.tensor
        def _(pe):
            mm = nc.tensor.matmul

            def proj(b, w, g, dh, src=hT):
                for k in range(KD):
                    m = mm(bank[b][:, 0:GT], aw[:, w, k, dh * P:(dh + 1) * P], src[:, k, g * GT:(g + 1) * GT],
                           start=(k == 0), stop=(k == KD - 1))
                return m

            def values(w, b, img, signal):
                for par in range(2):
                    for k in range(KD):
                        m = mm(bank[b][64 * par:64 * par + 64, (img % 4) * P:(img % 4 + 1) * P],
                               xTi[:, k, img, :], aw[:, w, k, par * P:(par + 1) * P],
                               start=(k == 0), stop=(k == KD - 1), skip_group_check=True)
                if img % 4 == 3:
                    m.then_inc(s(signal), 1)

            def out_proj(w, signal):
                for t in range(TILES):
                    for k in range(KD):
                        m = mm(rows(0, t), oT[:, k, t * P:(t + 1) * P], aw[:, w, k, :],
                               start=(k == 0), stop=(k == KD - 1), skip_group_check=True)
                    m.then_inc(s(signal), 1)

            def turn(base):
                for t in range(TILES):
                    pe.wait_ge(s("ln_ok"), base + t + 1)
                    for dh in range(KD):
                        to = bank[3 + dh][:, t * P:(t + 1) * P] if t < 4 else bank[5][:, dh * P:(dh + 1) * P]
                        m = nc.tensor.transpose(to, h[:, t, dh * P:(dh + 1) * P], ident)
                m.then_inc(s("lnT_mm"), 1)

            pe.wait_ge(s("ld_patch"), 32)
            for dh in range(KD):
                for g in range(2):
                    for k in range(PATCH_K):
                        m = mm(bank[piece(g, dh)][:, 0:GT], tokw[:, k, dh * P:(dh + 1) * P],
                               patches[:, k, g * GT:(g + 1) * GT], start=(k == 0), stop=(k == PATCH_K - 1))
                    m.then_inc(s("hT_mm"), 1)
            pe.wait_ge(s("relp_ok"), 1)
            ob = CB["bucket"][0]
            for hf in range(2):
                for kk in range(SEQ // 2):
                    k = hf * (SEQ // 2) + kk
                    for im in range(2):
                        m = mm(bank[6 + hf][64 * im:64 * im + 64, kk * HEADS:(kk + 1) * HEADS],
                               cb[0:96, ob + SEQ - 1 - k:ob + SEQ - 1 - k + SLOT], relp[:, :],
                               start=True, stop=True, skip_group_check=True)
            m.then_inc(s("bias_mm"), 1)
            pe.wait_ge(s("hT_sb"), 4)
            pe.wait_ge(s("hT_zero"), 1)
            for t in range(TILES):
                b = 4 + (t // 2) % 2
                if t == 4:
                    pe.wait_ge(s("h_res"), 1)
                for dh in range(KD):
                    m = nc.tensor.transpose(bank[b][:, (t % 2) * D + dh * P:(t % 2) * D + (dh + 1) * P],
                                            hT[:, dh, t * P:(t + 1) * P], ident)
                if t % 2 == 1 or t == 4:
                    m.then_inc(s("h_tr"), 1)
            pe.wait_ge(s("ld_attn0"), 64)
            for dh in range(KD):
                for g in range(2):
                    proj(piece(g, dh), 0, g, dh).then_inc(s("q_mm"), 1)
            pe.wait_ge(s("h_res"), 3)
            pe.wait_ge(s("bias_ok"), 1)
            for dh in range(KD):
                for g in range(2):
                    proj(4 + piece(g, dh), 1, g, dh).then_inc(s("k_mm"), 1)
            pe.wait_ge(s("xTi_ok"), 2)
            for img in range(NIMG):
                if img % 4 == 0:
                    pe.wait_ge(s("q_sb"), img // 4 + 1)
                values(2, img // 4, img, "v_mm")

            def scores0(i):
                if i == 0:
                    pe.wait_ge(s("q_sb"), 4)
                    pe.wait_ge(s("kbd_ok"), 3)
                    pe.wait_ge(s("kbd_act"), 1)
                    pe.wait_ge(s("v_sb_a"), 4)
                    pe.wait_ge(s("v_sb_d"), 4)
                if i >= 2:
                    pe.wait_ge(s("sc_free"), i - 1)
                for dh in range(KD):
                    for im in range(2):
                        img = 2 * i + im
                        m = mm(bank[2 * (i % 2) + dh][64 * im:64 * im + 64, 0:HH * SEQ], pads[:, 0, dh, img, :],
                               BD[:, piece(img // GROUP, dh), img % GROUP].rearrange("p a b -> p (a b)"),
                               start=True, stop=True, skip_group_check=True)
                m.then_inc(s("sc_mm"), 1)

            def turn0(i):
                pe.wait_ge(s("p_ok"), i + 1)
                if i >= 1:
                    pe.wait_ge(s("pt_ok"), i)
                for hp in range(HEADS // 2):
                    m = nc.tensor.transpose(bank[4 + hp // 4][:, (hp % 4) * P:(hp % 4 + 1) * P],
                                            Pb[:, i % 2, hp].rearrange("p a b -> p (a b)"), ident)
                m.then_inc(s("tr_mm"), 1)

            def apply0(i):
                pe.wait_ge(s("pt_ok"), i + 1)
                if i >= 2:
                    pe.wait_ge(s("oT_ok"), i - 1)
                for im in range(2):
                    for hp in range(HEADS // 2):
                        m = mm(bank[6 + i % 2][32 * (hp % 4):32 * (hp % 4) + 32,
                                              (hp // 4) * 2 * SEQ + im * SEQ:(hp // 4) * 2 * SEQ + (im + 1) * SEQ],
                               Vbd[:, 2 * i + im, hp, :], PT[:, i % 2, hp, im, :],
                               start=True, stop=True, skip_group_check=True)
                m.then_inc(s("av_mm"), 1)

            for i in range(PAIRS + 2):
                if i < PAIRS:
                    scores0(i)
                if 1 <= i <= PAIRS:
                    turn0(i - 1)
                if i >= 2:
                    apply0(i - 2)
            pe.wait_ge(s("oT_ok"), PAIRS)
            pe.wait_ge(s("sc_free"), PAIRS)
            out_proj(3, "wo_mm")
            turn(0)

            pe.wait_ge(s("lnT_sb"), 2)
            pe.wait_ge(s("ld_gate"), 16)
            for t in range(TILES):
                n = 0
                for part in (xhi, xlo):
                    for k in range(KD):
                        m = mm(bank[7][:, t * NEXP:(t + 1) * NEXP], part[:, k, t * P:(t + 1) * P], gate_w[:, k, :],
                               start=(n == 0), stop=(n == 3), skip_group_check=True)
                        n += 1
            m.then_inc(s("route_mm"), 1)

            def queue_places():
                pe.wait_ge(s("mask_ok"), 1)
                for t in range(TILES):
                    for j in range(t + 1):
                        m = mm(bank[6][:, t * NEXP:(t + 1) * NEXP], cbv["before" if j == t else "ones"],
                               maskb[:, j, :], start=(j == 0), stop=(j == t), skip_group_check=True)
                m.then_inc(s("pos_mm"), 1)

            def turn_gates():
                pe.wait_ge(s("g_ok"), 1)
                for t in range(TILES):
                    b, o = (7, t * P) if t < 4 else (6, 256)
                    m = nc.tensor.transpose(bank[b][0:NEXP, o:o + P], rsc[:, 5, t, :], ident)
                m.then_inc(s("gT_mm"), 1)

            def up(u):
                e, ch = u // 2, u % 2
                t0, n = CHUNKS[ch]
                pe.wait_ge(ld_moe[e // MOE_CHUNK], 16)
                if u == 1:
                    pe.wait_ge(s("gT_sb"), 2)
                if u >= 2:
                    pe.wait_ge(s("m_ok"), u - 1)
                for b in range(2):
                    j = 0
                    for part in (xhi, xlo):
                        for k in range(KD):
                            o = (b * KD + k) * P
                            m = mm(bank[3 + 2 * (u % 2) + b][:, 0:n], moe_w[:, e, o:o + P], part[:, k, t0:t0 + n],
                                   start=(j == 0), stop=(j == 3))
                            j += 1
                m.then_inc(s("ab_mm"), 1)

            def down(u):
                e, ch = u // 2, u % 2
                t0, n = CHUNKS[ch]
                pe.wait_ge(s("m_ok"), u + 1)
                if ch == 0:
                    pe.wait_ge(s("w2_ok"), e + 1)
                for t in range(t0 // P, -(-(t0 + n) // P)):
                    k = tiles(t)
                    m = mm(rows(0, t)[0:k], act_m[:, u % 2, t * P - t0:t * P - t0 + k], w2f[:, e % 2, :],
                           start=(e == 0 and t % 2 == 0), stop=(e == NEXP), skip_group_check=True)
                m.then_inc(s("w2_used"), 1)

            queue_places()
            turn_gates()
            units = 2 * (NEXP + 1)
            for u in range(units + 1):
                if u < units:
                    up(u)
                if u >= 1:
                    down(u - 1)
            turn(TILES)

            pe.wait_ge(s("lnT_sb"), 4)
            pe.wait_ge(s("ld_attn1"), 96)
            for n in range(8):
                g, dh = n % 2, (n // 2) % 2
                if n >= 4:
                    pe.wait_ge(s("qk_act"), n - 3)
                    pe.wait_ge(s("qk_dve"), n - 3)
                for w in range(2):
                    m = proj(2 * (n % 4) + w, 2 * (n // 4) + w, g, dh)
                m.then_inc(s("qk_mm"), 1)
            pe.wait_ge(s("x1i"), 2)
            for img in range(NIMG):
                if img % 8 == 0:
                    pe.wait_ge(s("qk_act"), 5 + img // 8)
                    pe.wait_ge(s("qk_dve"), 5 + img // 8)
                values(4, img // 4, img, "v1_mm")

            def scores1(st):
                u, j = st // 4, st % 4
                g, dh = u // 2, u % 2
                if st == 0:
                    pe.wait_ge(s("rope_ok"), 8)
                    pe.wait_ge(s("qk_act"), 8)
                    pe.wait_ge(s("v1_a"), 4)
                    pe.wait_ge(s("v1_d"), 4)
                if j == 0:
                    pe.wait_ge(s("q1d_ok"), u + 1)
                    pe.wait_ge(s("q1p_ok"), u + 1)
                if st >= 2:
                    pe.wait_ge(s("e1_ok"), st - 1)
                for kind in range(2):
                    bd = BD[:, 2 * (u % 2) + kind]
                    for im in range(2):
                        for par in range(2):
                            img = 2 * j + im
                            m = mm(bank[2 * (st % 2) + kind][64 * par:64 * par + 64, im * 144:(im + 1) * 144],
                                   pads[:, kind, dh, g * GROUP + img, :],
                                   bd[:, img].rearrange("p (a b) c -> p a b c", b=2)[:, :, par, :],
                                   start=True, stop=True, skip_group_check=True)
                m.then_inc(s("s1_mm"), 1)

            def apply1(st):
                u, j = st // 4, st % 4
                g, dh = u // 2, u % 2
                pe.wait_ge(s("e1m_ok"), st + 1)
                if st >= 2:
                    pe.wait_ge(s("o1_ok"), st - 1)
                for hp in range(4):
                    to = bank[4 + 2 * (st % 2)][32 * hp:32 * hp + 32, :]
                    for im in range(2):
                        mm(to[:, im * SEQ:(im + 1) * SEQ], Vbd[:, g * GROUP + 2 * j + im, dh * 4 + hp, :],
                           E1[:, st % 2, 0, im, hp, :], start=True, stop=True, skip_group_check=True)
                    m = mm(bank[5 + 2 * (st % 2)][32 * hp:32 * hp + 32, 0:2 * SEQ], c["ones32"],
                           E1[:, st % 2, 1, :, hp, :], start=True, stop=True, skip_group_check=True)
                m.then_inc(s("av1_mm"), 1)

            for st in range(17):
                if st < 16:
                    scores1(st)
                if st >= 1:
                    apply1(st - 1)
            pe.wait_ge(s("o1_ok"), 16)
            pe.wait_ge(s("e1_ok"), 16)
            out_proj(5, "wo1_mm")
            turn(2 * TILES)

            pe.wait_ge(s("lnT_sb"), 6)
            pe.wait_ge(s("ld_phi"), 32)

            def logits(u):
                hf, t = u // TILES, u % TILES
                for q in range(2):
                    n = 2 * u + q
                    if n >= 4:
                        pe.wait_ge(s("l_sb"), n - 3)
                    o = hf * HALF + q * 512
                    for k in range(KD):
                        m = mm(bank[n % 4][:, :], hT[:, k, t * P:(t + 1) * P], phi[:, k, o:o + 512],
                               start=(k == 0), stop=(k == KD - 1))
                    m.then_inc(s("l_mm"), 1)

            def gather(u):
                hf, t = u // TILES, u % TILES
                pe.wait_ge(s("nD"), u + 1)
                if u == TILES:
                    pe.wait_ge(s("xt_sb"), 4)
                k = tiles(t)
                for n in range(8):
                    m = mm(bank[4 + n // 2][:, (n % 2) * D:(n % 2 + 1) * D], Eb[0:k, u % 2, n * P:(n + 1) * P],
                           h[0:k, t, :], start=(t == 0 and n % 2 == 0), stop=(t == TILES - 1),
                           skip_group_check=True)
                m.then_inc(s("xt_mm"), 1)

            def slots_in(n):
                pe.wait_ge(s("xtan"), n + 1)
                if n >= 2:
                    pe.wait_ge(s("xtT_sb"), n - 1)
                for k in range(KD):
                    m = nc.tensor.transpose(bank[n % 2][:, k * P:(k + 1) * P], Xs[:, n, k * P:(k + 1) * P], ident)
                m.then_inc(s("xtT_mm"), 1)

            def slots_out(n):
                pe.wait_ge(s("xtT_sb"), n + 1)
                if n >= 2:
                    pe.wait_ge(s("yt_sb"), n - 1)
                for q in range(4 // EW_DMA):
                    e = 4 * n + q * EW_DMA
                    pe.wait_ge(ld_ew[(e % EW_SLOTS) // EW_DMA], 16 * (e // EW_SLOTS + 1))
                for k in range(KD):
                    for j in range(4):
                        e = 4 * n + j
                        m = mm(bank[2 + n % 2][32 * j:32 * j + 32, 0:D], XTt[:, n % 2, k, 32 * j:32 * j + 32],
                               ew[:, e % EW_SLOTS, k, :], start=(k == 0), stop=(k == KD - 1), skip_group_check=True)
                m.then_inc(s("yt_mm"), 1)

            def turn_weights(t):
                if t == 0:
                    pe.wait_ge(s("xt_sb"), 8)
                pe.wait_ge(s("nC"), t + 1)
                for b in range(4):
                    if t >= 1:
                        pe.wait_ge(s("ct_sb"), 4 * (t - 1) + b + 1)
                    for q in range(4):
                        n = 4 * b + q
                        m = nc.tensor.transpose(bank[4 + b][:, q * P:(q + 1) * P], L[:, t, n * P:(n + 1) * P], ident)
                    m.then_inc(s("ct_mm"), 1)

            def combine(t):
                pe.wait_ge(s("ct_sb"), 4 * (t + 1))
                if t == 0:
                    pe.wait_ge(s("yt_sb"), NPT)
                    pe.wait_ge(s("xtT_sb"), NPT)
                if t >= 2:
                    pe.wait_ge(s("y_sb"), t - 1)
                k = tiles(t)
                for n in range(NPT):
                    m = mm(bank[t % 2][0:k, 0:D], CT[:, t % 2, n, 0:k], Yt[:, n, :],
                           start=(n == 0), stop=(n == NPT - 1))
                m.then_inc(s("y_mm"), 1)

            for u in range(2 * TILES + 1):
                if u < 2 * TILES:
                    logits(u)
                if u >= 1:
                    gather(u - 1)
            pe.wait_ge(s("l_sb"), 4 * TILES)
            for n in range(NPT + 1):
                if n < NPT:
                    slots_in(n)
                if n >= 1:
                    slots_out(n - 1)
            for t in range(TILES + 1):
                if t < TILES:
                    turn_weights(t)
                if t >= 1:
                    combine(t - 1)

        @block.scalar
        def _(act):
            A = nc.scalar.activation

            def scaled_copies(to, src, n, width):
                for hd in range(HH):
                    m = A(to[:, :, hd, :], src, ACT.Copy, scale=c["head"][:, hd:hd + 1])
                return m

            def values_evac(b, j, par, signal):
                lo = 64 * par
                A(Vbd[lo:lo + 64, 4 * j:4 * j + 4, :, 16 * par:16 * par + 16],
                  bank[b][lo:lo + 64, :].rearrange("p (i h d) -> p i h d", i=4, h=8), ACT.Copy).then_inc(s(signal), 1)

            def std(n, width):
                act.wait_ge(s("var_ok"), n)
                A(ln[:, 1, 0:width], ln[:, 0, 0:width], ACT.Sqrt).then_inc(s("std_ok"), 1)

            act.wait_ge(s("ld_const"), 96)
            for i in range(4):
                dh, g = i // 2, i % 2
                act.wait_ge(s("hT_mm"), i + 1)
                A(hT[:, dh, g * GT:(g + 1) * GT], bank[i][:, 0:GT], ACT.Identity,
                  bias=tokb[:, dh:dh + 1]).then_inc(s("hT_sb"), 1)
            for i in range(4):
                dh, g = i // 2, i % 2
                act.wait_ge(s("q_mm"), i + 1)
                if i == 0:
                    act.wait_ge(s("zero_ok"), 4)
                A(pads[:, 0, dh, g * GROUP:(g + 1) * GROUP, 0:SEQ],
                  bank[i][:, 0:GT].rearrange("p (i t) -> p i t", i=GROUP), ACT.Copy, scale=SCALE).then_inc(s("q_sb"), 1)
            act.wait_ge(s("k_mm"), 4)
            scaled_copies(BD[:, 3], bank[7][:, 0:GT].rearrange("p (i t) -> p i t", i=GROUP), 0, 0)\
                .then_inc(s("kbd_act"), 1)
            for j in range(4):
                act.wait_ge(s("v_mm"), j + 1)
                values_evac(j, j, 0, "v_sb_a")

            def evac_pt(i):
                act.wait_ge(s("tr_mm"), i + 1)
                if i >= 2:
                    act.wait_ge(s("av_mm"), i - 1)
                for b in range(2):
                    m = A(PT[:, i % 2, 4 * b:4 * b + 4],
                          bank[4 + b][:, :].rearrange("p (h i q) -> p h i q", h=4, i=2)[:, :, :, 0:SEQ], ACT.Copy)
                m.then_inc(s("pt_ok"), 1)

            for i in range(PAIRS + 1):
                if i < PAIRS:
                    act.wait_ge(s("sub_ok"), i + 1)
                    A(S0[:, i % 2], S0[:, i % 2], ACT.Exp).then_inc(s("exp_ok"), 1)
                if i >= 1:
                    evac_pt(i - 1)
            std(1, TILES)

            act.wait_ge(s("lnT_mm"), 1)
            for dh in range(KD):
                A(xhi[:, dh, 0:4 * P], bank[3 + dh][:, :], ACT.Copy)
                m = A(xhi[:, dh, 4 * P:TPAD], bank[5][:, dh * P:(dh + 1) * P], ACT.Copy)
            m.then_inc(s("xhi_ok"), 1)
            act.wait_ge(s("route_mm"), 1)
            A(rsc[:, 0], bank[7][:, 0:TILES * NEXP].rearrange("p (t e) -> p t e", t=TILES), ACT.Exp,
              scale=-1.0).then_inc(s("route_exp"), 1)
            act.wait_ge(s("gT_mm"), 1)
            A(gT[0:NEXP, 0:4 * P], bank[7][0:NEXP, :], ACT.Copy).then_inc(s("gT_sb"), 1)
            A(gT[0:NEXP, 4 * P:TPAD], bank[6][0:NEXP, 256:256 + P], ACT.Copy).then_inc(s("gT_sb"), 1)

            for u in range(2 * (NEXP + 1)):
                n = CHUNKS[u % 2][1]
                act.wait_ge(s("ab_mm"), u + 1)
                if u >= 2:
                    act.wait_ge(s("m_ok"), u - 1)
                A(act_s[:, u % 2, 0:n], bank[3 + 2 * (u % 2)][:, 0:n], ACT.Silu).then_inc(s("silu_ok"), 1)
            std(2, TILES)

            act.wait_ge(s("lnT_mm"), 2)
            for dh in range(KD):
                A(hT[:, dh, 0:4 * P], bank[3 + dh][:, :], ACT.Copy)
                m = A(hT[:, dh, 4 * P:TPAD], bank[5][:, dh * P:(dh + 1) * P], ACT.Copy)
                m.then_inc(s("lnT_sb"), 1)
            for n in range(8):
                g, dh = n % 2, (n // 2) % 2
                act.wait_ge(s("qk_dve"), n + 1)
                src = bank[2 * (n % 4)][:, 0:GT]
                if n < 4:
                    A(Qs[:, 1, 2 * g + dh, :], src, ACT.Copy).then_inc(s("qk_act"), 1)
                else:
                    if n == 4:
                        act.wait_ge(s("zero_ok"), 6)
                    A(pads[:, 1, dh, g * GROUP:(g + 1) * GROUP, 0:SEQ], src.rearrange("p (i t) -> p i t", i=GROUP),
                      ACT.Copy).then_inc(s("qk_act"), 1)
            for j in range(4):
                act.wait_ge(s("v1_mm"), j + 1)
                values_evac(j, j, 0, "v1_a")
            for st in range(16):
                act.wait_ge(s("s1_mm"), st + 1)
                if st >= 2:
                    act.wait_ge(s("av1_mm"), st - 1)
                for kind in range(2):
                    m = A(E1[:, st % 2, kind].rearrange("p a b c -> p (a b c)"),
                          bank[2 * (st % 2) + kind][:, 0:288], ACT.Exp, scale=SCALE)
                m.then_inc(s("e1_ok"), 1)
            std(3, TILES)

            act.wait_ge(s("lnT_mm"), 3)
            for dh in range(KD):
                A(hT[:, dh, 0:4 * P], bank[3 + dh][:, :], ACT.Copy)
                m = A(hT[:, dh, 4 * P:TPAD], bank[5][:, dh * P:(dh + 1) * P], ACT.Copy)
                m.then_inc(s("lnT_sb"), 1)

            def exp_c(t):
                act.wait_ge(s("sC"), t + 1)
                A(L[:, t, :], L[:, t, :], ACT.Exp).then_inc(s("eC"), 1)

            for u in range(2 * TILES):
                act.wait_ge(s("sD"), u + 1)
                A(Eb[:, u % 2, :], Eb[:, u % 2, :], ACT.Exp).then_inc(s("eD"), 1)
                if u > TILES:
                    exp_c(u - TILES - 1)
            exp_c(TILES - 1)
            act.wait_ge(s("xvar"), 1)
            A(ln[:, 1, 0:8], ln[:, 0, 0:8], ACT.Sqrt).then_inc(s("xstd"), 1)
            act.wait_ge(s("xvar"), 2)
            A(ln[:, 1, 0:8], ln[:, 0, 0:8], ACT.Sqrt).then_inc(s("xstd"), 1)
            def slots_tanh(n):
                act.wait_ge(s("xln"), n + 1)
                A(Xs[:, n, :], Xs[:, n, :], ACT.Tanh).then_inc(s("xtan"), 1)

            def slots_turned(n):
                act.wait_ge(s("xtT_mm"), n + 1)
                if n >= 2:
                    act.wait_ge(s("yt_mm"), n - 1)
                A(XTt[:, n % 2].rearrange("p a b -> p (a b)"), bank[n % 2][:, 0:D], ACT.Copy).then_inc(s("xtT_sb"), 1)

            for n in range(NPT):
                slots_tanh(n)
            for n in range(NPT):
                slots_turned(n)
            for t in range(TILES):
                for b in range(4):
                    act.wait_ge(s("ct_mm"), 4 * t + b + 1)
                    if t >= 2 and b == 0:
                        act.wait_ge(s("y_mm"), t - 1)
                    A(CT[:, t % 2, 4 * b:4 * b + 4].rearrange("p a b -> p (a b)"), bank[4 + b][:, :],
                      ACT.Copy).then_inc(s("ct_sb"), 1)
            std(4, TILES)

        @block.vector
        def _(dve):
            V = nc.vector
            ch = Chain(dve, s("dve_chain"))
            link = ch.link

            def layernorm(n0, signal, counts, k_last):
                for t in range(TILES):
                    dve.wait_ge(s(signal), counts[t])
                    k = P if t < TILES - 1 else k_last
                    link(V.tensor_tensor(h[0:k, t, :], rows(0, t)[0:k], h[0:k, t, :], ALU.add))
                    link(V.bn_stats(stats[:, t, :], h[:, t, :]))
                    m = ch.mark(V.bn_aggr(mv[:, t, :], stats[:, t, :]))
                ch.need(m)
                rstd(n0, TILES, "var_ok", "std_ok")
                for t in range(TILES):
                    V.tensor_scalar(h[:, t, :], h[:, t, :], mv[:, t, 0:1], ln[:, 2, t:t + 1], ALU.subtract,
                                    ALU.mult).then_inc(s("ln_ok"), 1)

            def rstd(n, w, sv, ss):
                V.tensor_scalar(ln[:, 0, 0:w], mv[:, 0:w, 1], EPS, None, ALU.add).then_inc(s(sv), 1)
                dve.wait_ge(s(ss), n)
                link(V.reciprocal(ln[:, 2, 0:w], ln[:, 1, 0:w]))
                link(V.tensor_tensor(ln[:, 3, 0:w], ln[:, 2, 0:w], ln[:, 2, 0:w], ALU.mult))
                link(V.tensor_tensor(ln[:, 3, 0:w], ln[:, 3, 0:w], ln[:, 0, 0:w], ALU.mult))
                link(V.tensor_scalar(ln[:, 3, 0:w], ln[:, 3, 0:w], -0.5, 1.5, ALU.mult, ALU.add))
                link(V.tensor_tensor(ln[:, 2, 0:w], ln[:, 2, 0:w], ln[:, 3, 0:w], ALU.mult))

            def values_evac(b, j, par, signal):
                lo = 64 * par
                V.tensor_copy(Vbd[lo:lo + 64, 4 * j:4 * j + 4, :, 16 * par:16 * par + 16],
                              bank[b][lo:lo + 64, :].rearrange("p (i h d) -> p i h d", i=4, h=8)
                              ).then_inc(s(signal), 1)

            def expand(to, src):
                return V.tensor_tensor(to, src.unsqueeze(2).broadcast_to([P, GROUP, HH, SEQ]),
                                       c["head"].unsqueeze(1).unsqueeze(3).broadcast_to([P, GROUP, HH, SEQ]),
                                       ALU.mult)

            V.memset(hT[:, :, TOK:TPAD], 0.0).then_inc(s("hT_zero"), 1)
            dve.wait_ge(s("ld_const"), 96)
            link(V.tensor_copy(relp[0:32, :], relf[:, 0, :]))
            link(V.tensor_tensor(relf[:, 1, :], relf[:, 0, :], relp[0:32, :], ALU.subtract))
            link(V.tensor_copy(relp[32:64, :], relf[:, 1, :]))
            link(V.tensor_copy(sm0[0:32, 0, 0].bitcast(BF16)[:, 0:HEADS], relf[:, 1, :]))
            link(V.tensor_tensor(relf[:, 1, :], relf[:, 1, :], sm0[0:32, 0, 0].bitcast(BF16)[:, 0:HEADS],
                                 ALU.subtract))
            V.tensor_copy(relp[64:96, :], relf[:, 1, :]).then_inc(s("relp_ok"), 1)
            dve.wait_ge(s("bias_mm"), 1)
            for hf in range(2):
                k0 = hf * (SEQ // 2)
                m = V.tensor_tensor(
                    bias0[:, :, k0:k0 + SEQ // 2],
                    bank[6 + hf][:, 0:SEQ // 2 * HEADS].rearrange("p (k h) -> p h k", h=HEADS),
                    c["cmask"][:, k0:k0 + SEQ // 2].unsqueeze(1).broadcast_to([P, HEADS, SEQ // 2]), ALU.add)
            m.then_inc(s("bias_ok"), 1)
            for i in range(3):
                dve.wait_ge(s("h_tr"), i + 1)
                w = 2 if i < 2 else 1
                V.tensor_tensor(h[:, 2 * i:2 * i + w, :],
                                bank[4 + i % 2][:, 0:w * D].rearrange("p (t d) -> p t d", t=w),
                                attn_b[:, :].unsqueeze(1).broadcast_to([P, w, D]), ALU.add).then_inc(s("h_res"), 1)
            dve.wait_ge(s("hT_mm"), 4)
            for i in range(3):
                dve.wait_ge(s("k_mm"), i + 1)
                expand(BD[:, i], bank[4 + i][:, 0:GT].rearrange("p (i t) -> p i t", i=GROUP)).then_inc(s("kbd_ok"), 1)
            dve.wait_ge(s("zero_ok"), 4)
            for j in range(4):
                dve.wait_ge(s("v_mm"), j + 1)
                values_evac(j, j, 1, "v_sb_d")

            def add0(i):
                dve.wait_ge(s("sc_mm"), i + 1)
                if i >= 2:
                    dve.wait_ge(s("p_ok"), i - 1)
                for dh in range(KD):
                    m = V.tensor_tensor(S0[:, i % 2, 8 * dh:8 * dh + 8, :],
                                        bank[2 * (i % 2) + dh][:, 0:288].rearrange("p (h k) -> p h k", h=8),
                                        bias0[:, 8 * dh:8 * dh + 8, :], ALU.add)
                m.then_inc(s("sc_free"), 1)
                dve.wait_ge(s("sc_free"), i + 1)
                V.tensor_reduce(sm0[:, i % 2, 0, :], S0[:, i % 2], AX.X, ALU.max).then_inc(s("mx_ok"), 1)

            def sum0(i):
                dve.wait_ge(s("exp_ok"), i + 1)
                link(V.tensor_reduce(sm0[:, i % 2, 1, :], S0[:, i % 2], AX.X, ALU.add))
                V.reciprocal(sm0[:, i % 2, 2, :], sm0[:, i % 2, 1, :]).then_inc(s("rs_ok"), 1)

            def out0(i):
                dve.wait_ge(s("av_mm"), i + 1)
                V.tensor_copy(oT[:, :, 2 * i * SEQ:2 * (i + 1) * SEQ],
                              bank[6 + i % 2][:, 0:4 * SEQ].rearrange("p (a b) -> p a b", a=KD)).then_inc(s("oT_ok"), 1)

            for i in range(PAIRS + 3):
                if i < PAIRS:
                    add0(i)
                if 1 <= i <= PAIRS:
                    sum0(i - 1)
                if i >= 3:
                    out0(i - 3)
            layernorm(1, "wo_mm", (2, 2, 4, 4, 5), P)
            dve.wait_ge(s("lnT_mm"), 1)
            dve.wait_ge(s("xhi_ok"), 1)
            for dh in range(KD):
                V.tensor_tensor(xlo[:, dh, 0:4 * P], bank[3 + dh][:, :], xhi[:, dh, 0:4 * P], ALU.subtract)
                V.tensor_tensor(xlo[:, dh, 4 * P:TPAD], bank[5][:, dh * P:(dh + 1) * P], xhi[:, dh, 4 * P:TPAD],
                                ALU.subtract).then_inc(s("lnT_sb"), 1)

            dve.wait_ge(s("route_exp"), 1)
            link(V.tensor_scalar(rsc[:, 1], rsc[:, 0], 1.0, None, ALU.add))
            link(V.reciprocal(rsc[:, 1], rsc[:, 1]))
            link(V.tensor_tensor(rsc[:, 2], rsc[:, 1], route_b[:, :].unsqueeze(1).broadcast_to([P, TILES, NEXP]),
                                 ALU.add))
            for t in range(TILES):
                link(V.max(rmax[:, t, :], rsc[:, 2, t, :]))
                link(V.max_index(ridx[:, t, :].bitcast(U32), rmax[:, t, :], rsc[:, 2, t, :]))
                link(V.tensor_tensor(req, c["iota"].unsqueeze(2).broadcast_to([P, NEXP, TOPK]),
                                     ridx[:, t, 0:TOPK].bitcast(U32).unsqueeze(1).broadcast_to([P, NEXP, TOPK]),
                                     ALU.is_equal))
                link(V.tensor_reduce(rsc[:, 3, t, :], req, AX.X, ALU.add))
            V.tensor_copy(maskb, rsc[:, 3]).then_inc(s("mask_ok"), 1)
            link(V.tensor_tensor(rsc[:, 4], rsc[:, 1], rsc[:, 3], ALU.mult))
            link(V.tensor_reduce(rsum[:, 0, :], rsc[:, 4], AX.X, ALU.add))
            link(V.tensor_scalar(rsum[:, 0, :], rsum[:, 0, :], 1e-12, None, ALU.max))
            link(V.reciprocal(rsum[:, 1, :], rsum[:, 0, :]))
            link(V.tensor_tensor(rsc[:, 4], rsc[:, 4], rsum[:, 1, :].unsqueeze(2).broadcast_to([P, TILES, NEXP]),
                                 ALU.mult))
            dve.wait_ge(s("pos_mm"), 1)
            link(V.tensor_scalar(rsc[:, 6], bank[6][:, 0:TILES * NEXP].rearrange("p (t e) -> p t e", t=TILES),
                                 float(CAP), None, ALU.is_lt))
            V.tensor_tensor(rsc[:, 5], rsc[:, 4], rsc[:, 6], ALU.mult).then_inc(s("g_ok"), 1)

            for u in range(2 * (NEXP + 1)):
                e, t0, n = u // 2, *CHUNKS[u % 2]
                dve.wait_ge(s("silu_ok"), u + 1)
                if u >= 2:
                    dve.wait_ge(s("w2_used"), u - 1)
                ins = V.tensor_tensor(act_m[:, u % 2, 0:n], bank[4 + 2 * (u % 2)][:, 0:n], act_s[:, u % 2, 0:n],
                                      ALU.mult)
                if e == 0:
                    ins.then_inc(s("m_ok"), 1)
                    continue
                link(ins)
                dve.wait_ge(ld_g[(e - 1) % 3], 16 * ((e - 1) // 3 + 1))
                V.tensor_tensor(act_m[:, u % 2, 0:n], act_m[:, u % 2, 0:n], gbc[:, (e - 1) % 3, t0:t0 + n],
                                ALU.mult).then_inc(s("m_ok"), 1)
            layernorm(2, "w2_used", (2 * (NEXP + 1),) * TILES, LAST)

            for n in range(8):
                dve.wait_ge(s("qk_mm"), n + 1)
                if n >= 2:
                    dve.wait_ge(s("rope_ok"), n - 1)
                for w, tab in ((0, "cos"), (1, "sin")):
                    m = V.tensor_tensor(rt[:, n % 2, w].rearrange("p (i t) -> p i t", i=GROUP),
                                        bank[2 * (n % 4) + w][:, 0:GT].rearrange("p (i t) -> p i t", i=GROUP),
                                        c[tab].unsqueeze(1).broadcast_to([P, GROUP, SEQ]), ALU.mult)
                m.then_inc(s("qk_dve"), 1)
            dve.wait_ge(s("zero_ok"), 6)
            for j in range(4):
                dve.wait_ge(s("v1_mm"), j + 1)
                values_evac(j, j, 1, "v1_d")

            def plain1(u):
                if u >= 2:
                    dve.wait_ge(s("s1_mm"), 4 * (u - 1))
                if u == 0:
                    dve.wait_ge(s("qk_act"), 4)
                expand(BD[:, 2 * (u % 2) + 1], Qs[:, 1, u, :].rearrange("p (i t) -> p i t", i=GROUP))\
                    .then_inc(s("q1d_ok"), 1)

            def out1(st):
                u, j = st // 4, st % 4
                g, dh = u // 2, u % 2
                dve.wait_ge(s("av1_mm"), st + 1)
                link(V.reciprocal(dn1[:, st % 2, :], bank[5 + 2 * (st % 2)][:, 0:2 * SEQ]))
                o = (g * GROUP + 2 * j) * SEQ
                V.tensor_tensor(oT[:, dh, o:o + 2 * SEQ], bank[4 + 2 * (st % 2)][:, 0:2 * SEQ], dn1[:, st % 2, :],
                                ALU.mult).then_inc(s("o1_ok"), 1)

            plain1(0)
            plain1(1)
            for st in range(17):
                if st >= 1:
                    out1(st - 1)
                if st % 4 == 0 and 4 <= st < 12:
                    plain1(st // 4 + 1)
            dve.wait_ge(s("ld_bo1"), 16)
            for t in range(TILES):
                m = V.tensor_tensor(h[:, t, :], h[:, t, :], attn_b[:, :], ALU.add)
            link(m)
            layernorm(3, "wo1_mm", (2, 2, 4, 4, 5), P)

            def max_c(t):
                V.tensor_reduce(smC[:, t % 2, 0, :], L[:, t, :].rearrange("p (n s) -> p s n", s=SP), AX.X,
                                ALU.max).then_inc(s("mC"), 1)

            def sum_c(t):
                dve.wait_ge(s("eC"), t + 1)
                link(V.tensor_reduce(smC[:, t % 2, 1, :], L[:, t, :].rearrange("p (n s) -> p s n", s=SP), AX.X,
                                     ALU.add))
                link(V.reciprocal(smC[:, t % 2, 1, :], smC[:, t % 2, 1, :]))
                V.tensor_tensor(L[:, t, :].rearrange("p (n s) -> p n s", s=SP),
                                L[:, t, :].rearrange("p (n s) -> p n s", s=SP),
                                smC[:, t % 2, 1, :].unsqueeze(1).broadcast_to([P, SE, SP]),
                                ALU.mult).then_inc(s("nC"), 1)

            def add_d(u):
                hf, t = u // TILES, u % TILES
                if u == 0:
                    dve.wait_ge(s("ld_phib"), 16)
                for q in range(2):
                    o = hf * HALF + q * 512
                    dve.wait_ge(s("l_mm"), 2 * u + q + 1)
                    V.tensor_tensor(L[:, t, o:o + 512], bank[(2 * u + q) % 4][:, :], phib[:, o:o + 512],
                                    ALU.add).then_inc(s("l_sb"), 1)
                dve.wait_ge(s("l_sb"), 2 * u + 2)
                V.tensor_reduce(smD[:, u % 2, 0, :],
                                L[:, t, hf * HALF:(hf + 1) * HALF].rearrange("p (n s) -> p n s", s=SP), AX.X,
                                ALU.max).then_inc(s("mD"), 1)

            def sum_d(u):
                dve.wait_ge(s("eD"), u + 1)
                if u >= 2:
                    dve.wait_ge(s("nD"), u - 1)
                link(V.tensor_reduce(smD[:, u % 2, 1, :], Eb[:, u % 2].rearrange("p (n s) -> p n s", s=SP), AX.X,
                                     ALU.add))
                V.reciprocal(smD[:, u % 2, 1, :], smD[:, u % 2, 1, :]).then_inc(s("rD"), 1)

            def slots_stats(hf):
                dve.wait_ge(s("xt_mm"), TILES * (hf + 1))
                for b in range(4):
                    V.tensor_scalar(Xs[:, 8 * hf + 2 * b:8 * hf + 2 * b + 2, :],
                                    bank[4 + b][:, :].rearrange("p (n d) -> p n d", n=2), -33000.0, 65000.0,
                                    ALU.max, ALU.min).then_inc(s("xt_sb"), 1)
                dve.wait_ge(s("xt_sb"), 4 * (hf + 1))

            def slots_norm(hf):
                for n in range(8):
                    m = V.bn_stats(stats[:, n, :], Xs[:, 8 * hf + n, :])
                link(m)
                for n in range(8):
                    m = V.bn_aggr(mv[:, n, :], stats[:, n, :])
                link(m)
                rstd(hf + 1, 8, "xvar", "xstd")
                for n in range(8):
                    m = V.tensor_scalar(Xs[:, 8 * hf + n, :], Xs[:, 8 * hf + n, :], mv[:, n, 0:1], ln[:, 2, n:n + 1],
                                    ALU.subtract, ALU.mult)
                    m.then_inc(s("xln"), 1)
                dve.wait_ge(s("xln"), 8 * (hf + 1))

            for u in range(2 * TILES + 1):
                if u < 2 * TILES:
                    add_d(u)
                    if u >= TILES:
                        if u >= TILES + 2:
                            dve.wait_ge(s("sC"), u - TILES - 1)
                        max_c(u - TILES)
                if u >= 1:
                    sum_d(u - 1)
                if u == TILES:
                    slots_stats(0)
                if u > TILES + 1:
                    sum_c(u - TILES - 2)
            slots_stats(1)
            sum_c(TILES - 1)
            slots_norm(0)
            slots_norm(1)
            for n in range(NPT):
                dve.wait_ge(s("yt_mm"), n + 1)
                dve.wait_ge(ld_eb[n % 2], 64 * (n // 2 + 1))
                V.tensor_tensor(Yt[:, n, :], bank[2 + n % 2][:, 0:D], ebr[:, n % 2, :], ALU.add)\
                    .then_inc(s("yt_sb"), 1)
            for t in range(TILES):
                k = tiles(t)
                dve.wait_ge(s("y_mm"), t + 1)
                V.tensor_tensor(h[0:k, t, :], bank[t % 2][0:k, 0:D], h[0:k, t, :], ALU.add).then_inc(s("y_sb"), 1)
                dve.wait_ge(s("y_sb"), t + 1)
                link(V.bn_stats(stats[:, t, :], h[:, t, :]))
                link(V.bn_aggr(mv[:, t, :], stats[:, t, :]))
            rstd(4, TILES, "var_ok", "std_ok")
            for t in range(TILES):
                V.tensor_scalar(h[:, t, :], h[:, t, :], mv[:, t, 0:1], ln[:, 2, t:t + 1], ALU.subtract,
                                ALU.mult).then_inc(s("fin_ok"), 1)

        @block.gpsimd
        def _(pool):
            G = nc.gpsimd
            pool.wait_ge(s("hT_mm"), 4)
            G.memset(pads[:, 0, :, :, SEQ:SLOT], 0.0).then_inc(s("zero_ok"), 1)
            G.memset(xTi[:, :, :, SEQ:SLOT], 0.0).then_inc(s("zero_ok"), 1)
            G.memset(Vbd[:, :, :, :], 0.0).then_inc(s("zero_ok"), 1)
            G.memset(oT[:, :, TOK:TPAD], 0.0)
            G.memset(Pb[:, :, :, :, :], 0.0).then_inc(s("zero_ok"), 1)
            for dh in range(KD):
                pool.wait_ge(s("hT_sb"), 2 * (dh + 1))
                G.tensor_copy(xTi[:, dh, :, 0:SEQ], hT[:, dh, 0:TOK].rearrange("p (i t) -> p i t", i=NIMG))\
                    .then_inc(s("xTi_ok"), 1)

            def bcast(v):
                return v.unsqueeze(2).broadcast_to([P, HEADS, SEQ])

            def norm0(i):
                pool.wait_ge(s("rs_ok"), i + 1)
                if i >= 2:
                    pool.wait_ge(s("tr_mm"), i - 1)
                G.tensor_tensor(Pb[:, i % 2].rearrange("p a b c -> p (a b) c")[:, :, 0:SEQ], S0[:, i % 2],
                                bcast(sm0[:, i % 2, 2, :]), ALU.mult).then_inc(s("p_ok"), 1)

            for i in range(PAIRS + 1):
                if i < PAIRS:
                    pool.wait_ge(s("mx_ok"), i + 1)
                    G.tensor_tensor(S0[:, i % 2], S0[:, i % 2], bcast(sm0[:, i % 2, 0, :]), ALU.subtract)\
                        .then_inc(s("sub_ok"), 1)
                if i >= 1:
                    norm0(i - 1)
            for e in range(NEXP + 1):
                pool.wait_ge(ld_moe[e // MOE_CHUNK], 16)
                if e == 0:
                    pool.wait_ge(s("mask_ok"), 1)
                if e >= 2:
                    pool.wait_ge(s("w2_used"), 2 * (e - 1))
                ins = G.tensor_copy(w2f[:, e % 2, :], moe_w[:, e, 2 * KD * P:MOE_W])
                ins.then_inc(s("w2_ok"), 1)
            pool.wait_ge(s("w2_used"), 2 * (NEXP + 1))
            G.memset(pads[:, :, :, :, SEQ:SLOT], 0.0).then_inc(s("zero_ok"), 1)
            G.memset(xTi[:, :, :, SEQ:SLOT], 0.0)
            G.memset(Vbd[:, :, :, :], 0.0).then_inc(s("zero_ok"), 1)
            for dh in range(KD):
                pool.wait_ge(s("lnT_sb"), 4)
                G.tensor_copy(xTi[:, dh, :, 0:SEQ], hT[:, dh, 0:TOK].rearrange("p (i t) -> p i t", i=NIMG))\
                    .then_inc(s("x1i"), 1)
            for n in range(8):
                g, dh = n % 2, (n // 2) % 2
                pool.wait_ge(s("qk_dve"), n + 1)
                if n < 4:
                    to = Qs[:, 0, 2 * g + dh, :]
                    x, y = rt[:, n % 2, 0], rt[:, n % 2, 1]
                else:
                    to = pads[:, 0, dh, g * GROUP:(g + 1) * GROUP, 0:SEQ]
                    x, y = (rt[:, n % 2, w].rearrange("p (i t) -> p i t", i=GROUP) for w in range(2))
                G.tensor_tensor(to, x, y, ALU.add).then_inc(s("rope_ok"), 1)

            def rotated1(u):
                if u >= 2:
                    pool.wait_ge(s("s1_mm"), 4 * (u - 1))
                if u == 0:
                    pool.wait_ge(s("rope_ok"), 4)
                src = Qs[:, 0, u, :].rearrange("p (i t) -> p i t", i=GROUP)
                G.tensor_tensor(BD[:, 2 * (u % 2)], src.unsqueeze(2).broadcast_to([P, GROUP, HH, SEQ]),
                                c["head"].unsqueeze(1).unsqueeze(3).broadcast_to([P, GROUP, HH, SEQ]),
                                ALU.mult).then_inc(s("q1p_ok"), 1)

            rotated1(0)
            rotated1(1)
            for st in range(16):
                pool.wait_ge(s("e1_ok"), st + 1)
                v = E1[:, st % 2, 0].rearrange("p a b c -> p (a b) c")
                G.tensor_tensor(v, v, c["keep"].unsqueeze(1).broadcast_to([P, 8, SEQ]), ALU.mult)\
                    .then_inc(s("e1m_ok"), 1)
                if st % 4 == 3 and st < 8:
                    rotated1(st // 4 + 2)

            def by_expert(v):
                return v.rearrange("p (n s) -> p n s", s=SP)

            def sub_d(u):
                hf, t = u // TILES, u % TILES
                pool.wait_ge(s("mD"), u + 1)
                if u >= 2:
                    pool.wait_ge(s("xt_mm"), u - 1)
                G.tensor_tensor(by_expert(Eb[:, u % 2]), by_expert(L[:, t, hf * HALF:(hf + 1) * HALF]),
                                smD[:, u % 2, 0, :].unsqueeze(2).broadcast_to([P, HALF // SP, SP]),
                                ALU.subtract).then_inc(s("sD"), 1)

            def norm_d(u):
                pool.wait_ge(s("rD"), u + 1)
                G.tensor_tensor(by_expert(Eb[:, u % 2]), by_expert(Eb[:, u % 2]),
                                smD[:, u % 2, 1, :].unsqueeze(2).broadcast_to([P, HALF // SP, SP]),
                                ALU.mult).then_inc(s("nD"), 1)

            def sub_c(t):
                pool.wait_ge(s("mC"), t + 1)
                pool.wait_ge(s("sD"), TILES + t + 1)
                G.tensor_tensor(by_expert(L[:, t, :]), by_expert(L[:, t, :]),
                                smC[:, t % 2, 0, :].unsqueeze(1).broadcast_to([P, SE, SP]),
                                ALU.subtract).then_inc(s("sC"), 1)

            for u in range(2 * TILES + 1):
                if u < 2 * TILES:
                    sub_d(u)
                if u > TILES:
                    sub_c(u - TILES - 1)
                if u >= 1:
                    norm_d(u - 1)


def vit_tower(nc, *args):
    build(nc, dict(zip(NAMES, args[:-1])), args[-1])


NAMES = ["patches", "tok_w", "tok_b", "wq0", "wk0", "wv0", "wo0", "bo0", "rel_emb", "gate_w", "route_b", "moe_w",
         "wq1", "wqs1", "wk1", "wks1", "wv1", "wo1", "bo1", "phi_w", "phi_b", "expert_w", "expert_b", "cf", "cb"]


def constants(np):
    cf = np.zeros((P, CF_W), np.float32)
    cb = np.zeros((P, CB_W), np.float32)

    def f(n):
        return cf[:, CF[n][0]:CF[n][0] + CF[n][1]]

    def b(n):
        return cb[:, CB[n][0]:CB[n][0] + CB[n][1]]

    p = np.arange(P)
    f("ident")[:] = np.eye(P)
    f("head")[:] = (p[:, None] // DH == np.arange(HH)[None])
    q, k = p % SLOT, np.arange(SEQ)
    f("cmask")[:] = np.where((k[None] > q[:, None]), -3e38, 0.0)
    f("keep")[:] = (q[:, None] <= k[None])
    f("ones32")[:] = ((p[:, None] // SLOT == np.arange(32)[None] // DH) & (q[:, None] < SEQ))
    f("iota")[:] = np.arange(NEXP)[None]
    d = p % DH
    theta = (np.float32(10000.0) ** (np.float32(-2.0) * ((d // 2).astype(np.float32) - np.float32(1.0)) / np.float32(DH)))
    ang = (np.arange(SEQ, dtype=np.float32)[None] * theta[:, None].astype(np.float32)).astype(np.float32)
    f("cos")[:] = np.cos(ang.astype(np.float64))
    f("sin")[:] = np.sin(ang.astype(np.float64)) * np.where(d % 2 == 0, 1.0, -1.0)[:, None]
    b("before")[:] = (p[:, None] < p[None])
    b("ones")[:] = 1.0
    n = np.maximum(np.arange(SEQ + SLOT - 1) - (SEQ - 1), 0)
    exact = BUCKETS // 2
    large = exact + (np.log(np.maximum(n, 1).astype(np.float32) / exact) / np.log(np.float32(128 / exact))
                     * (BUCKETS - exact)).astype(np.int32)
    bucket = np.where(n < exact, n, np.minimum(large, BUCKETS - 1))
    for part in range(3):
        for i in range(BUCKETS):
            b("bucket")[part * BUCKETS + i] = (bucket == i)
    return cf, cb


def kernel(**inputs):
    import numpy as _np
    import concourse.bacc as _bacc
    from concourse import mybir as _mybir
    from concourse.bass_utils import run_bass_kernel_spmd as _run

    i = {n: _np.asarray(v) for n, v in inputs.items()}
    side = int(round(SEQ ** 0.5))
    px = 16

    def by_parity(w):
        return w.reshape(D, HEADS // 2, 2, DH).transpose(0, 2, 1, 3).reshape(D, D)

    def partners(w):
        return w.reshape(D, D // 2, 2)[:, :, ::-1].reshape(D, D)

    def expert(w1, w3, w2):
        n = w1.shape[0]
        up = [w.reshape(n, KD, P, P).transpose(0, 2, 1, 3).reshape(n, P, KD * P) for w in (w1, w3)]
        return _np.concatenate(up + [w2], axis=2)

    qkv = i["L1_attn_w_qkv"].T
    q1, k1, v1 = qkv[:, 0:D], qkv[:, D:2 * D], qkv[:, 2 * D:3 * D]
    cf, cb = constants(_np)
    host = {
        "patches": i["x"].reshape(NIMG, 3, side, px, side, px).transpose(1, 3, 5, 0, 2, 4).reshape(3 * px * px, TOK),
        "tok_w": i["L0_tok_W"], "tok_b": i["L0_tok_b"].reshape(KD, P).T,
        "wq0": i["L0_attn_Wq"], "wk0": i["L0_attn_Wk"], "wv0": by_parity(i["L0_attn_Wv"]), "wo0": i["L0_attn_Wo"],
        "bo0": i["L0_attn_bo"], "rel_emb": i["L0_attn_rel_emb"],
        "gate_w": i["L0_ffn_gate_w"].T, "route_b": i["L0_ffn_bias"],
        "moe_w": _np.concatenate([
            expert(i["L0_ffn_sw1"].T[None], i["L0_ffn_sw3"].T[None], i["L0_ffn_sw2"].T[None]),
            expert(i["L0_ffn_W1"], i["L0_ffn_W3"], i["L0_ffn_W2"])]),
        "wq1": q1, "wqs1": partners(q1), "wk1": k1, "wks1": partners(k1), "wv1": by_parity(v1),
        "wo1": i["L1_attn_w_out"].T, "bo1": i["L1_attn_b_out"],
        "phi_w": i["L1_ffn_phi_w"].T, "phi_b": i["L1_ffn_phi_b"],
        "expert_w": i["L1_ffn_expert_w"], "expert_b": i["L1_ffn_expert_b"],
        "cf": cf, "cb": cb.astype(i["L0_ffn_gate_w"].dtype),
    }
    nc = _bacc.Bacc("TRN2", target_bir_lowering=False, num_devices=1)
    arrays, args = {}, []
    for name in NAMES:
        v = _np.ascontiguousarray(host[name])
        arrays[f"in_{name}_dram"] = v
        args.append(nc.dram_tensor(f"in_{name}_dram", v.shape, _mybir.dt.from_np(v.dtype), kind="ExternalInput").ap())
    out = nc.dram_tensor("out_0_dram", (TOK, D), _mybir.dt.float32, kind="ExternalOutput").ap()
    vit_tower(nc, *args, out)
    r = _run(nc, [arrays], core_ids=[0])
    return r.results[0]["out_0_dram"].reshape(NIMG, SEQ, D)
```

```python
from contextlib import ExitStack

import concourse.bass as bass
from concourse import mybir

ALU = mybir.AluOpType
ACT = mybir.ActivationFunctionType
AX = mybir.AxisListType
F32 = mybir.dt.float32
F16 = mybir.dt.float16
BF16 = mybir.dt.bfloat16
U32 = mybir.dt.uint32

P = 128
NIMG, SEQ = 16, 36
TOK = NIMG * SEQ
D = 256
KD = D // P
TILES = -(-TOK // P)
TPAD = TILES * P
LAST = TOK - (TILES - 1) * P
HEADS, DH = 16, 16
HH = HEADS // KD
GROUP = NIMG // 2
GT = GROUP * SEQ
SLOT = 64
PAIRS = NIMG // 2
PATCH_K = 768 // P
NEXP, TOPK, CAP = 32, 4, 256
CHUNKS = [(0, 256), (256, TOK - 256)]
SE, SP = 64, 32
NP_ = SE * SP
NPT = NP_ // P
HALF = NP_ // 2
EPS = 1e-5
SCALE = DH ** -0.5
MOE_W = 2 * KD * P + D
MOE_CHUNK = 3
PARTS = 4
MOE_LAG = 4
UNITS = 2 * (NEXP + 1)
EW_SLOTS = 32
EW_DMA = 2
BUCKETS = 32

CF = {}
CB = {}
_at = 0
for _n, _w in (("ident", P), ("head", HH), ("cmask", SEQ), ("keep", SEQ), ("ones32", 32), ("iota", NEXP),
               ("cos", SEQ), ("sin", SEQ)):
    CF[_n] = (_at, _w)
    _at += _w
CF_W = _at
_at = 0
for _n, _w in (("before", P), ("ones", P), ("bucket", SEQ + SLOT - 1)):
    CB[_n] = (_at, _w)
    _at += _w
CB_W = _at + _at % 2


class Chain:

    def __init__(self, eng, sem):
        self.eng, self.sem, self.n = eng, sem, 0

    def mark(self, ins):
        ins.then_inc(self.sem, 1)
        self.n += 1
        return self.n

    def need(self, n):
        self.eng.wait_ge(self.sem, n)

    def link(self, ins):
        self.need(self.mark(ins))


def build(nc, a, out):
    ctx = ExitStack()
    with ctx:
        def sb(name, shape, dt=F32):
            return ctx.enter_context(nc.sbuf_tensor("sb_" + name, shape, dt))

        def sem(name):
            return ctx.enter_context(nc.semaphore(name))

        bank = [ctx.enter_context(nc.psum_tensor(f"bank{i}", [P, 512], F32)) for i in range(8)]

        cf = sb("cf", [P, CF_W])
        cb = sb("cb", [P, CB_W], BF16)
        c = {n: cf[:, o:o + w] for n, (o, w) in CF.items()}
        cbv = {n: cb[:, o:o + w] for n, (o, w) in CB.items()}
        ident = c["ident"]
        tokb = sb("tokb", [P, KD])
        attn_b = sb("attn_b", [P, D])
        route_b = sb("route_b", [P, NEXP])
        relp = sb("relp", [96, HEADS], BF16)
        relf = sb("relf", [BUCKETS, 2, HEADS])
        gate_w = sb("gate_w", [P, KD, NEXP], BF16)
        aw = sb("aw", [P, 6, KD, D])
        phi = sb("phi", [P, KD, NP_])
        h = sb("h", [P, TILES, D])
        hT = sb("hT", [P, KD, TPAD])
        xhi = sb("xhi", [P, KD, TPAD], F16)
        xlo = sb("xlo", [P, KD, TPAD], F16)
        stats = sb("stats", [P, 8, 6])
        mv = sb("mv", [P, 8, 2])
        ln = sb("ln", [P, 5, 8])
        ew = sb("ew", [P, EW_SLOTS, KD, D])
        moe_slots = -(-(NEXP + 1) * MOE_W // (2 * KD * D))
        ew_first = EW_SLOTS - moe_slots
        moe_w = ew[:, ew_first:, :, :].rearrange("p a b c -> p (a b c)").bitcast(BF16)[:, 0:(NEXP + 1) * MOE_W]
        moe_w = moe_w.rearrange("p (e w) -> p e w", w=MOE_W)

        R1 = 24800
        r1 = sb("r1", [P, R1])

        def carve(at, *shape):
            n = 1
            for s in shape:
                n *= s
            v = r1[:, at:at + n]
            assert at + n <= R1, (at, shape)
            if len(shape) > 1:
                names = "abcdef"[:len(shape)]
                v = v.rearrange("p (" + " ".join(names) + ") -> p " + " ".join(names),
                                **{x: s for x, s in zip(names[1:], shape[1:])})
            return v

        patches = carve(0, PATCH_K, TOK)
        tokw = carve(PATCH_K * TOK, PATCH_K, D)
        BD = carve(0, 4, GROUP, HH, SEQ)
        at = 4 * GROUP * HH * SEQ
        Vbd = carve(at, NIMG, HEADS // 2, 32); at += NIMG * HEADS // 2 * 32
        xTi = carve(at, KD, NIMG, SLOT); at += KD * NIMG * SLOT
        pads = carve(at, 2, KD, NIMG, SLOT); at += 2 * KD * NIMG * SLOT
        oT = carve(at, KD, TPAD); at += KD * TPAD
        low = at
        pad1 = at - KD * TPAD - KD * NIMG * SLOT
        S0 = carve(pad1, 3, HEADS, SEQ)
        bias0 = carve(at, HEADS, SEQ); at += HEADS * SEQ
        Pb = carve(at, 2, HEADS // 2, 2, SLOT); at += 2 * HEADS * SLOT
        PT = carve(at, 2, HEADS // 2, 2, SEQ); at += 2 * HEADS * SEQ
        sm0 = carve(at, 3, 3, HEADS); at += 9 * HEADS
        at = low
        Qs = carve(at, 2, 4, GT); at += 8 * GT
        rt = carve(at, 2, 2, GT)
        E1 = carve(at, 3, 2, 2, 4, SEQ); at += 12 * 4 * SEQ
        dn1 = xhi[:, 0, 0:8 * SEQ].bitcast(F32).rearrange("p (a b) -> p a b", a=2)
        at = 0
        act_s = carve(at, 2, 320); at += 640
        act_p = carve(at, 2, 320); at += 640
        act_m = carve(at, 3, 320); at += 960
        act_r = carve(at, 2, 320); at += 640
        parts = carve(at, PARTS * 3 * 160).bitcast(BF16).rearrange("p (u j n) -> p u j n", u=PARTS, j=3)
        at += PARTS * 3 * 160
        gbc = carve(at, 3, TOK); at += 3 * TOK
        gT = carve(at, TPAD); at += TPAD
        rsc = carve(at, 8, TILES, NEXP); at += 8 * TILES * NEXP
        rmask = carve(at, TILES * NEXP // 2); at += TILES * NEXP // 2
        rmax = carve(at, TILES, 8); at += 8 * TILES
        ridx = carve(at, TILES, 8); at += 8 * TILES
        req = carve(at, TILES, NEXP, TOPK); at += TILES * NEXP * TOPK
        rsum = carve(at, 2, TILES); at += 2 * TILES
        maskb = rmask.bitcast(BF16).rearrange("p (t e) -> p t e", t=TILES)
        at = 0
        L = carve(at, TILES, NP_); at += TILES * NP_
        phib = carve(at, NP_); at += NP_
        ebr = carve(at, 2, D); at += 2 * D
        Eb = carve(at, 4, HALF)
        CT = carve(at, 2, NPT, P); at += 2 * NPT * P
        XTt = carve(at, 2, KD, P); at += 2 * KD * P
        Yt = carve(at, NPT, D); at += NPT * D
        smD = carve(at, 2, 2, HALF // SP); at += 4 * HALF // SP
        smC = carve(at, TILES, 2, SP); at += 2 * TILES * SP
        Xs = Yt

        phi_slots = phi[:, :, :].rearrange("p k n -> p (k n)").rearrange("p (s k h) -> p s k h", k=KD, h=D)
        AW_SLOTS, PHI_SLOTS = 6, NP_ // D
        AGAIN = EW_SLOTS + AW_SLOTS + PHI_SLOTS

        def expert_at(e, n=1):
            if e < EW_SLOTS:
                return ew[:, e:e + n]
            if e < EW_SLOTS + AW_SLOTS:
                return aw[:, e - EW_SLOTS:e - EW_SLOTS + n]
            if e < AGAIN:
                return phi_slots[:, e - EW_SLOTS - AW_SLOTS:e - EW_SLOTS - AW_SLOTS + n]
            return ew[:, e - AGAIN:e - AGAIN + n]

        gT_dram = nc.dram_tensor("gT_scratch", [NEXP, TOK], F32, kind="Internal").ap()

        S = {}

        def s(name):
            if name not in S:
                S[name] = sem(name)
            return S[name]

        for n in ("ld_bo1 ld_const ld_attn0 ld_attn1 ld_phi ld_phib ld_gate ld_out "
                  "dve_chain").split():
            s(n)
        ld_moe = [sem(f"ld_moe{i}") for i in range(-(-(NEXP + 1) // MOE_CHUNK))]
        ld_ew = [sem(f"ld_ew{i}") for i in range(EW_SLOTS // EW_DMA)]
        ld_patch = [sem(f"ld_patch{i}") for i in range(PATCH_K)]
        ld_g = [sem(f"ld_g{i}") for i in range(3)]
        ld_eb = [sem(f"ld_eb{i}") for i in range(2)]
        for n in ("hT_mm hT_sb h_tr h_res xTi_ok zero_ok bias_mm bias_ok relp_ok "
                  "q_mm q_sb k_mm kbd_ok kbd_act v_mm v_sb_a v_sb_d sc_mm sc_free mx_ok sub_ok exp_ok rs_ok p_ok "
                  "tr_mm pt_ok av_mm oT_ok wo_mm r_ok var_ok std_ok ln_ok lnT_mm lnT_sb "
                  "route_mm route_sc mask_ok pos_mm g_ok gT_mm gT_sb g_st ab_mm silu_ok p1_ok m_ok hi_ok rest_ok "
                  "mid_ok parts_ok w2_used "
                  "x1T qk_mm qk_act qk_dve rope_ok rope_free x1i q1d_ok q1p_ok v1_mm v1_a v1_d s1_mm e1_ok e1m_ok av1_mm o1_ok "
                  "wo1_mm l_mm l_sb mD sD eD rD nD xt_mm xt_sb mC sC eC rC nC xvar xstd xln xtan xtT_mm xtT_sb "
                  "yt_mm yt_sb ct_mm ct_sb y_mm y_sb fin_ok hT_zero xhi_ok").split():
            s(n)

        block = ctx.enter_context(nc.Block())

        def tiles(t):
            return P if t < TILES - 1 else LAST

        def rows(b, t):
            return bank[b + t // 2][:, (t % 2) * D:(t % 2 + 1) * D]

        def piece(g, dh):
            return dh * 2 + g

        @block.sync
        def _(sp):
            for k in range(PATCH_K):
                sp.dma_start(tokw[:, k, :], a["tok_w"][k * P:(k + 1) * P, :]).then_inc(ld_patch[k], 16)
                sp.dma_start(patches[:, k, :], a["patches"][k * P:(k + 1) * P, :]).then_inc(ld_patch[k], 16)
            sp.dma_start(cf[:, :], a["cf"]).then_inc(s("ld_const"), 16)
            sp.dma_start(cb[:, :], a["cb"]).then_inc(s("ld_const"), 16)
            sp.dma_start(tokb[:, :], a["tok_b"]).then_inc(s("ld_const"), 16)
            sp.dma_start(attn_b[:, :], a["bo0"].partition_broadcast(P)).then_inc(s("ld_const"), 16)
            sp.dma_start(route_b[:, :], a["route_b"].partition_broadcast(P)).then_inc(s("ld_const"), 16)
            sp.dma_start(relf[:, 0, :], a["rel_emb"]).then_inc(s("ld_const"), 16)
            for i, n in enumerate(("wq0", "wk0", "wv0", "wo0")):
                sp.dma_start(aw[:, i], a[n].rearrange("(k p) n -> p k n", p=P)).then_inc(s("ld_attn0"), 16)
            sp.dma_start(gate_w[:, :, :], a["gate_w"].rearrange("(k p) n -> p k n", p=P)).then_inc(s("ld_gate"), 16)
            for i, q in enumerate(ld_moe):
                e0 = i * MOE_CHUNK
                e1 = min(e0 + MOE_CHUNK, NEXP + 1)
                sp.dma_start(moe_w[:, e0:e1, :], a["moe_w"][e0:e1].rearrange("e p w -> p e w")).then_inc(q, 16)
            for k in range(KD):
                sp.dma_start(phi[:, k, :], a["phi_w"][k * P:(k + 1) * P, :]).then_inc(s("ld_phi"), 16)
            sp.wait_ge(s("wo_mm"), TILES)
            sp.wait_ge(s("h_res"), 3)
            for i, n in enumerate(("wq1", "wqs1", "wk1", "wks1", "wv1", "wo1")):
                sp.dma_start(aw[:, i], a[n].rearrange("(k p) n -> p k n", p=P)).then_inc(s("ld_attn1"), 16)
            sp.wait_ge(s("gT_sb"), 2)
            sp.dma_start(gT_dram, gT[0:NEXP, 0:TOK]).then_inc(s("g_st"), 16)
            sp.wait_ge(s("g_st"), 16)
            for e in range(NEXP):
                if e >= 3:
                    sp.wait_ge(s("m_ok"), 2 * (e - 1))
                sp.dma_start(gbc[:, e % 3, :], gT_dram[e].partition_broadcast(P)).then_inc(ld_g[e % 3], 16)
            sp.wait_ge(s("w2_used"), UNITS)
            sp.dma_start(attn_b[:, :], a["bo1"].partition_broadcast(P)).then_inc(s("ld_bo1"), 16)
            ewd = a["expert_w"].rearrange("n (k p) h -> p n k h", p=P)

            def load_experts(e0, e1):
                for e in range(e0, e1, EW_DMA):
                    i = e // EW_DMA
                    if i >= len(ld_ew):
                        sp.wait_ge(ld_ew[i % len(ld_ew)], 16)
                    sp.dma_start(expert_at(e, EW_DMA).rearrange("p n k h -> p (n k) h"),
                                 ewd[:, e:e + EW_DMA].rearrange("p n k h -> p (n k) h")).then_inc(ld_ew[i % len(ld_ew)], 16)

            def slot_bias(n):
                for j in range(4):
                    sp.dma_start(ebr[32 * j:32 * j + 32, n % 2, :],
                                 a["expert_b"][4 * n + j].partition_broadcast(32)).then_inc(ld_eb[n % 2], 16)

            load_experts(0, EW_SLOTS)
            sp.wait_ge(s("wo1_mm"), TILES)
            sp.dma_start(phib, a["phi_b"].partition_broadcast(P)).then_inc(s("ld_phib"), 16)
            load_experts(EW_SLOTS, EW_SLOTS + AW_SLOTS)
            slot_bias(0)
            slot_bias(1)
            sp.wait_ge(s("l_mm"), 4 * TILES)
            load_experts(EW_SLOTS + AW_SLOTS, AGAIN)
            for n in range(2, NPT):
                sp.wait_ge(s("yt_sb"), n - 1)
                slot_bias(n)
                e = AGAIN + 4 * (n - 2)
                if e < SE:
                    load_experts(e, min(e + 4, SE))
            outs = 0
            for t in range(TILES):
                sp.wait_ge(s("fin_ok"), t + 1)
                n = tiles(t)
                sp.dma_start(out[t * P:t * P + n, :], h[0:n, t, :]).then_inc(s("ld_out"), 16)
                outs += 16
            sp.wait_ge(s("ld_out"), outs)

        @block.tensor
        def _(pe):
            mm = nc.tensor.matmul

            def proj(b, w, g, dh, src=hT):
                for k in range(KD):
                    m = mm(bank[b][:, 0:GT], aw[:, w, k, dh * P:(dh + 1) * P], src[:, k, g * GT:(g + 1) * GT],
                           start=(k == 0), stop=(k == KD - 1))
                return m

            def values(w, b, signal):
                for j in range(2):
                    for k in range(KD):
                        m = mm(bank[b][:, j * D:(j + 1) * D],
                               xTi[:, k, 4 * b + 2 * j:4 * b + 2 * j + 2, :].rearrange("p i t -> p (i t)"),
                               aw[:, w, k, :], start=(k == 0), stop=(k == KD - 1), skip_group_check=True)
                m.then_inc(s(signal), 1)

            def out_proj(w, signal):
                for t in range(TILES):
                    for k in range(KD):
                        m = mm(rows(0, t), oT[:, k, t * P:(t + 1) * P], aw[:, w, k, :],
                               start=(k == 0), stop=(k == KD - 1), skip_group_check=True)
                    m.then_inc(s(signal), 1)

            def turn(base):
                for t in range(TILES):
                    pe.wait_ge(s("ln_ok"), base + t + 1)
                    for dh in range(KD):
                        to = bank[3 + dh][:, t * P:(t + 1) * P] if t < 4 else bank[5][:, dh * P:(dh + 1) * P]
                        m = nc.tensor.transpose(to, h[:, t, dh * P:(dh + 1) * P], ident)
                m.then_inc(s("lnT_mm"), 1)

            for k in range(PATCH_K):
                pe.wait_ge(ld_patch[k], 32)
                for dh in range(KD):
                    for g in range(2):
                        m = mm(bank[piece(g, dh)][:, 0:GT], tokw[:, k, dh * P:(dh + 1) * P],
                               patches[:, k, g * GT:(g + 1) * GT], start=(k == 0), stop=(k == PATCH_K - 1))
                        if k == PATCH_K - 1:
                            m.then_inc(s("hT_mm"), 1)
            pe.wait_ge(s("relp_ok"), 1)
            ob = CB["bucket"][0]
            for hf in range(2):
                for kk in range(SEQ // 2):
                    k = hf * (SEQ // 2) + kk
                    for im in range(2):
                        m = mm(bank[6 + hf][64 * im:64 * im + 64, kk * HEADS:(kk + 1) * HEADS],
                               cb[0:96, ob + SEQ - 1 - k:ob + SEQ - 1 - k + SLOT], relp[:, :],
                               start=True, stop=True, skip_group_check=True)
            m.then_inc(s("bias_mm"), 1)
            pe.wait_ge(s("hT_sb"), 4)
            pe.wait_ge(s("hT_zero"), 1)
            for t in range(TILES):
                b = 4 + (t // 2) % 2
                if t == 4:
                    pe.wait_ge(s("h_res"), 1)
                for dh in range(KD):
                    m = nc.tensor.transpose(bank[b][:, (t % 2) * D + dh * P:(t % 2) * D + (dh + 1) * P],
                                            hT[:, dh, t * P:(t + 1) * P], ident)
                if t % 2 == 1 or t == 4:
                    m.then_inc(s("h_tr"), 1)
            pe.wait_ge(s("ld_attn0"), 64)
            for dh in range(KD):
                for g in range(2):
                    proj(piece(g, dh), 0, g, dh).then_inc(s("q_mm"), 1)
            pe.wait_ge(s("h_res"), 3)
            pe.wait_ge(s("bias_ok"), 1)
            for dh in range(KD):
                for g in range(2):
                    proj(4 + piece(g, dh), 1, g, dh).then_inc(s("k_mm"), 1)
            pe.wait_ge(s("xTi_ok"), 2)
            for b in range(4):
                pe.wait_ge(s("q_sb"), b + 1)
                values(2, b, "v_mm")

            def scores0(i):
                if i == 0:
                    pe.wait_ge(s("q_sb"), 4)
                    pe.wait_ge(s("kbd_ok"), 3)
                    pe.wait_ge(s("kbd_act"), 1)
                    pe.wait_ge(s("v_sb_a"), 4)
                    pe.wait_ge(s("v_sb_d"), 4)
                if i >= 2:
                    pe.wait_ge(s("sc_free"), i - 1)
                for dh in range(KD):
                    for im in range(2):
                        img = 2 * i + im
                        m = mm(bank[2 * (i % 2) + dh][64 * im:64 * im + 64, 0:HH * SEQ], pads[:, 0, dh, img, :],
                               BD[:, piece(img // GROUP, dh), img % GROUP].rearrange("p a b -> p (a b)"),
                               start=True, stop=True, skip_group_check=True)
                m.then_inc(s("sc_mm"), 1)

            def turn0(i):
                pe.wait_ge(s("p_ok"), i + 1)
                if i >= 1:
                    pe.wait_ge(s("pt_ok"), i)
                for hp in range(HEADS // 2):
                    m = nc.tensor.transpose(bank[4 + hp // 4][:, (hp % 4) * P:(hp % 4 + 1) * P],
                                            Pb[:, i % 2, hp].rearrange("p a b -> p (a b)"), ident)
                m.then_inc(s("tr_mm"), 1)

            def apply0(i):
                pe.wait_ge(s("pt_ok"), i + 1)
                if i >= 2:
                    pe.wait_ge(s("oT_ok"), i - 1)
                for im in range(2):
                    for hp in range(HEADS // 2):
                        m = mm(bank[6 + i % 2][32 * (hp % 4):32 * (hp % 4) + 32,
                                              (hp // 4) * 2 * SEQ + im * SEQ:(hp // 4) * 2 * SEQ + (im + 1) * SEQ],
                               Vbd[:, 2 * i + im, hp, :], PT[:, i % 2, hp, im, :],
                               start=True, stop=True, skip_group_check=True)
                m.then_inc(s("av_mm"), 1)

            for i in range(PAIRS + 3):
                if i < PAIRS:
                    scores0(i)
                if 2 <= i < PAIRS + 2:
                    turn0(i - 2)
                if i >= 3:
                    apply0(i - 3)
            pe.wait_ge(s("oT_ok"), PAIRS)
            pe.wait_ge(s("sc_free"), PAIRS)
            out_proj(3, "wo_mm")
            turn(0)

            pe.wait_ge(s("lnT_sb"), 2)
            pe.wait_ge(s("ld_gate"), 16)
            for t in range(TILES):
                n = 0
                for part in (xhi, xlo):
                    for k in range(KD):
                        m = mm(bank[7][:, t * NEXP:(t + 1) * NEXP], part[:, k, t * P:(t + 1) * P], gate_w[:, k, :],
                               start=(n == 0), stop=(n == 3), skip_group_check=True)
                        n += 1
            m.then_inc(s("route_mm"), 1)

            def queue_places():
                pe.wait_ge(s("mask_ok"), 1)
                for t in range(TILES):
                    for j in range(t + 1):
                        m = mm(bank[7][:, t * NEXP:(t + 1) * NEXP], cbv["before" if j == t else "ones"],
                               maskb[:, j, :], start=(j == 0), stop=(j == t), skip_group_check=True)
                m.then_inc(s("pos_mm"), 1)

            def turn_gates():
                pe.wait_ge(s("g_ok"), 1)
                for t in range(TILES):
                    b, o = (7, t * P) if t < 4 else (0, 0)
                    m = nc.tensor.transpose(bank[b][0:NEXP, o:o + P], rsc[:, 5, t, :], ident)
                m.then_inc(s("gT_mm"), 1)

            def up(u):
                e, ch = u // 2, u % 2
                t0, n = CHUNKS[ch]
                pe.wait_ge(ld_moe[e // MOE_CHUNK], 16)
                if u >= 2:
                    pe.wait_ge(s("p1_ok"), u - 1)
                for b in range(2):
                    j = 0
                    for part in (xhi, xlo):
                        for k in range(KD):
                            o = (b * KD + k) * P
                            m = mm(bank[3 + 2 * (u % 2) + b][:, 0:n], moe_w[:, e, o:o + P], part[:, k, t0:t0 + n],
                                   start=(j == 0), stop=(j == 3))
                            j += 1
                m.then_inc(s("ab_mm"), 1)

            def down(u):
                e, ch = u // 2, u % 2
                t0, n = CHUNKS[ch]
                pe.wait_ge(s("parts_ok"), u + 1)
                if u == 0:
                    pe.wait_ge(s("gT_sb"), 2)
                for t in range(t0 // P, -(-(t0 + n) // P)):
                    k = tiles(t)
                    for j in range(3):
                        m = mm(rows(0, t)[0:k], parts[:, u % PARTS, j, t * P - t0:t * P - t0 + k],
                               moe_w[:, e, 2 * KD * P:MOE_W], start=(e == 0 and t % 2 == 0 and j == 0),
                               stop=(e == NEXP and j == 2), skip_group_check=True)
                m.then_inc(s("w2_used"), 1)

            for u in range(UNITS + MOE_LAG):
                if u < UNITS:
                    up(u)
                if u == 1:
                    queue_places()
                    turn_gates()
                if u >= MOE_LAG:
                    down(u - MOE_LAG)
            turn(TILES)

            pe.wait_ge(s("lnT_sb"), 4)
            pe.wait_ge(s("ld_attn1"), 96)
            for n in range(8):
                g, dh = n % 2, (n // 2) % 2
                if n >= 4:
                    pe.wait_ge(s("qk_act"), n - 3)
                    pe.wait_ge(s("qk_dve"), n - 3)
                for w in range(2):
                    m = proj(2 * (n % 4) + w, 2 * (n // 4) + w, g, dh)
                m.then_inc(s("qk_mm"), 1)
            pe.wait_ge(s("x1i"), 2)
            for b in range(4):
                if b % 2 == 0:
                    pe.wait_ge(s("qk_act"), 5 + b // 2)
                    pe.wait_ge(s("qk_dve"), 5 + b // 2)
                values(4, b, "v1_mm")

            def scores1(st):
                u, j = st // 4, st % 4
                g, dh = u // 2, u % 2
                if st == 0:
                    pe.wait_ge(s("rope_ok"), 8)
                    pe.wait_ge(s("qk_act"), 8)
                    pe.wait_ge(s("v1_a"), 4)
                    pe.wait_ge(s("v1_d"), 4)
                if j == 0:
                    pe.wait_ge(s("q1d_ok"), u + 1)
                    pe.wait_ge(s("q1p_ok"), u + 1)
                if st >= 2:
                    pe.wait_ge(s("e1_ok"), st - 1)
                for kind in range(2):
                    bd = BD[:, 2 * (u % 2) + kind]
                    for im in range(2):
                        for par in range(2):
                            img = 2 * j + im
                            m = mm(bank[2 * (st % 2) + kind][64 * par:64 * par + 64, im * 144:(im + 1) * 144],
                                   pads[:, kind, dh, g * GROUP + img, :],
                                   bd[:, img].rearrange("p (a b) c -> p a b c", b=2)[:, :, par, :],
                                   start=True, stop=True, skip_group_check=True)
                m.then_inc(s("s1_mm"), 1)

            def apply1(st):
                u, j = st // 4, st % 4
                g, dh = u // 2, u % 2
                pe.wait_ge(s("e1m_ok"), st + 1)
                if st >= 2:
                    pe.wait_ge(s("o1_ok"), st - 1)
                for hp in range(4):
                    to = bank[4 + 2 * (st % 2)][32 * hp:32 * hp + 32, :]
                    for im in range(2):
                        mm(to[:, im * SEQ:(im + 1) * SEQ], Vbd[:, g * GROUP + 2 * j + im, dh * 4 + hp, :],
                           E1[:, st % 3, 0, im, hp, :], start=True, stop=True, skip_group_check=True)
                    m = mm(bank[5 + 2 * (st % 2)][32 * hp:32 * hp + 32, 0:2 * SEQ], c["ones32"],
                           E1[:, st % 3, 1, :, hp, :], start=True, stop=True, skip_group_check=True)
                m.then_inc(s("av1_mm"), 1)

            for st in range(18):
                if st < 16:
                    scores1(st)
                if st >= 2:
                    apply1(st - 2)
            pe.wait_ge(s("o1_ok"), 16)
            pe.wait_ge(s("e1_ok"), 16)
            out_proj(5, "wo1_mm")
            turn(2 * TILES)

            pe.wait_ge(s("lnT_sb"), 6)
            pe.wait_ge(s("ld_phi"), 32)

            def logits(u):
                hf, t = u // TILES, u % TILES
                for q in range(2):
                    n = 2 * u + q
                    if n >= 4:
                        pe.wait_ge(s("l_sb"), n - 3)
                    o = hf * HALF + q * 512
                    for k in range(KD):
                        m = mm(bank[n % 4][:, :], hT[:, k, t * P:(t + 1) * P], phi[:, k, o:o + 512],
                               start=(k == 0), stop=(k == KD - 1))
                    m.then_inc(s("l_mm"), 1)

            def gather(u):
                hf, t = u // TILES, u % TILES
                pe.wait_ge(s("nD"), u + 1)
                if u == TILES:
                    pe.wait_ge(s("xt_sb"), 4)
                k = tiles(t)
                for n in range(8):
                    m = mm(bank[4 + n // 2][:, (n % 2) * D:(n % 2 + 1) * D], Eb[0:k, u % 4, n * P:(n + 1) * P],
                           h[0:k, t, :], start=(t == 0 and n % 2 == 0), stop=(t == TILES - 1),
                           skip_group_check=True)
                m.then_inc(s("xt_mm"), 1)

            def slots_in(n):
                pe.wait_ge(s("xtan"), n + 1)
                if n >= 2:
                    pe.wait_ge(s("xtT_sb"), n - 1)
                for k in range(KD):
                    m = nc.tensor.transpose(bank[n % 2][:, k * P:(k + 1) * P], Xs[:, n, k * P:(k + 1) * P], ident)
                m.then_inc(s("xtT_mm"), 1)

            def slots_out(n):
                pe.wait_ge(s("xtT_sb"), n + 1)
                if n >= 2:
                    pe.wait_ge(s("yt_sb"), n - 1)
                for e in range(4 * n, 4 * n + 4, EW_DMA):
                    i = e // EW_DMA
                    pe.wait_ge(ld_ew[i % len(ld_ew)], 16 * (i // len(ld_ew) + 1))
                for k in range(KD):
                    for j in range(4):
                        e = 4 * n + j
                        m = mm(bank[2 + n % 2][32 * j:32 * j + 32, 0:D], XTt[:, n % 2, k, 32 * j:32 * j + 32],
                               expert_at(e)[:, 0, k, :], start=(k == 0), stop=(k == KD - 1), skip_group_check=True)
                m.then_inc(s("yt_mm"), 1)

            def turn_weights(t):
                if t == 0:
                    pe.wait_ge(s("xt_sb"), 8)
                pe.wait_ge(s("nC"), t + 1)
                for b in range(4):
                    if t >= 1:
                        pe.wait_ge(s("ct_sb"), 4 * (t - 1) + b + 1)
                    for q in range(4):
                        n = 4 * b + q
                        m = nc.tensor.transpose(bank[4 + b][:, q * P:(q + 1) * P], L[:, t, n * P:(n + 1) * P], ident)
                    m.then_inc(s("ct_mm"), 1)

            def combine(t):
                pe.wait_ge(s("ct_sb"), 4 * (t + 1))
                if t == 0:
                    pe.wait_ge(s("yt_sb"), NPT)
                    pe.wait_ge(s("xtT_sb"), NPT)
                if t >= 2:
                    pe.wait_ge(s("y_sb"), t - 1)
                k = tiles(t)
                for n in range(NPT):
                    m = mm(bank[t % 2][0:k, 0:D], CT[:, t % 2, n, 0:k], Yt[:, n, :],
                           start=(n == 0), stop=(n == NPT - 1))
                m.then_inc(s("y_mm"), 1)

            def slots(n0, n1):
                for n in range(n0, n1 + 1):
                    if n < n1:
                        slots_in(n)
                    if n > n0:
                        slots_out(n - 1)

            for u in range(2 * TILES + 2):
                if u < 2 * TILES:
                    logits(u)
                if u >= 2:
                    gather(u - 2)
            pe.wait_ge(s("l_sb"), 4 * TILES)
            slots(0, NPT // 2)
            turn_weights(0)
            slots(NPT // 2, NPT)
            for t in range(1, TILES + 1):
                if t < TILES:
                    turn_weights(t)
                combine(t - 1)

        @block.scalar
        def _(act):
            A = nc.scalar.activation

            def scaled_copies(to, src, n, width):
                for hd in range(HH):
                    m = A(to[:, :, hd, :], src, ACT.Copy, scale=c["head"][:, hd:hd + 1])
                return m

            def values_evac(b, im, signal):
                v = bank[b][64 * im:64 * im + 64, :].rearrange("p (j h a d) -> p j h a d", j=2, a=2, d=DH)
                for par in range(2):
                    to = Vbd[64 * par:64 * par + 64, 4 * b:4 * b + 4].rearrange("p (j i) h d -> p j i h d", i=2)
                    m = A(to[:, :, im, :, DH * par:DH * par + DH], v[:, :, :, par, :], ACT.Copy)
                m.then_inc(s(signal), 1)

            def std(n, width):
                act.wait_ge(s("var_ok"), n)
                A(ln[:, 1, 0:width], ln[:, 0, 0:width], ACT.Sqrt).then_inc(s("std_ok"), 1)

            act.wait_ge(s("ld_const"), 96)
            for i in range(4):
                dh, g = i // 2, i % 2
                act.wait_ge(s("hT_mm"), i + 1)
                A(hT[:, dh, g * GT:(g + 1) * GT], bank[i][:, 0:GT], ACT.Identity,
                  bias=tokb[:, dh:dh + 1]).then_inc(s("hT_sb"), 1)
            for i in range(4):
                dh, g = i // 2, i % 2
                act.wait_ge(s("q_mm"), i + 1)
                if i == 0:
                    act.wait_ge(s("zero_ok"), 4)
                A(pads[:, 0, dh, g * GROUP:(g + 1) * GROUP, 0:SEQ],
                  bank[i][:, 0:GT].rearrange("p (i t) -> p i t", i=GROUP), ACT.Copy, scale=SCALE).then_inc(s("q_sb"), 1)
            act.wait_ge(s("k_mm"), 4)
            scaled_copies(BD[:, 3], bank[7][:, 0:GT].rearrange("p (i t) -> p i t", i=GROUP), 0, 0)\
                .then_inc(s("kbd_act"), 1)
            for j in range(4):
                act.wait_ge(s("v_mm"), j + 1)
                values_evac(j, 0, "v_sb_a")

            def evac_pt(i):
                act.wait_ge(s("tr_mm"), i + 1)
                if i >= 2:
                    act.wait_ge(s("av_mm"), i - 1)
                for b in range(2):
                    m = A(PT[:, i % 2, 4 * b:4 * b + 4],
                          bank[4 + b][:, :].rearrange("p (h i q) -> p h i q", h=4, i=2)[:, :, :, 0:SEQ], ACT.Copy)
                m.then_inc(s("pt_ok"), 1)

            for i in range(PAIRS + 2):
                if i < PAIRS:
                    act.wait_ge(s("sub_ok"), i + 1)
                    A(S0[:, i % 3], S0[:, i % 3], ACT.Exp).then_inc(s("exp_ok"), 1)
                if i >= 2:
                    evac_pt(i - 2)
            std(1, TILES)

            act.wait_ge(s("lnT_mm"), 1)
            for dh in range(KD):
                A(xhi[:, dh, 0:4 * P], bank[3 + dh][:, :], ACT.Copy)
                m = A(xhi[:, dh, 4 * P:TPAD], bank[5][:, dh * P:(dh + 1) * P], ACT.Copy)
            m.then_inc(s("xhi_ok"), 1)
            act.wait_ge(s("route_mm"), 1)
            A(rsc[:, 1], bank[7][:, 0:TILES * NEXP].rearrange("p (t e) -> p t e", t=TILES),
              ACT.Sigmoid).then_inc(s("route_sc"), 1)

            def unit(u):
                return u % 2, CHUNKS[u % 2][1]

            def silu(u):
                act.wait_ge(s("ab_mm"), u + 1)
                if u >= 2:
                    act.wait_ge(s("p1_ok"), u - 1)
                A(act_s[:, u % 2, 0:unit(u)[1]], bank[3 + 2 * (u % 2)][:, 0:unit(u)[1]], ACT.Silu)\
                    .then_inc(s("silu_ok"), 1)

            def high(u):
                act.wait_ge(s("m_ok"), u + 1)
                if u >= PARTS:
                    act.wait_ge(s("w2_used"), u - PARTS + 1)
                n = unit(u)[1]
                A(parts[:, u % PARTS, 0, 0:n], act_m[:, u % 3, 0:n], ACT.Copy).then_inc(s("hi_ok"), 1)

            def middle(u):
                act.wait_ge(s("rest_ok"), u + 1)
                n = unit(u)[1]
                A(parts[:, u % PARTS, 1, 0:n], act_r[:, u % 2, 0:n], ACT.Copy).then_inc(s("mid_ok"), 1)

            for u in range(UNITS + 2):
                if u < UNITS:
                    silu(u)
                if u == 1:
                    act.wait_ge(s("gT_mm"), 1)
                    A(gT[0:NEXP, 0:4 * P], bank[7][0:NEXP, :], ACT.Copy).then_inc(s("gT_sb"), 1)
                    A(gT[0:NEXP, 4 * P:TPAD], bank[0][0:NEXP, 0:P], ACT.Copy).then_inc(s("gT_sb"), 1)
                if 1 <= u <= UNITS:
                    high(u - 1)
                if u >= 2:
                    middle(u - 2)
            std(2, TILES)

            act.wait_ge(s("lnT_mm"), 2)
            for dh in range(KD):
                A(hT[:, dh, 0:4 * P], bank[3 + dh][:, :], ACT.Copy)
                m = A(hT[:, dh, 4 * P:TPAD], bank[5][:, dh * P:(dh + 1) * P], ACT.Copy)
                m.then_inc(s("lnT_sb"), 1)
            for n in range(8):
                g, dh = n % 2, (n // 2) % 2
                act.wait_ge(s("qk_dve"), n + 1)
                src = bank[2 * (n % 4)][:, 0:GT]
                if n < 4:
                    A(Qs[:, 1, 2 * g + dh, :], src, ACT.Copy).then_inc(s("qk_act"), 1)
                else:
                    if n == 4:
                        act.wait_ge(s("zero_ok"), 6)
                    A(pads[:, 1, dh, g * GROUP:(g + 1) * GROUP, 0:SEQ], src.rearrange("p (i t) -> p i t", i=GROUP),
                      ACT.Copy).then_inc(s("qk_act"), 1)
            for j in range(4):
                act.wait_ge(s("v1_mm"), j + 1)
                values_evac(j, 0, "v1_a")
            for st in range(16):
                act.wait_ge(s("s1_mm"), st + 1)
                if st >= 3:
                    act.wait_ge(s("av1_mm"), st - 2)
                for kind in range(2):
                    m = A(E1[:, st % 3, kind].rearrange("p a b c -> p (a b c)"),
                          bank[2 * (st % 2) + kind][:, 0:288], ACT.Exp, scale=SCALE)
                m.then_inc(s("e1_ok"), 1)
            std(3, TILES)

            act.wait_ge(s("lnT_mm"), 3)
            for dh in range(KD):
                A(hT[:, dh, 0:4 * P], bank[3 + dh][:, :], ACT.Copy)
                m = A(hT[:, dh, 4 * P:TPAD], bank[5][:, dh * P:(dh + 1) * P], ACT.Copy)
                m.then_inc(s("lnT_sb"), 1)

            def exp_c(t):
                act.wait_ge(s("sC"), t + 1)
                A(L[:, t, :], L[:, t, :], ACT.Exp).then_inc(s("eC"), 1)

            def slots_tanh(n):
                act.wait_ge(s("xln"), n + 1)
                A(Xs[:, n, :], Xs[:, n, :], ACT.Tanh).then_inc(s("xtan"), 1)

            def slots_turned(n):
                act.wait_ge(s("xtT_mm"), n + 1)
                if n >= 2:
                    act.wait_ge(s("yt_mm"), n - 1)
                A(XTt[:, n % 2].rearrange("p a b -> p (a b)"), bank[n % 2][:, 0:D], ACT.Copy).then_inc(s("xtT_sb"), 1)

            def slots(hf):
                act.wait_ge(s("xvar"), hf + 1)
                A(ln[:, 1, 0:8], ln[:, 0, 0:8], ACT.Sqrt).then_inc(s("xstd"), 1)
                n0 = hf * NPT // 2
                for n in range(n0 - 2, n0 + NPT // 2):
                    if n >= n0:
                        slots_turned(n)
                    if n + 2 < n0 + NPT // 2:
                        slots_tanh(n + 2)

            def weights_turned(t):
                for b in range(4):
                    act.wait_ge(s("ct_mm"), 4 * t + b + 1)
                    if t >= 2 and b == 0:
                        act.wait_ge(s("y_mm"), t - 1)
                    A(CT[:, t % 2, 4 * b:4 * b + 4].rearrange("p a b -> p (a b)"), bank[4 + b][:, :],
                      ACT.Copy).then_inc(s("ct_sb"), 1)

            for u in range(2 * TILES):
                act.wait_ge(s("sD"), u + 1)
                A(Eb[:, u % 4, :], Eb[:, u % 4, :], ACT.Exp).then_inc(s("eD"), 1)
            exp_c(0)
            slots(0)
            exp_c(1)
            weights_turned(0)
            slots(1)
            for t in range(1, TILES):
                if t + 1 < TILES:
                    exp_c(t + 1)
                weights_turned(t)
            std(4, TILES)

        @block.vector
        def _(dve):
            V = nc.vector
            ch = Chain(dve, s("dve_chain"))
            link = ch.link

            def layernorm(n0, signal, counts, k_last):
                added = []
                for b in range(3):
                    dve.wait_ge(s(signal), counts[b])
                    w, k = (2, P) if b < 2 else (1, k_last)
                    added.append(ch.mark(V.tensor_tensor(
                        h[0:k, 2 * b:2 * b + w, :], bank[b][0:k, 0:w * D].rearrange("p (t d) -> p t d", t=w),
                        h[0:k, 2 * b:2 * b + w, :], ALU.add)))
                    if b:
                        statistics(2 * b - 2, 2, added[b - 1])
                statistics(TILES - 1, 1, added[2])
                for t in range(TILES):
                    m = V.bn_aggr(mv[:, t, :], stats[:, t, :])
                link(m)
                rstd(n0, TILES, "var_ok", "std_ok")
                for t in range(TILES):
                    V.tensor_scalar(h[:, t, :], h[:, t, :], mv[:, t, 0:1], ln[:, 2, t:t + 1], ALU.subtract,
                                    ALU.mult).then_inc(s("ln_ok"), 1)

            def statistics(t0, n, after):
                ch.need(after)
                for t in range(t0, t0 + n):
                    m = V.bn_stats(stats[:, t, :], h[:, t, :])
                ch.link(m)

            def rstd(n, w, sv, ss):
                V.tensor_scalar(ln[:, 0, 0:w], mv[:, 0:w, 1], EPS, None, ALU.add).then_inc(s(sv), 1)
                dve.wait_ge(s(ss), n)
                link(V.reciprocal(ln[:, 2, 0:w], ln[:, 1, 0:w]))
                link(V.tensor_tensor(ln[:, 3, 0:w], ln[:, 2, 0:w], ln[:, 2, 0:w], ALU.mult))
                link(V.tensor_tensor(ln[:, 3, 0:w], ln[:, 3, 0:w], ln[:, 0, 0:w], ALU.mult))
                link(V.tensor_scalar(ln[:, 3, 0:w], ln[:, 3, 0:w], -0.5, 1.5, ALU.mult, ALU.add))
                link(V.tensor_tensor(ln[:, 2, 0:w], ln[:, 2, 0:w], ln[:, 3, 0:w], ALU.mult))

            def values_evac(b, im, signal):
                v = bank[b][64 * im:64 * im + 64, :].rearrange("p (j h a d) -> p j h a d", j=2, a=2, d=DH)
                for par in range(2):
                    to = Vbd[64 * par:64 * par + 64, 4 * b:4 * b + 4].rearrange("p (j i) h d -> p j i h d", i=2)
                    m = V.tensor_copy(to[:, :, im, :, DH * par:DH * par + DH], v[:, :, :, par, :])
                m.then_inc(s(signal), 1)

            def expand(to, src):
                return V.tensor_tensor(to, src.unsqueeze(2).broadcast_to([P, GROUP, HH, SEQ]),
                                       c["head"].unsqueeze(1).unsqueeze(3).broadcast_to([P, GROUP, HH, SEQ]),
                                       ALU.mult)

            V.memset(hT[:, :, TOK:TPAD], 0.0).then_inc(s("hT_zero"), 1)
            dve.wait_ge(s("ld_const"), 96)
            link(V.tensor_copy(relp[0:32, :], relf[:, 0, :]))
            link(V.tensor_tensor(relf[:, 1, :], relf[:, 0, :], relp[0:32, :], ALU.subtract))
            link(V.tensor_copy(relp[32:64, :], relf[:, 1, :]))
            link(V.tensor_copy(sm0[0:32, 0, 0].bitcast(BF16)[:, 0:HEADS], relf[:, 1, :]))
            link(V.tensor_tensor(relf[:, 1, :], relf[:, 1, :], sm0[0:32, 0, 0].bitcast(BF16)[:, 0:HEADS],
                                 ALU.subtract))
            V.tensor_copy(relp[64:96, :], relf[:, 1, :]).then_inc(s("relp_ok"), 1)
            dve.wait_ge(s("bias_mm"), 1)
            for hf in range(2):
                k0 = hf * (SEQ // 2)
                m = V.tensor_tensor(
                    bias0[:, :, k0:k0 + SEQ // 2],
                    bank[6 + hf][:, 0:SEQ // 2 * HEADS].rearrange("p (k h) -> p h k", h=HEADS),
                    c["cmask"][:, k0:k0 + SEQ // 2].unsqueeze(1).broadcast_to([P, HEADS, SEQ // 2]), ALU.add)
            m.then_inc(s("bias_ok"), 1)
            for i in range(3):
                dve.wait_ge(s("h_tr"), i + 1)
                w = 2 if i < 2 else 1
                V.tensor_tensor(h[:, 2 * i:2 * i + w, :],
                                bank[4 + i % 2][:, 0:w * D].rearrange("p (t d) -> p t d", t=w),
                                attn_b[:, :].unsqueeze(1).broadcast_to([P, w, D]), ALU.add).then_inc(s("h_res"), 1)
            dve.wait_ge(s("hT_mm"), 4)
            for i in range(3):
                dve.wait_ge(s("k_mm"), i + 1)
                expand(BD[:, i], bank[4 + i][:, 0:GT].rearrange("p (i t) -> p i t", i=GROUP)).then_inc(s("kbd_ok"), 1)
            dve.wait_ge(s("zero_ok"), 4)
            for j in range(4):
                dve.wait_ge(s("v_mm"), j + 1)
                values_evac(j, 1, "v_sb_d")

            def add0(i):
                dve.wait_ge(s("sc_mm"), i + 1)
                if i >= 3:
                    dve.wait_ge(s("p_ok"), i - 2)
                for dh in range(KD):
                    m = V.tensor_tensor(S0[:, i % 3, 8 * dh:8 * dh + 8, :],
                                        bank[2 * (i % 2) + dh][:, 0:288].rearrange("p (h k) -> p h k", h=8),
                                        bias0[:, 8 * dh:8 * dh + 8, :], ALU.add)
                m.then_inc(s("sc_free"), 1)
                dve.wait_ge(s("sc_free"), i + 1)
                V.tensor_reduce(sm0[:, i % 3, 0, :], S0[:, i % 3], AX.X, ALU.max).then_inc(s("mx_ok"), 1)

            def sum0(i):
                dve.wait_ge(s("exp_ok"), i + 1)
                link(V.tensor_reduce(sm0[:, i % 3, 1, :], S0[:, i % 3], AX.X, ALU.add))
                V.reciprocal(sm0[:, i % 3, 2, :], sm0[:, i % 3, 1, :]).then_inc(s("rs_ok"), 1)

            def out0(i):
                dve.wait_ge(s("av_mm"), i + 1)
                V.tensor_copy(oT[:, :, 2 * i * SEQ:2 * (i + 1) * SEQ],
                              bank[6 + i % 2][:, 0:4 * SEQ].rearrange("p (a b) -> p a b", a=KD)).then_inc(s("oT_ok"), 1)

            for i in range(PAIRS + 4):
                if i < PAIRS:
                    add0(i)
                if 1 <= i <= PAIRS:
                    sum0(i - 1)
                if i >= 4:
                    out0(i - 4)
            layernorm(1, "wo_mm", (2, 4, 5), P)
            dve.wait_ge(s("lnT_mm"), 1)
            dve.wait_ge(s("xhi_ok"), 1)
            for dh in range(KD):
                V.tensor_tensor(xlo[:, dh, 0:4 * P], bank[3 + dh][:, :], xhi[:, dh, 0:4 * P], ALU.subtract)
                V.tensor_tensor(xlo[:, dh, 4 * P:TPAD], bank[5][:, dh * P:(dh + 1) * P], xhi[:, dh, 4 * P:TPAD],
                                ALU.subtract).then_inc(s("lnT_sb"), 1)

            dve.wait_ge(s("route_sc"), 1)
            link(V.tensor_tensor(rsc[:, 2], rsc[:, 1], route_b[:, :].unsqueeze(1).broadcast_to([P, TILES, NEXP]),
                                 ALU.add))
            for t in range(TILES):
                m = V.max(rmax[:, t, :], rsc[:, 2, t, :])
            link(m)
            for t in range(TILES):
                m = V.max_index(ridx[:, t, :].bitcast(U32), rmax[:, t, :], rsc[:, 2, t, :])
            link(m)
            link(V.tensor_tensor(req, c["iota"].unsqueeze(1).unsqueeze(3).broadcast_to([P, TILES, NEXP, TOPK]),
                                 ridx[:, :, 0:TOPK].bitcast(U32).unsqueeze(2).broadcast_to([P, TILES, NEXP, TOPK]),
                                 ALU.is_equal))
            link(V.tensor_reduce(rsc[:, 3], req, AX.X, ALU.add))
            V.tensor_copy(maskb, rsc[:, 3]).then_inc(s("mask_ok"), 1)
            link(V.tensor_tensor(rsc[:, 4], rsc[:, 1], rsc[:, 3], ALU.mult))
            link(V.tensor_reduce(rsum[:, 0, :], rsc[:, 4], AX.X, ALU.add))
            link(V.tensor_scalar(rsum[:, 0, :], rsum[:, 0, :], 1e-12, None, ALU.max))
            link(V.reciprocal(rsum[:, 1, :], rsum[:, 0, :]))
            link(V.tensor_tensor(rsc[:, 4], rsc[:, 4], rsum[:, 1, :].unsqueeze(2).broadcast_to([P, TILES, NEXP]),
                                 ALU.mult))
            dve.wait_ge(s("pos_mm"), 1)
            link(V.tensor_scalar(rsc[:, 6], bank[7][:, 0:TILES * NEXP].rearrange("p (t e) -> p t e", t=TILES),
                                 float(CAP), None, ALU.is_lt))
            V.tensor_tensor(rsc[:, 5], rsc[:, 4], rsc[:, 6], ALU.mult).then_inc(s("g_ok"), 1)

            def product(u):
                n = CHUNKS[u % 2][1]
                dve.wait_ge(s("silu_ok"), u + 1)
                if u >= 2:
                    dve.wait_ge(s("m_ok"), u - 1)
                V.tensor_tensor(act_p[:, u % 2, 0:n], bank[4 + 2 * (u % 2)][:, 0:n], act_s[:, u % 2, 0:n],
                                ALU.mult).then_inc(s("p1_ok"), 1)

            def rest(u):
                n = CHUNKS[u % 2][1]
                dve.wait_ge(s("hi_ok"), u + 1)
                V.tensor_tensor(act_r[:, u % 2, 0:n], act_m[:, u % 3, 0:n], parts[:, u % PARTS, 0, 0:n],
                                ALU.subtract).then_inc(s("rest_ok"), 1)

            def low_part(u):
                n = CHUNKS[u % 2][1]
                dve.wait_ge(s("mid_ok"), u + 1)
                V.tensor_tensor(parts[:, u % PARTS, 2, 0:n], act_r[:, u % 2, 0:n], parts[:, u % PARTS, 1, 0:n],
                                ALU.subtract).then_inc(s("parts_ok"), 1)

            for u in range(UNITS + 2):
                if u < UNITS:
                    product(u)
                if u >= 2:
                    low_part(u - 2)
                if 1 <= u <= UNITS:
                    rest(u - 1)
            layernorm(2, "w2_used", (UNITS,) * 3, LAST)

            for n in range(8):
                dve.wait_ge(s("qk_mm"), n + 1)
                if n >= 2:
                    dve.wait_ge(s("rope_ok"), n - 1)
                for w, tab in ((0, "cos"), (1, "sin")):
                    m = V.tensor_tensor(rt[:, n % 2, w].rearrange("p (i t) -> p i t", i=GROUP),
                                        bank[2 * (n % 4) + w][:, 0:GT].rearrange("p (i t) -> p i t", i=GROUP),
                                        c[tab].unsqueeze(1).broadcast_to([P, GROUP, SEQ]), ALU.mult)
                m.then_inc(s("qk_dve"), 1)
            dve.wait_ge(s("zero_ok"), 6)
            for j in range(4):
                dve.wait_ge(s("v1_mm"), j + 1)
                values_evac(j, 1, "v1_d")

            def plain1(u):
                if u >= 2:
                    dve.wait_ge(s("s1_mm"), 4 * (u - 1))
                if u == 0:
                    dve.wait_ge(s("qk_act"), 4)
                expand(BD[:, 2 * (u % 2) + 1], Qs[:, 1, u, :].rearrange("p (i t) -> p i t", i=GROUP))\
                    .then_inc(s("q1d_ok"), 1)

            def out1(st):
                u, j = st // 4, st % 4
                g, dh = u // 2, u % 2
                dve.wait_ge(s("av1_mm"), st + 1)
                link(V.reciprocal(dn1[:, st % 2, :], bank[5 + 2 * (st % 2)][:, 0:2 * SEQ]))
                o = (g * GROUP + 2 * j) * SEQ
                V.tensor_tensor(oT[:, dh, o:o + 2 * SEQ], bank[4 + 2 * (st % 2)][:, 0:2 * SEQ], dn1[:, st % 2, :],
                                ALU.mult).then_inc(s("o1_ok"), 1)

            plain1(0)
            plain1(1)
            for st in range(17):
                if st >= 1:
                    out1(st - 1)
                if st % 4 == 0 and 4 <= st < 12:
                    plain1(st // 4 + 1)
            dve.wait_ge(s("ld_bo1"), 16)
            for t in range(TILES):
                m = V.tensor_tensor(h[:, t, :], h[:, t, :], attn_b[:, :], ALU.add)
            link(m)
            layernorm(3, "wo1_mm", (2, 4, 5), P)

            def max_c(t):
                V.tensor_reduce(smC[:, t, 0, :], L[:, t, :].rearrange("p (n s) -> p s n", s=SP), AX.X,
                                ALU.max).then_inc(s("mC"), 1)

            def sum_c(t):
                dve.wait_ge(s("eC"), t + 1)
                link(V.tensor_reduce(smC[:, t, 1, :], L[:, t, :].rearrange("p (n s) -> p s n", s=SP), AX.X,
                                     ALU.add))
                link(V.reciprocal(smC[:, t, 1, :], smC[:, t, 1, :]))
                V.tensor_tensor(L[:, t, :].rearrange("p (n s) -> p n s", s=SP),
                                L[:, t, :].rearrange("p (n s) -> p n s", s=SP),
                                smC[:, t, 1, :].unsqueeze(1).broadcast_to([P, SE, SP]),
                                ALU.mult).then_inc(s("nC"), 1)

            def add_d(u):
                hf, t = u // TILES, u % TILES
                if u == 0:
                    dve.wait_ge(s("ld_phib"), 16)
                for q in range(2):
                    o = hf * HALF + q * 512
                    dve.wait_ge(s("l_mm"), 2 * u + q + 1)
                    V.tensor_tensor(L[:, t, o:o + 512], bank[(2 * u + q) % 4][:, :], phib[:, o:o + 512],
                                    ALU.add).then_inc(s("l_sb"), 1)
                dve.wait_ge(s("l_sb"), 2 * u + 2)
                V.tensor_reduce(smD[:, u % 2, 0, :],
                                L[:, t, hf * HALF:(hf + 1) * HALF].rearrange("p (n s) -> p n s", s=SP), AX.X,
                                ALU.max).then_inc(s("mD"), 1)

            def sum_d(u):
                dve.wait_ge(s("eD"), u + 1)
                if u >= 2:
                    dve.wait_ge(s("nD"), u - 1)
                link(V.tensor_reduce(smD[:, u % 2, 1, :], Eb[:, u % 4].rearrange("p (n s) -> p n s", s=SP), AX.X,
                                     ALU.add))
                V.reciprocal(smD[:, u % 2, 1, :], smD[:, u % 2, 1, :]).then_inc(s("rD"), 1)

            def slots_stats(hf):
                dve.wait_ge(s("xt_mm"), TILES * (hf + 1))
                for b in range(4):
                    V.tensor_scalar(Xs[:, 8 * hf + 2 * b:8 * hf + 2 * b + 2, :],
                                    bank[4 + b][:, :].rearrange("p (n d) -> p n d", n=2), -33000.0, 65000.0,
                                    ALU.max, ALU.min).then_inc(s("xt_sb"), 1)
                dve.wait_ge(s("xt_sb"), 4 * (hf + 1))

            def slots_norm(hf):
                for n in range(8):
                    m = V.bn_stats(stats[:, n, :], Xs[:, 8 * hf + n, :])
                link(m)
                for n in range(8):
                    m = V.bn_aggr(mv[:, n, :], stats[:, n, :])
                link(m)
                rstd(hf + 1, 8, "xvar", "xstd")
                for n in range(8):
                    m = V.tensor_scalar(Xs[:, 8 * hf + n, :], Xs[:, 8 * hf + n, :], mv[:, n, 0:1], ln[:, 2, n:n + 1],
                                    ALU.subtract, ALU.mult)
                    m.then_inc(s("xln"), 1)
                dve.wait_ge(s("xln"), 8 * (hf + 1))

            def slots_out(hf):
                for n in range(hf * NPT // 2, (hf + 1) * NPT // 2):
                    dve.wait_ge(s("yt_mm"), n + 1)
                    dve.wait_ge(ld_eb[n % 2], 64 * (n // 2 + 1))
                    V.tensor_tensor(Yt[:, n, :], bank[2 + n % 2][:, 0:D], ebr[:, n % 2, :], ALU.add)\
                        .then_inc(s("yt_sb"), 1)

            for u in range(2 * TILES + 1):
                if u == TILES + 2:
                    slots_stats(0)
                if u < 2 * TILES:
                    add_d(u)
                if u >= 1:
                    sum_d(u - 1)
                if u > TILES:
                    max_c(u - TILES - 1)
            slots_norm(0)
            sum_c(0)
            slots_stats(1)
            slots_out(0)
            slots_norm(1)
            sum_c(1)
            slots_out(1)
            for t in range(2, TILES):
                sum_c(t)
            for t in range(TILES):
                k = tiles(t)
                dve.wait_ge(s("y_mm"), t + 1)
                V.tensor_tensor(h[0:k, t, :], bank[t % 2][0:k, 0:D], h[0:k, t, :], ALU.add).then_inc(s("y_sb"), 1)
                dve.wait_ge(s("y_sb"), t + 1)
                link(V.bn_stats(stats[:, t, :], h[:, t, :]))
                link(V.bn_aggr(mv[:, t, :], stats[:, t, :]))
            rstd(4, TILES, "var_ok", "std_ok")
            for t in range(TILES):
                V.tensor_scalar(h[:, t, :], h[:, t, :], mv[:, t, 0:1], ln[:, 2, t:t + 1], ALU.subtract,
                                ALU.mult).then_inc(s("fin_ok"), 1)

        @block.gpsimd
        def _(pool):
            G = nc.gpsimd
            pool.wait_ge(s("hT_mm"), 4)
            G.memset(pads[:, 0, :, :, SEQ:SLOT], 0.0).then_inc(s("zero_ok"), 1)
            G.memset(xTi[:, :, :, SEQ:SLOT], 0.0).then_inc(s("zero_ok"), 1)
            G.memset(Vbd[:, :, :, :], 0.0).then_inc(s("zero_ok"), 1)
            G.memset(oT[:, :, TOK:TPAD], 0.0)
            G.memset(Pb[:, :, :, :, :], 0.0).then_inc(s("zero_ok"), 1)
            for dh in range(KD):
                pool.wait_ge(s("hT_sb"), 2 * (dh + 1))
                G.tensor_copy(xTi[:, dh, :, 0:SEQ], hT[:, dh, 0:TOK].rearrange("p (i t) -> p i t", i=NIMG))\
                    .then_inc(s("xTi_ok"), 1)

            def bcast(v):
                return v.unsqueeze(2).broadcast_to([P, HEADS, SEQ])

            def norm0(i):
                pool.wait_ge(s("rs_ok"), i + 1)
                if i >= 2:
                    pool.wait_ge(s("tr_mm"), i - 1)
                G.tensor_tensor(Pb[:, i % 2].rearrange("p a b c -> p (a b) c")[:, :, 0:SEQ], S0[:, i % 3],
                                bcast(sm0[:, i % 3, 2, :]), ALU.mult).then_inc(s("p_ok"), 1)

            for i in range(PAIRS + 1):
                if i < PAIRS:
                    pool.wait_ge(s("mx_ok"), i + 1)
                    G.tensor_tensor(S0[:, i % 3], S0[:, i % 3], bcast(sm0[:, i % 3, 0, :]), ALU.subtract)\
                        .then_inc(s("sub_ok"), 1)
                if i >= 1:
                    norm0(i - 1)
            for u in range(UNITS):
                e, (t0, n) = u // 2, CHUNKS[u % 2]
                pool.wait_ge(s("p1_ok"), u + 1)
                if u >= 3:
                    pool.wait_ge(s("rest_ok"), u - 2)
                if e == 0:
                    G.tensor_copy(act_m[:, u % 3, 0:n], act_p[:, u % 2, 0:n]).then_inc(s("m_ok"), 1)
                    continue
                pool.wait_ge(ld_g[(e - 1) % 3], 16 * ((e - 1) // 3 + 1))
                G.tensor_tensor(act_m[:, u % 3, 0:n], act_p[:, u % 2, 0:n], gbc[:, (e - 1) % 3, t0:t0 + n],
                                ALU.mult).then_inc(s("m_ok"), 1)
            pool.wait_ge(s("w2_used"), UNITS)
            G.memset(pads[:, :, :, :, SEQ:SLOT], 0.0).then_inc(s("zero_ok"), 1)
            G.memset(xTi[:, :, :, SEQ:SLOT], 0.0)
            G.memset(Vbd[:, :, :, :], 0.0).then_inc(s("zero_ok"), 1)
            for dh in range(KD):
                pool.wait_ge(s("lnT_sb"), 4)
                G.tensor_copy(xTi[:, dh, :, 0:SEQ], hT[:, dh, 0:TOK].rearrange("p (i t) -> p i t", i=NIMG))\
                    .then_inc(s("x1i"), 1)
            for n in range(8):
                g, dh = n % 2, (n // 2) % 2
                pool.wait_ge(s("qk_dve"), n + 1)
                if n < 4:
                    to = Qs[:, 0, 2 * g + dh, :]
                    x, y = rt[:, n % 2, 0], rt[:, n % 2, 1]
                else:
                    to = pads[:, 0, dh, g * GROUP:(g + 1) * GROUP, 0:SEQ]
                    x, y = (rt[:, n % 2, w].rearrange("p (i t) -> p i t", i=GROUP) for w in range(2))
                G.tensor_tensor(to, x, y, ALU.add).then_inc(s("rope_ok"), 1)

            def rotated1(u):
                if u >= 2:
                    pool.wait_ge(s("s1_mm"), 4 * (u - 1))
                if u == 0:
                    pool.wait_ge(s("rope_ok"), 4)
                src = Qs[:, 0, u, :].rearrange("p (i t) -> p i t", i=GROUP)
                G.tensor_tensor(BD[:, 2 * (u % 2)], src.unsqueeze(2).broadcast_to([P, GROUP, HH, SEQ]),
                                c["head"].unsqueeze(1).unsqueeze(3).broadcast_to([P, GROUP, HH, SEQ]),
                                ALU.mult).then_inc(s("q1p_ok"), 1)

            rotated1(0)
            rotated1(1)
            for st in range(16):
                pool.wait_ge(s("e1_ok"), st + 1)
                v = E1[:, st % 3, 0].rearrange("p a b c -> p (a b) c")
                G.tensor_tensor(v, v, c["keep"].unsqueeze(1).broadcast_to([P, 8, SEQ]), ALU.mult)\
                    .then_inc(s("e1m_ok"), 1)
                if st % 4 == 3 and st < 8:
                    rotated1(st // 4 + 2)

            def by_expert(v):
                return v.rearrange("p (n s) -> p n s", s=SP)

            def sub_d(u):
                hf, t = u // TILES, u % TILES
                pool.wait_ge(s("mD"), u + 1)
                if u >= 4:
                    pool.wait_ge(s("xt_mm"), u - 3)
                G.tensor_tensor(by_expert(Eb[:, u % 4]), by_expert(L[:, t, hf * HALF:(hf + 1) * HALF]),
                                smD[:, u % 2, 0, :].unsqueeze(2).broadcast_to([P, HALF // SP, SP]),
                                ALU.subtract).then_inc(s("sD"), 1)

            def norm_d(u):
                pool.wait_ge(s("rD"), u + 1)
                G.tensor_tensor(by_expert(Eb[:, u % 4]), by_expert(Eb[:, u % 4]),
                                smD[:, u % 2, 1, :].unsqueeze(2).broadcast_to([P, HALF // SP, SP]),
                                ALU.mult).then_inc(s("nD"), 1)

            def sub_c(t):
                pool.wait_ge(s("mC"), t + 1)
                pool.wait_ge(s("sD"), TILES + t + 1)
                G.tensor_tensor(by_expert(L[:, t, :]), by_expert(L[:, t, :]),
                                smC[:, t, 0, :].unsqueeze(1).broadcast_to([P, SE, SP]),
                                ALU.subtract).then_inc(s("sC"), 1)

            for u in range(2 * TILES + 1):
                if u < 2 * TILES:
                    sub_d(u)
                if u >= 1:
                    norm_d(u - 1)
                if u == 2 * TILES - 2:
                    sub_c(0)
            for t in range(1, TILES):
                sub_c(t)


def vit_tower(nc, *args):
    build(nc, dict(zip(NAMES, args[:-1])), args[-1])


NAMES = ["patches", "tok_w", "tok_b", "wq0", "wk0", "wv0", "wo0", "bo0", "rel_emb", "gate_w", "route_b", "moe_w",
         "wq1", "wqs1", "wk1", "wks1", "wv1", "wo1", "bo1", "phi_w", "phi_b", "expert_w", "expert_b", "cf", "cb"]


def constants(np):
    cf = np.zeros((P, CF_W), np.float32)
    cb = np.zeros((P, CB_W), np.float32)

    def f(n):
        return cf[:, CF[n][0]:CF[n][0] + CF[n][1]]

    def b(n):
        return cb[:, CB[n][0]:CB[n][0] + CB[n][1]]

    p = np.arange(P)
    f("ident")[:] = np.eye(P)
    f("head")[:] = (p[:, None] // DH == np.arange(HH)[None])
    q, k = p % SLOT, np.arange(SEQ)
    f("cmask")[:] = np.where((k[None] > q[:, None]), -3e38, 0.0)
    f("keep")[:] = (q[:, None] <= k[None])
    f("ones32")[:] = ((p[:, None] // SLOT == np.arange(32)[None] // DH) & (q[:, None] < SEQ))
    f("iota")[:] = np.arange(NEXP)[None]
    d = p % DH
    theta = (np.float32(10000.0) ** (np.float32(-2.0) * ((d // 2).astype(np.float32) - np.float32(1.0)) / np.float32(DH)))
    ang = (np.arange(SEQ, dtype=np.float32)[None] * theta[:, None].astype(np.float32)).astype(np.float32)
    f("cos")[:] = np.cos(ang.astype(np.float64))
    f("sin")[:] = np.sin(ang.astype(np.float64)) * np.where(d % 2 == 0, 1.0, -1.0)[:, None]
    b("before")[:] = (p[:, None] < p[None])
    b("ones")[:] = 1.0
    n = np.maximum(np.arange(SEQ + SLOT - 1) - (SEQ - 1), 0)
    exact = BUCKETS // 2
    large = exact + (np.log(np.maximum(n, 1).astype(np.float32) / exact) / np.log(np.float32(128 / exact))
                     * (BUCKETS - exact)).astype(np.int32)
    bucket = np.where(n < exact, n, np.minimum(large, BUCKETS - 1))
    for part in range(3):
        for i in range(BUCKETS):
            b("bucket")[part * BUCKETS + i] = (bucket == i)
    return cf, cb


def kernel(**inputs):
    import numpy as _np
    import concourse.bacc as _bacc
    from concourse import mybir as _mybir
    from concourse.bass_utils import run_bass_kernel_spmd as _run

    i = {n: _np.asarray(v) for n, v in inputs.items()}
    side = int(round(SEQ ** 0.5))
    px = 16

    def partners(w):
        return w.reshape(D, D // 2, 2)[:, :, ::-1].reshape(D, D)

    def expert(w1, w3, w2):
        n = w1.shape[0]
        up = [w.reshape(n, KD, P, P).transpose(0, 2, 1, 3).reshape(n, P, KD * P) for w in (w1, w3)]
        return _np.concatenate(up + [w2], axis=2)

    qkv = i["L1_attn_w_qkv"].T
    q1, k1, v1 = qkv[:, 0:D], qkv[:, D:2 * D], qkv[:, 2 * D:3 * D]
    cf, cb = constants(_np)
    host = {
        "patches": i["x"].reshape(NIMG, 3, side, px, side, px).transpose(1, 3, 5, 0, 2, 4).reshape(3 * px * px, TOK),
        "tok_w": i["L0_tok_W"], "tok_b": i["L0_tok_b"].reshape(KD, P).T,
        "wq0": i["L0_attn_Wq"], "wk0": i["L0_attn_Wk"], "wv0": i["L0_attn_Wv"], "wo0": i["L0_attn_Wo"],
        "bo0": i["L0_attn_bo"], "rel_emb": i["L0_attn_rel_emb"],
        "gate_w": i["L0_ffn_gate_w"].T, "route_b": i["L0_ffn_bias"],
        "moe_w": _np.concatenate([
            expert(i["L0_ffn_sw1"].T[None], i["L0_ffn_sw3"].T[None], i["L0_ffn_sw2"].T[None]),
            expert(i["L0_ffn_W1"], i["L0_ffn_W3"], i["L0_ffn_W2"])]),
        "wq1": q1, "wqs1": partners(q1), "wk1": k1, "wks1": partners(k1), "wv1": v1,
        "wo1": i["L1_attn_w_out"].T, "bo1": i["L1_attn_b_out"],
        "phi_w": i["L1_ffn_phi_w"].T, "phi_b": i["L1_ffn_phi_b"],
        "expert_w": i["L1_ffn_expert_w"], "expert_b": i["L1_ffn_expert_b"],
        "cf": cf, "cb": cb.astype(i["L0_ffn_gate_w"].dtype),
    }
    nc = _bacc.Bacc("TRN2", target_bir_lowering=False, num_devices=1)
    arrays, args = {}, []
    for name in NAMES:
        v = _np.ascontiguousarray(host[name])
        arrays[f"in_{name}_dram"] = v
        args.append(nc.dram_tensor(f"in_{name}_dram", v.shape, _mybir.dt.from_np(v.dtype), kind="ExternalInput").ap())
    out = nc.dram_tensor("out_0_dram", (TOK, D), _mybir.dt.float32, kind="ExternalOutput").ap()
    vit_tower(nc, *args, out)
    r = _run(nc, [arrays], core_ids=[0])
    return r.results[0]["out_0_dram"].reshape(NIMG, SEQ, D)
```

```python
from contextlib import ExitStack

import concourse.bass as bass
from concourse import mybir

ALU = mybir.AluOpType
ACT = mybir.ActivationFunctionType
AX = mybir.AxisListType
F32 = mybir.dt.float32
F16 = mybir.dt.float16
BF16 = mybir.dt.bfloat16
U32 = mybir.dt.uint32
I32 = mybir.dt.int32

P = 128
NIMG, SEQ = 16, 36
TOK = NIMG * SEQ
D = 256
KD = D // P
TILES = -(-TOK // P)
TPAD = TILES * P
LAST = TOK - (TILES - 1) * P
HEADS, DH = 16, 16
HH = HEADS // KD
GROUP = NIMG // 2
GT = GROUP * SEQ
SLOT = 64
PAIRS = NIMG // 2
PATCH_K = 768 // P
NEXP, TOPK, CAP = 32, 4, 256
CHUNKS = [(0, 256), (256, TOK - 256)]
SE, SP = 64, 32
NP_ = SE * SP
NPT = NP_ // P
HALF = NP_ // 2
PAIRS_OF_SLOTS = NPT // 2
EPS = 1e-5
TURNED = ((0, 2 * P), (2 * P, TPAD))
SCALE = DH ** -0.5
MOE_W = 2 * KD * P + D
MOE_CHUNK = 3
PARTS = 6
MOE_LAG = 6
GATE_LAG = 3
TURN_AT = 6
BIAS_FIRST = 6
PHI_FIRST = 36
UNITS = 2 * (NEXP + 1)
EW_SLOTS = 32
C_SCALE = 1024.0
W_SCALE = 256.0
SPLIT = ((0, 0), (0, 1), (1, 0))
EW_DMA = 2
BUCKETS = 32

CF = {}
CB = {}
_at = 0
for _n, _w in (("ident", P), ("head", HH), ("cmask", SEQ), ("keep", SEQ), ("ones32", 32), ("iota", NEXP),
               ("cos", SEQ), ("sin", SEQ)):
    CF[_n] = (_at, _w)
    _at += _w
CF_W = _at
_at = 0
for _n, _w in (("before", P), ("ones", P), ("bucket", SEQ + SLOT - 1)):
    CB[_n] = (_at, _w)
    _at += _w
CB_W = _at + _at % 2


class Chain:

    def __init__(self, eng, sem):
        self.eng, self.sem, self.n = eng, sem, 0

    def mark(self, ins):
        ins.then_inc(self.sem, 1)
        self.n += 1
        return self.n

    def need(self, n):
        self.eng.wait_ge(self.sem, n)

    def link(self, ins):
        self.need(self.mark(ins))


def build(nc, a, out):
    ctx = ExitStack()
    with ctx:
        def sb(name, shape, dt=F32):
            return ctx.enter_context(nc.sbuf_tensor("sb_" + name, shape, dt))

        def sem(name):
            return ctx.enter_context(nc.semaphore(name))

        bank = [ctx.enter_context(nc.psum_tensor(f"bank{i}", [P, 512], F32)) for i in range(8)]

        cf = sb("cf", [P, CF_W])
        cb = sb("cb", [P, CB_W], BF16)
        c = {n: cf[:, o:o + w] for n, (o, w) in CF.items()}
        cbv = {n: cb[:, o:o + w] for n, (o, w) in CB.items()}
        ident = c["ident"]
        spare = sb("spare", [P, 2])
        tokb = sb("tokb", [P, KD])
        attn_b = sb("attn_b", [P, D])
        route_b = sb("route_b", [P, NEXP])
        relp = sb("relp", [96, HEADS], BF16)
        relf = sb("relf", [BUCKETS, 2, HEADS])
        gate_w = sb("gate_w", [P, KD, NEXP], BF16)
        aw = sb("aw", [P, 6, KD, D])
        phi = sb("phi", [P, KD, NP_])
        h = sb("h", [P, TILES, D])
        hT = sb("hT", [P, KD, TPAD])
        xhi = sb("xhi", [P, KD, TPAD], F16)
        xlo = sb("xlo", [P, KD, TPAD], F16)
        stats = sb("stats", [P, 8, 6])
        mv = sb("mv", [P, 8, 2])
        ln = sb("ln", [P, 5, 16])
        ew = sb("ew", [P, EW_SLOTS, KD, D])
        moe_slots = -(-(NEXP + 1) * MOE_W // (2 * KD * D))
        ew_first = EW_SLOTS - moe_slots
        moe_w = ew[:, ew_first:, :, :].rearrange("p a b c -> p (a b c)").bitcast(BF16)[:, 0:(NEXP + 1) * MOE_W]
        moe_w = moe_w.rearrange("p (e w) -> p e w", w=MOE_W)

        R1 = 24768
        r1 = sb("r1", [P, R1])

        def carve(at, *shape):
            n = 1
            for s in shape:
                n *= s
            v = r1[:, at:at + n]
            assert at + n <= R1, (at, shape)
            if len(shape) > 1:
                names = "abcdef"[:len(shape)]
                v = v.rearrange("p (" + " ".join(names) + ") -> p " + " ".join(names),
                                **{x: s for x, s in zip(names[1:], shape[1:])})
            return v

        patches = carve(0, PATCH_K, TOK)
        tokw = carve(PATCH_K * TOK, PATCH_K, D)
        BD = carve(0, 4, GROUP, HH, SEQ)
        at = 4 * GROUP * HH * SEQ
        Vbd = carve(at, NIMG, HEADS // 2, 32); at += NIMG * HEADS // 2 * 32
        xTi = carve(at, KD, NIMG, SLOT); at += KD * NIMG * SLOT
        pads = carve(at, 2, KD, NIMG, SLOT); at += 2 * KD * NIMG * SLOT
        oT = carve(at, KD, TPAD); at += KD * TPAD
        low = at
        pad1 = at - KD * TPAD - KD * NIMG * SLOT
        S0 = carve(pad1, 3, HEADS, SEQ)
        bias0 = carve(at, HEADS, SEQ); at += HEADS * SEQ
        Pb = carve(at, 2, HEADS // 2, 2, SLOT); at += 2 * HEADS * SLOT
        PT = carve(at, 2, HEADS // 2, 2, SEQ); at += 2 * HEADS * SEQ
        sm0 = carve(at, 3, 3, HEADS); at += 9 * HEADS
        at = low
        Qs = carve(at, 2, 4, GT); at += 8 * GT
        E1 = carve(at, 3, 2, 2, 4, SEQ); at += 12 * 4 * SEQ
        dn1 = xhi[:, 0, 0:8 * SEQ].bitcast(F32).rearrange("p (a b) -> p a b", a=2)
        at = 0
        act_s = carve(at, 2, 320); at += 640
        act_p = carve(at, GATE_LAG + 1, 320); at += (GATE_LAG + 1) * 320
        act_m = carve(at, 3, 320); at += 960
        act_r = carve(at, 2, 320); at += 640
        parts = carve(at, PARTS * 3 * 160).bitcast(BF16).rearrange("p (u j n) -> p u j n", u=PARTS, j=3)
        at += PARTS * 3 * 160
        gbc = carve(at, 3, TOK); at += 3 * TOK
        gT = carve(at, TPAD); at += TPAD
        rsc = carve(at, 8, TILES, NEXP); at += 8 * TILES * NEXP
        rmask = carve(at, TILES * NEXP // 2); at += TILES * NEXP // 2
        rmax = carve(at, TILES, 8); at += 8 * TILES
        ridx = carve(at, TILES, 8); at += 8 * TILES
        req = carve(at, TILES, NEXP, TOPK); at += TILES * NEXP * TOPK
        rsum = carve(at, 2, TILES); at += 2 * TILES
        phib = carve(at, NP_); at += NP_
        maskb = rmask.bitcast(BF16).rearrange("p (t e) -> p t e", t=TILES)
        at = 0
        L = carve(at, TILES, NP_); at += TILES * NP_
        Eb = carve(at, 3, HALF)
        Dp = carve(at + 3 * HALF, 3 * HALF).bitcast(F16).rearrange("p (b j n) -> p b j n", b=3, j=2)
        CT = carve(at, 2 * NPT * P).bitcast(F16).rearrange("p (b j n t) -> p b j n t", b=2, j=2, n=NPT)
        at += 2 * NPT * P
        ebr = [None, carve(at, NPT // 2, D)]; at += NPT // 2 * D
        XTt = carve(at, 2, 2, KD, P); at += 4 * KD * P
        Yt = carve(at, NPT, D); at += NPT * D
        Yp = r1[:, at - NPT * D:at].bitcast(F16).rearrange("p (n j d) -> p n j d", n=NPT, j=2)
        ebr[0] = carve(at, NPT // 2, D); at += NPT // 2 * D
        smD = carve(at, 2, 2, HALF // SP); at += 4 * HALF // SP
        smC = carve(at, TILES, 3, SP); at += 3 * TILES * SP
        Xs = Yt

        AW_SLOTS, PHI_SLOTS, BIAS_SLOTS = 6, NP_ // D, NP_ // (2 * KD * D)
        PARTS_AT = 8
        UPPER_AT = PARTS_AT + PHI_SLOTS

        def slot_floats(e0, e1):
            return ew[:, e0:e1].rearrange("p a b c -> p (a b c)")

        phib3 = slot_floats(0, BIAS_SLOTS).bitcast(BF16)
        phip = slot_floats(PARTS_AT, UPPER_AT).bitcast(F16).rearrange("p (j k n) -> p j k n", j=2, k=KD)
        rt = slot_floats(EW_SLOTS - 4, EW_SLOTS)[:, 0:4 * GT].rearrange("p (b i n) -> p b i n", b=2, i=2)
        phi_slots = phi[:, :, :].rearrange("p k n -> p (k n)").rearrange("p (s k h) -> p s k h", k=KD, h=D)
        hp = hT[:, :, :].rearrange("p k n -> p (k n)").bitcast(F16).rearrange("p (t j d) -> p t j d", t=TILES, j=2)
        PHI_E = PARTS_AT - BIAS_SLOTS
        UPPER_E = PHI_E + PHI_SLOTS
        AW_E = UPPER_E + EW_SLOTS - UPPER_AT
        PARTS_E = AW_E + AW_SLOTS
        AGAIN = PARTS_E + BIAS_SLOTS + PHI_SLOTS

        def expert_at(e, n=1):
            e %= AGAIN
            for first, place, at in ((PARTS_E + BIAS_SLOTS, ew, PARTS_AT), (PARTS_E, ew, 0), (AW_E, aw, 0),
                                     (UPPER_E, ew, UPPER_AT), (PHI_E, phi_slots, 0), (0, ew, BIAS_SLOTS)):
                if e >= first:
                    return place[:, at + e - first:at + e - first + n]

        def units_below(slot):
            return 2 * -(-(slot - ew_first) * KD * D * 2 // MOE_W)

        gT_dram = nc.dram_tensor("gT_scratch", [NEXP, TOK], F32, kind="Internal").ap()

        S = {}

        def s(name):
            if name not in S:
                S[name] = sem(name)
            return S[name]

        for n in ("ld_bo1 ld_const ld_attn0 ld_attn1 ld_phi ld_phib ld_gate ld_out "
                  "dve_chain").split():
            s(n)
        ld_moe = [sem(f"ld_moe{i}") for i in range(-(-(NEXP + 1) // MOE_CHUNK))]
        ld_ew = [sem(f"ld_ew{i}") for i in range(EW_SLOTS // EW_DMA)]
        ld_patch = [sem(f"ld_patch{i}") for i in range(PATCH_K)]
        ld_g = [sem(f"ld_g{i}") for i in range(3)]
        ld_eb = [sem(f"ld_eb{i}") for i in range(2)]
        for n in ("hT_mm hT_sb h_tr h_res xTi_ok zero_ok bias_mm bias_ok relp_ok "
                  "q_mm q_sb k_mm kbd_ok kbd_act v_mm v_sb_a v_sb_d sc_mm sc_free mx_ok sub_ok exp_ok rs_ok p_ok "
                  "tr_mm pt_ok av_mm oT_ok wo_mm var_ok std_ok ln_ok lnT_mm lnT_sb "
                  "route_mm route_sc mask_ok pos_mm g_ok gT_mm gT_sb g_st ab_mm silu_ok p1_ok m_ok hi_ok rest_ok "
                  "mid_ok parts_ok w2_used "
                  "qk_mm qk_act rope_ok x1i q1a_ok q1d_ok q1p_ok v1_mm v1_a v1_d s1_mm e1_ok e1m_ok av1_mm o1_ok "
                  "wo1_mm pC l_mm l_sb mD sD eD rD nD xt_mm xt_sb mC sC eC nC xln xtan xtT_mm xtT_sb "
                  "yh_ok yl_ok ct_lo "
                  "phi_hi phi_lo phib_ok dh_ok dl_ok hh_ok hl_ok spare_ok "
                  "yt_mm yt_sb ct_mm ct_sb y_mm y_sb fin_ok hT_zero xhi_ok").split():
            s(n)

        block = ctx.enter_context(nc.Block())

        def tiles(t):
            return P if t < TILES - 1 else LAST

        def rows(b, t):
            return bank[b + t // 2][:, (t % 2) * D:(t % 2 + 1) * D]

        def eighth(q):
            return q // 4, slice(q % 4 * 512, (q % 4 + 1) * 512)

        def piece(g, dh):
            return dh * 2 + g

        @block.sync
        def _(sp):
            for k in range(PATCH_K):
                sp.dma_start(tokw[:, k, :], a["tok_w"][k * P:(k + 1) * P, :]).then_inc(ld_patch[k], 16)
                sp.dma_start(patches[:, k, :], a["patches"][k * P:(k + 1) * P, :]).then_inc(ld_patch[k], 16)
            sp.dma_start(cf[:, :], a["cf"]).then_inc(s("ld_const"), 16)
            sp.dma_start(cb[:, :], a["cb"]).then_inc(s("ld_const"), 16)
            sp.dma_start(tokb[:, :], a["tok_b"]).then_inc(s("ld_const"), 16)
            sp.dma_start(attn_b[:, :], a["bo0"].partition_broadcast(P)).then_inc(s("ld_const"), 16)
            sp.dma_start(route_b[:, :], a["route_b"].partition_broadcast(P)).then_inc(s("ld_const"), 16)
            sp.dma_start(relf[:, 0, :], a["rel_emb"]).then_inc(s("ld_const"), 16)
            for i, n in enumerate(("wq0", "wk0", "wv0", "wo0")):
                sp.dma_start(aw[:, i], a[n].rearrange("(k p) n -> p k n", p=P)).then_inc(s("ld_attn0"), 16)
            sp.dma_start(gate_w[:, :, :], a["gate_w"].rearrange("(k p) n -> p k n", p=P)).then_inc(s("ld_gate"), 16)
            for i, q in enumerate(ld_moe):
                e0 = i * MOE_CHUNK
                e1 = min(e0 + MOE_CHUNK, NEXP + 1)
                sp.dma_start(moe_w[:, e0:e1, :], a["moe_w"][e0:e1].rearrange("e p w -> p e w")).then_inc(q, 16)
            for k in range(KD):
                sp.dma_start(phi[:, k, :], a["phi_w"][k * P:(k + 1) * P, :]).then_inc(s("ld_phi"), 16)
            sp.wait_ge(s("wo_mm"), TILES)
            sp.wait_ge(s("h_res"), 3)
            for i, n in enumerate(("wq1", "wk1", "wv1", "wo1")):
                sp.dma_start(aw[:, i], a[n].rearrange("(k p) n -> p k n", p=P)).then_inc(s("ld_attn1"), 16)
            sp.wait_ge(s("gT_sb"), 2)
            sp.dma_start(phib[0:96, :], a["phi_b"].partition_broadcast(96)).then_inc(s("ld_phib"), 16)
            sp.dma_start(gT_dram, gT[0:NEXP, 0:TOK]).then_inc(s("g_st"), 16)
            sp.wait_ge(s("g_st"), 16)
            for e in range(NEXP):
                if e >= 3:
                    sp.wait_ge(s("m_ok"), 2 * (e - 1))
                sp.dma_start(gbc[:, e % 3, :], gT_dram[e].partition_broadcast(P)).then_inc(ld_g[e % 3], 16)
            ewd = a["expert_w"].rearrange("n (k p) h -> p n k h", p=P)

            def load_experts(e0, e1):
                for e in range(e0, e1, EW_DMA):
                    i = e // EW_DMA
                    if i >= len(ld_ew):
                        sp.wait_ge(ld_ew[i % len(ld_ew)], 16)
                    sp.dma_start(expert_at(e, EW_DMA).rearrange("p n k h -> p (n k) h"),
                                 ewd[:, e:e + EW_DMA].rearrange("p n k h -> p (n k) h")).then_inc(ld_ew[i % len(ld_ew)], 16)

            def slot_bias(hf):
                for j in range(4):
                    sp.dma_start(ebr[hf][32 * j:32 * j + 32].rearrange("p n d -> p (n d)"),
                                 a["expert_b"][j, hf * NPT // 2 * D:(hf + 1) * NPT // 2 * D]
                                 .partition_broadcast(32)).then_inc(ld_eb[hf], 16)

            sp.wait_ge(s("w2_used"), units_below(PARTS_AT))
            load_experts(0, PHI_E)
            sp.wait_ge(s("phi_lo"), 8)
            load_experts(PHI_E, UPPER_E)
            sp.wait_ge(s("w2_used"), UNITS)
            sp.dma_start(attn_b[:, :], a["bo1"].partition_broadcast(P)).then_inc(s("ld_bo1"), 16)
            load_experts(UPPER_E, AW_E - 4)
            sp.wait_ge(s("rope_ok"), 8)
            load_experts(AW_E - 4, AW_E)
            sp.wait_ge(s("wo1_mm"), TILES)
            load_experts(AW_E, PARTS_E)
            slot_bias(0)
            sp.wait_ge(s("l_mm"), 4 * TILES)
            load_experts(PARTS_E, AGAIN)
            sp.wait_ge(s("xt_mm"), 2 * TILES)
            slot_bias(1)
            for e in range(AGAIN, SE, EW_DMA):
                sp.wait_ge(s("yt_mm"), (e - AGAIN) // 8 + 1)
                load_experts(e, e + EW_DMA)
            outs = 0
            for t in range(TILES):
                sp.wait_ge(s("fin_ok"), t + 1)
                n = tiles(t)
                sp.dma_start(out[t * P:t * P + n, :], h[0:n, t, :]).then_inc(s("ld_out"), 16)
                outs += 16
            sp.wait_ge(s("ld_out"), outs)

        @block.tensor
        def _(pe):
            mm = nc.tensor.matmul

            def proj(b, w, g, dh, src=hT):
                for k in range(KD):
                    m = mm(bank[b][:, 0:GT], aw[:, w, k, dh * P:(dh + 1) * P], src[:, k, g * GT:(g + 1) * GT],
                           start=(k == 0), stop=(k == KD - 1))
                return m

            def values(w, b, signal, first=0):
                for j in range(2):
                    for k in range(KD):
                        m = mm(bank[first + b][:, j * D:(j + 1) * D],
                               xTi[:, k, 4 * b + 2 * j:4 * b + 2 * j + 2, :].rearrange("p i t -> p (i t)"),
                               aw[:, w, k, :], start=(k == 0), stop=(k == KD - 1), skip_group_check=True)
                m.then_inc(s(signal), 1)

            def out_proj(w, signal):
                for t in range(TILES):
                    for k in range(KD):
                        m = mm(rows(0, t), oT[:, k, t * P:(t + 1) * P], aw[:, w, k, :],
                               start=(k == 0), stop=(k == KD - 1), skip_group_check=True)
                    m.then_inc(s(signal), 1)

            def turn(base):
                for t in range(TILES):
                    pe.wait_ge(s("ln_ok"), base + t + 1)
                    for dh in range(KD):
                        to = bank[3 + dh][:, t * P:(t + 1) * P] if t < 2 else bank[5 + dh][:, (t - 2) * P:(t - 1) * P]
                        m = nc.tensor.transpose(to, h[:, t, dh * P:(dh + 1) * P], ident)
                    if t in (1, TILES - 1):
                        m.then_inc(s("lnT_mm"), 1)

            for k in range(PATCH_K):
                pe.wait_ge(ld_patch[k], 32)
                for dh in range(KD):
                    for g in range(2):
                        m = mm(bank[piece(g, dh)][:, 0:GT], tokw[:, k, dh * P:(dh + 1) * P],
                               patches[:, k, g * GT:(g + 1) * GT], start=(k == 0), stop=(k == PATCH_K - 1))
                        if k == PATCH_K - 1:
                            m.then_inc(s("hT_mm"), 1)
            pe.wait_ge(s("relp_ok"), 1)
            ob = CB["bucket"][0]
            for hf in range(2):
                for kk in range(SEQ // 2):
                    k = hf * (SEQ // 2) + kk
                    for im in range(2):
                        m = mm(bank[6 + hf][64 * im:64 * im + 64, kk * HEADS:(kk + 1) * HEADS],
                               cb[0:96, ob + SEQ - 1 - k:ob + SEQ - 1 - k + SLOT], relp[:, :],
                               start=True, stop=True, skip_group_check=True)
            m.then_inc(s("bias_mm"), 1)
            pe.wait_ge(s("hT_sb"), 4)
            pe.wait_ge(s("hT_zero"), 1)
            for t in range(TILES):
                b = 4 + (t // 2) % 2
                if t == 4:
                    pe.wait_ge(s("h_res"), 1)
                for dh in range(KD):
                    m = nc.tensor.transpose(bank[b][:, (t % 2) * D + dh * P:(t % 2) * D + (dh + 1) * P],
                                            hT[:, dh, t * P:(t + 1) * P], ident)
                if t % 2 == 1 or t == 4:
                    m.then_inc(s("h_tr"), 1)
            pe.wait_ge(s("ld_attn0"), 64)
            for dh in range(KD):
                for g in range(2):
                    proj(piece(g, dh), 0, g, dh).then_inc(s("q_mm"), 1)
            pe.wait_ge(s("h_res"), 3)
            pe.wait_ge(s("bias_ok"), 1)
            for g in range(2):
                for dh in range(KD):
                    proj(4 + piece(g, dh), 1, g, dh).then_inc(s("k_mm"), 1)

            def scores0(i):
                if i == 0:
                    pe.wait_ge(s("q_sb"), 4)
                    pe.wait_ge(s("kbd_ok"), 1)
                    pe.wait_ge(s("kbd_act"), 1)
                if i == GROUP // 2:
                    pe.wait_ge(s("kbd_ok"), 2)
                    pe.wait_ge(s("kbd_act"), 2)
                if i >= 2:
                    pe.wait_ge(s("sc_free"), i - 1)
                for dh in range(KD):
                    for im in range(2):
                        img = 2 * i + im
                        m = mm(bank[2 * (i % 2) + dh][64 * im:64 * im + 64, 0:HH * SEQ], pads[:, 0, dh, img, :],
                               BD[:, piece(img // GROUP, dh), img % GROUP].rearrange("p a b -> p (a b)"),
                               start=True, stop=True, skip_group_check=True)
                m.then_inc(s("sc_mm"), 1)

            def turn0(i):
                pe.wait_ge(s("p_ok"), i + 1)
                if i == 0:
                    pe.wait_ge(s("v_sb_a"), 4)
                    pe.wait_ge(s("v_sb_d"), 4)
                if i >= 1:
                    pe.wait_ge(s("pt_ok"), i)
                for hp in range(HEADS // 2):
                    m = nc.tensor.transpose(bank[4 + hp // 4][:, (hp % 4) * P:(hp % 4 + 1) * P],
                                            Pb[:, i % 2, hp].rearrange("p a b -> p (a b)"), ident)
                m.then_inc(s("tr_mm"), 1)

            def apply0(i):
                pe.wait_ge(s("pt_ok"), i + 1)
                if i >= 2:
                    pe.wait_ge(s("oT_ok"), i - 1)
                for im in range(2):
                    for hp in range(HEADS // 2):
                        m = mm(bank[6 + i % 2][32 * (hp % 4):32 * (hp % 4) + 32,
                                              (hp // 4) * 2 * SEQ + im * SEQ:(hp // 4) * 2 * SEQ + (im + 1) * SEQ],
                               Vbd[:, 2 * i + im, hp, :], PT[:, i % 2, hp, im, :],
                               start=True, stop=True, skip_group_check=True)
                m.then_inc(s("av_mm"), 1)

            for i in range(PAIRS + 3):
                if i < PAIRS:
                    scores0(i)
                if i == 1:
                    pe.wait_ge(s("xTi_ok"), 2)
                    for b in range(4):
                        pe.wait_ge(s("kbd_ok"), 1 + b % 2)
                        if b >= 2:
                            pe.wait_ge(s("kbd_act"), b - 1)
                        values(2, b, "v_mm", 4)
                if 2 <= i < PAIRS + 2:
                    turn0(i - 2)
                if i >= 3:
                    apply0(i - 3)
            pe.wait_ge(s("oT_ok"), PAIRS)
            pe.wait_ge(s("sc_free"), PAIRS)
            out_proj(3, "wo_mm")
            turn(0)

            pe.wait_ge(s("lnT_sb"), 4)
            pe.wait_ge(s("ld_gate"), 16)
            for t in range(TILES):
                n = 0
                for part in (xhi, xlo):
                    for k in range(KD):
                        m = mm(bank[7][:, t * NEXP:(t + 1) * NEXP], part[:, k, t * P:(t + 1) * P], gate_w[:, k, :],
                               start=(n == 0), stop=(n == 3), skip_group_check=True)
                        n += 1
            m.then_inc(s("route_mm"), 1)

            def queue_places():
                pe.wait_ge(s("mask_ok"), 1)
                for t in range(TILES):
                    for j in range(t + 1):
                        m = mm(bank[7][:, t * NEXP:(t + 1) * NEXP], cbv["before" if j == t else "ones"],
                               maskb[:, j, :], start=(j == 0), stop=(j == t), skip_group_check=True)
                m.then_inc(s("pos_mm"), 1)

            def turn_gates():
                pe.wait_ge(s("g_ok"), 1)
                for t in range(TILES):
                    b, o = (7, t * P) if t < 4 else (0, 0)
                    m = nc.tensor.transpose(bank[b][0:NEXP, o:o + P], rsc[:, 5, t, :], ident)
                m.then_inc(s("gT_mm"), 1)

            def up(u):
                e, ch = u // 2, u % 2
                t0, n = CHUNKS[ch]
                pe.wait_ge(ld_moe[e // MOE_CHUNK], 16)
                if u >= 2:
                    pe.wait_ge(s("p1_ok"), u - 1)
                for b in range(2):
                    j = 0
                    for part in (xhi, xlo):
                        for k in range(KD):
                            o = (b * KD + k) * P
                            m = mm(bank[3 + 2 * (u % 2) + b][:, 0:n], moe_w[:, e, o:o + P], part[:, k, t0:t0 + n],
                                   start=(j == 0), stop=(j == 3))
                            j += 1
                m.then_inc(s("ab_mm"), 1)

            def down(u):
                e, ch = u // 2, u % 2
                t0, n = CHUNKS[ch]
                pe.wait_ge(s("parts_ok"), u + 1)
                if u == 0:
                    pe.wait_ge(s("gT_sb"), 2)
                for t in range(t0 // P, -(-(t0 + n) // P)):
                    k = tiles(t)
                    for j in range(3):
                        m = mm(rows(0, t)[0:k], parts[:, u % PARTS, j, t * P - t0:t * P - t0 + k],
                               moe_w[:, e, 2 * KD * P:MOE_W], start=(e == 0 and t % 2 == 0 and j == 0),
                               stop=(e == NEXP and j == 2), skip_group_check=True)
                m.then_inc(s("w2_used"), 1)

            for u in range(UNITS + MOE_LAG):
                if u < UNITS:
                    up(u)
                if u == 1:
                    queue_places()
                    turn_gates()
                if u >= MOE_LAG:
                    down(u - MOE_LAG)
            turn(TILES)

            pe.wait_ge(s("lnT_sb"), 8)
            pe.wait_ge(s("ld_attn1"), 64)
            for n in range(8):
                g, dh = n % 2, (n // 2) % 2
                proj(n, n // 4, g, dh).then_inc(s("qk_mm"), 1)
            pe.wait_ge(s("x1i"), 2)
            for b in range(4):
                pe.wait_ge(s("qk_act"), 4 + b + 1)
                values(2, b, "v1_mm", 4)

            def scores1(st):
                u, j = st // 4, st % 4
                g, dh = u // 2, u % 2
                if j == 0:
                    pe.wait_ge(s("rope_ok"), 4 + 2 * dh + g + 1)
                    pe.wait_ge(s("qk_act"), 4 + 2 * dh + g + 1)
                    pe.wait_ge(s("q1a_ok" if u < 2 else "q1d_ok"), u % 2 + 1)
                    pe.wait_ge(s("q1p_ok"), u + 1)
                if st >= 2:
                    pe.wait_ge(s("e1_ok"), st - 1)
                for kind in range(2):
                    bd = BD[:, 2 * (u % 2) + kind]
                    for im in range(2):
                        for par in range(2):
                            img = 2 * j + im
                            m = mm(bank[2 * (st % 2) + kind][64 * par:64 * par + 64, im * 144:(im + 1) * 144],
                                   pads[:, kind, dh, g * GROUP + img, :],
                                   bd[:, img].rearrange("p (a b) c -> p a b c", b=2)[:, :, par, :],
                                   start=True, stop=True, skip_group_check=True)
                m.then_inc(s("s1_mm"), 1)

            def apply1(st):
                u, j = st // 4, st % 4
                g, dh = u // 2, u % 2
                if st == 0:
                    pe.wait_ge(s("v1_a"), 4)
                    pe.wait_ge(s("v1_d"), 4)
                pe.wait_ge(s("e1m_ok"), st + 1)
                if st >= 2:
                    pe.wait_ge(s("o1_ok"), st - 1)
                for hp in range(4):
                    to = bank[4 + 2 * (st % 2)][32 * hp:32 * hp + 32, :]
                    for im in range(2):
                        mm(to[:, im * SEQ:(im + 1) * SEQ], Vbd[:, g * GROUP + 2 * j + im, dh * 4 + hp, :],
                           E1[:, st % 3, 0, im, hp, :], start=True, stop=True, skip_group_check=True)
                    m = mm(bank[5 + 2 * (st % 2)][32 * hp:32 * hp + 32, 0:2 * SEQ], c["ones32"],
                           E1[:, st % 3, 1, :, hp, :], start=True, stop=True, skip_group_check=True)
                m.then_inc(s("av1_mm"), 1)

            for st in range(18):
                if st < 16:
                    scores1(st)
                if st >= 2:
                    apply1(st - 2)
            pe.wait_ge(s("o1_ok"), 16)
            pe.wait_ge(s("e1_ok"), 16)
            out_proj(3, "wo1_mm")
            turn(2 * TILES)

            pe.wait_ge(s("phi_lo"), 8)
            pe.wait_ge(s("phib_ok"), 4)

            def logits(u):
                hf, t = u // TILES, u % TILES
                if u in (0, 2):
                    pe.wait_ge(s("lnT_sb"), 10 + u)
                for q in range(2):
                    n = 2 * u + q
                    if n >= 4:
                        pe.wait_ge(s("l_sb"), n - 3)
                    o = hf * HALF + q * 512
                    mm(bank[n % 4][:, :], cbv["ones"][0:96], phib3[0:96, o:o + 512], start=True, stop=False)
                    for k in range(KD):
                        for i, j in SPLIT:
                            m = mm(bank[n % 4][:, :], (xhi, xlo)[i][:, k, t * P:(t + 1) * P],
                                   phip[:, j, k, o:o + 512], start=False, stop=(k == KD - 1 and i == 1))
                    m.then_inc(s("l_mm"), 1)

            def gather(u):
                hf, t = u // TILES, u % TILES
                pe.wait_ge(s("dl_ok"), u + 1)
                if u == 0:
                    pe.wait_ge(s("hl_ok"), 1)
                if u == TILES:
                    pe.wait_ge(s("xt_sb"), 4)
                k = tiles(t)
                for n in range(8):
                    for i, j in SPLIT:
                        m = mm(bank[4 + n // 2][:, (n % 2) * D:(n % 2 + 1) * D],
                               Dp[0:k, u % 3, i, n * P:(n + 1) * P], hp[0:k, t, j, :],
                               start=(t == 0 and n % 2 == 0 and i + j == 0), stop=(t == TILES - 1 and i == 1),
                               skip_group_check=True)
                m.then_inc(s("xt_mm"), 1)

            def slots_in(m):
                pe.wait_ge(s("xtan"), 2 * m + 2)
                if m >= 2:
                    pe.wait_ge(s("xtT_sb"), m - 1)
                for i in range(2):
                    for k in range(KD):
                        o = (i * KD + k) * P
                        x = nc.tensor.transpose(bank[m % 2][:, o:o + P], Xs[:, 2 * m + i, k * P:(k + 1) * P], ident)
                x.then_inc(s("xtT_mm"), 1)

            def slots_out(m):
                pe.wait_ge(s("xtT_sb"), m + 1)
                if m >= 2:
                    pe.wait_ge(s("yt_sb"), m - 1)
                for e in range(8 * m, 8 * m + 8, EW_DMA):
                    i = e // EW_DMA
                    pe.wait_ge(ld_ew[i % len(ld_ew)], 16 * (i // len(ld_ew) + 1))
                for i in range(2):
                    for k in range(KD):
                        for j in range(4):
                            x = mm(bank[2 + m % 2][32 * j:32 * j + 32, i * D:(i + 1) * D],
                                   XTt[:, m % 2, i, k, 32 * j:32 * j + 32], expert_at(8 * m + 4 * i + j)[:, 0, k, :],
                                   start=(k == 0), stop=(k == KD - 1), skip_group_check=True)
                x.then_inc(s("yt_mm"), 1)

            def turn_weights(t):
                if t == 0:
                    pe.wait_ge(s("xt_sb"), 8)
                pe.wait_ge(s("nC"), t + 1)
                for b in range(4):
                    if t >= 1:
                        pe.wait_ge(s("ct_lo"), 4 * (t - 1) + b + 1)
                    for q in range(4):
                        n = 4 * b + q
                        m = nc.tensor.transpose(bank[4 + b][:, q * P:(q + 1) * P], L[:, t, n * P:(n + 1) * P], ident)
                    m.then_inc(s("ct_mm"), 1)

            def combine(t):
                pe.wait_ge(s("ct_sb"), 4 * (t + 1))
                pe.wait_ge(s("ct_lo"), 4 * (t + 1))
                if t == 0:
                    pe.wait_ge(s("xtT_sb"), PAIRS_OF_SLOTS)
                if t >= 2:
                    pe.wait_ge(s("y_sb"), t - 1)
                k = tiles(t)
                for n in range(NPT):
                    if t == 0 and n % 4 == 0:
                        pe.wait_ge(s("yh_ok"), n // 4 + 1)
                        pe.wait_ge(s("yl_ok"), n // 4 + 1)
                    for i, j in SPLIT:
                        m = mm(bank[t % 2][0:k, 0:D], CT[:, t % 2, i, n, 0:k], Yp[:, n, j, :],
                               start=(n == 0 and i + j == 0), stop=(n == NPT - 1 and i == 1))
                m.then_inc(s("y_mm"), 1)

            for u in range(2 * TILES + 4):
                if u < 2 * TILES:
                    logits(u)
                if u >= 4:
                    gather(u - 4)
            pe.wait_ge(s("l_sb"), 4 * TILES)
            for m in range(PAIRS_OF_SLOTS + 1):
                if m == TURN_AT:
                    turn_weights(0)
                if m < PAIRS_OF_SLOTS:
                    slots_in(m)
                if m > 0:
                    slots_out(m - 1)
            for t in range(1, TILES + 1):
                if t < TILES:
                    turn_weights(t)
                combine(t - 1)

        @block.scalar
        def _(act):
            A = nc.scalar.activation

            def scaled_copies(to, src):
                for hd in range(HH):
                    m = A(to[:, :, hd, :], src, ACT.Copy, scale=c["head"][:, hd:hd + 1])
                return m

            def values_evac(b, im, signal, first=0):
                v = bank[first + b][64 * im:64 * im + 64, :].rearrange("p (j h a d) -> p j h a d", j=2, a=2, d=DH)
                for par in range(2):
                    to = Vbd[64 * par:64 * par + 64, 4 * b:4 * b + 4].rearrange("p (j i) h d -> p j i h d", i=2)
                    m = A(to[:, :, im, :, DH * par:DH * par + DH], v[:, :, :, par, :], ACT.Copy)
                m.then_inc(s(signal), 1)

            roots = [0]

            def std(t0, t1):
                roots[0] += 1
                act.wait_ge(s("var_ok"), roots[0])
                A(ln[:, 1, t0:t1], ln[:, 0, t0:t1], ACT.Sqrt).then_inc(s("std_ok"), 1)

            def high_rows(n):
                for i, (c0, c1) in enumerate(TURNED):
                    act.wait_ge(s("lnT_mm"), 2 * n - 1 + i)
                    for dh in range(KD):
                        A(xhi[:, dh, c0:c1], bank[3 + 2 * i + dh][:, 0:c1 - c0], ACT.Copy).then_inc(s("xhi_ok"), 1)

            def warm(f):
                A(spare[:, 1:2], spare[:, 0:1], f)

            act.wait_ge(s("spare_ok"), 1)
            act.wait_ge(s("ld_const"), 96)
            for i in range(4):
                dh, g = i // 2, i % 2
                act.wait_ge(s("hT_mm"), i + 1)
                A(hT[:, dh, g * GT:(g + 1) * GT], bank[i][:, 0:GT], ACT.Identity,
                  bias=tokb[:, dh:dh + 1]).then_inc(s("hT_sb"), 1)
            for i in range(4):
                dh, g = i // 2, i % 2
                act.wait_ge(s("q_mm"), i + 1)
                if i == 0:
                    act.wait_ge(s("zero_ok"), 4)
                A(pads[:, 0, dh, g * GROUP:(g + 1) * GROUP, 0:SEQ],
                  bank[i][:, 0:GT].rearrange("p (i t) -> p i t", i=GROUP), ACT.Copy, scale=SCALE).then_inc(s("q_sb"), 1)
            for g in range(2):
                act.wait_ge(s("k_mm"), 2 * g + 2)
                scaled_copies(BD[:, piece(g, 1)], bank[4 + piece(g, 1)][:, 0:GT].rearrange("p (i t) -> p i t", i=GROUP))\
                    .then_inc(s("kbd_act"), 1)
            for b in range(4):
                act.wait_ge(s("v_mm"), b + 1)
                values_evac(b, 0, "v_sb_a", 4)

            def evac_pt(i):
                act.wait_ge(s("tr_mm"), i + 1)
                if i >= 2:
                    act.wait_ge(s("av_mm"), i - 1)
                for b in range(2):
                    m = A(PT[:, i % 2, 4 * b:4 * b + 4],
                          bank[4 + b][:, :].rearrange("p (h i q) -> p h i q", h=4, i=2)[:, :, :, 0:SEQ], ACT.Copy)
                m.then_inc(s("pt_ok"), 1)

            for i in range(PAIRS + 2):
                if i < PAIRS:
                    act.wait_ge(s("sub_ok"), i + 1)
                    A(S0[:, i % 3], S0[:, i % 3], ACT.Exp).then_inc(s("exp_ok"), 1)
                if i >= 2:
                    evac_pt(i - 2)
            std(0, 2)
            std(2, 5)
            warm(ACT.Sigmoid)

            high_rows(1)
            act.wait_ge(s("route_mm"), 1)
            A(rsc[:, 1], bank[7][:, 0:TILES * NEXP].rearrange("p (t e) -> p t e", t=TILES),
              ACT.Sigmoid).then_inc(s("route_sc"), 1)

            def unit(u):
                return u % 2, CHUNKS[u % 2][1]

            def silu(u):
                act.wait_ge(s("ab_mm"), u + 1)
                if u >= 2:
                    act.wait_ge(s("p1_ok"), u - 1)
                A(act_s[:, u % 2, 0:unit(u)[1]], bank[3 + 2 * (u % 2)][:, 0:unit(u)[1]], ACT.Silu)\
                    .then_inc(s("silu_ok"), 1)

            def high(u):
                act.wait_ge(s("m_ok"), u + 1)
                if u >= PARTS:
                    act.wait_ge(s("w2_used"), u - PARTS + 1)
                n = unit(u)[1]
                A(parts[:, u % PARTS, 0, 0:n], act_m[:, u % 3, 0:n], ACT.Copy).then_inc(s("hi_ok"), 1)

            def middle(u):
                act.wait_ge(s("rest_ok"), u + 1)
                n = unit(u)[1]
                A(parts[:, u % PARTS, 1, 0:n], act_r[:, u % 2, 0:n], ACT.Copy).then_inc(s("mid_ok"), 1)

            for u in range(UNITS + GATE_LAG + 1):
                if u < UNITS:
                    silu(u)
                if u == 1:
                    act.wait_ge(s("gT_mm"), 1)
                    A(gT[0:NEXP, 0:4 * P], bank[7][0:NEXP, :], ACT.Copy).then_inc(s("gT_sb"), 1)
                    A(gT[0:NEXP, 4 * P:TPAD], bank[0][0:NEXP, 0:P], ACT.Copy).then_inc(s("gT_sb"), 1)
                if GATE_LAG <= u < UNITS + GATE_LAG:
                    high(u - GATE_LAG)
                if u > GATE_LAG:
                    middle(u - GATE_LAG - 1)
                if u in range(PHI_FIRST, PHI_FIRST + 16, 2):
                    k, o = eighth((u - PHI_FIRST) // 2)
                    if u == PHI_FIRST:
                        act.wait_ge(s("ld_phi"), 32)
                        act.wait_ge(s("w2_used"), units_below(UPPER_AT))
                    A(phip[:, 0, k, o], phi[:, k, o], ACT.Copy, scale=W_SCALE).then_inc(s("phi_hi"), 1)
            std(0, 2)
            std(2, 5)
            warm(ACT.Exp)

            for i, (c0, c1) in enumerate(TURNED):
                act.wait_ge(s("lnT_mm"), 3 + i)
                A(hT[:, 0, c0:c1], bank[3 + 2 * i][:, 0:c1 - c0], ACT.Copy).then_inc(s("lnT_sb"), 1)
            def plain1(u):
                src = Qs[:, 1, u, :].rearrange("p (i t) -> p i t", i=GROUP)
                scaled_copies(BD[:, 2 * u + 1], src).then_inc(s("q1a_ok"), 1)

            for n in range(8):
                g, dh = n % 2, (n // 2) % 2
                act.wait_ge(s("qk_mm"), n + 1)
                src = bank[n][:, 0:GT]
                if n < 4:
                    A(Qs[:, 1, 2 * g + dh, :], src, ACT.Copy).then_inc(s("qk_act"), 1)
                else:
                    if n == 4:
                        act.wait_ge(s("qk_act"), 4)
                        plain1(0)
                        act.wait_ge(s("zero_ok"), 6)
                    A(pads[:, 1, dh, g * GROUP:(g + 1) * GROUP, 0:SEQ], src.rearrange("p (i t) -> p i t", i=GROUP),
                      ACT.Copy).then_inc(s("qk_act"), 1)
            for j in range(4):
                act.wait_ge(s("v1_mm"), j + 1)
                values_evac(j, 0, "v1_a", 4)
            plain1(1)
            for st in range(16):
                act.wait_ge(s("s1_mm"), st + 1)
                if st >= 3:
                    act.wait_ge(s("av1_mm"), st - 2)
                for kind in range(2):
                    m = A(E1[:, st % 3, kind].rearrange("p a b c -> p (a b c)"),
                          bank[2 * (st % 2) + kind][:, 0:288], ACT.Exp, scale=SCALE)
                m.then_inc(s("e1_ok"), 1)
            std(0, 2)
            std(2, 5)
            warm(ACT.Exp)

            high_rows(3)
            A(hp[:, :, 0, :], h[:, :, :], ACT.Copy).then_inc(s("hh_ok"), 1)

            def exp_c(t):
                act.wait_ge(s("sC"), t + 1)
                A(L[:, t, :], L[:, t, :], ACT.Exp).then_inc(s("eC"), 1)

            def slots_tanh(n):
                if n % 8 == 0:
                    act.wait_ge(s("xln"), n // 8 + 1)
                A(Xs[:, n, :], Xs[:, n, :], ACT.Tanh, bias=ln[:, 4, n:n + 1], scale=ln[:, 2, n:n + 1])\
                    .then_inc(s("xtan"), 1)

            def slots_turned(m):
                act.wait_ge(s("xtT_mm"), m + 1)
                if m >= 2:
                    act.wait_ge(s("yt_mm"), m - 1)
                A(XTt[:, m % 2].rearrange("p i a b -> p (i a b)"), bank[m % 2][:, :], ACT.Copy)\
                    .then_inc(s("xtT_sb"), 1)

            def slots_high(q):
                act.wait_ge(s("yt_sb"), 2 * q + 2)
                n = slice(4 * (q % 2), 4 * (q % 2) + 4)
                A(Yp[:, 4 * q:4 * q + 4, 0, :], ebr[q // 2][:, n, :], ACT.Copy).then_inc(s("yh_ok"), 1)

            def weights_turned(t):
                for b in range(4):
                    act.wait_ge(s("ct_mm"), 4 * t + b + 1)
                    if t >= 2 and b == 0:
                        act.wait_ge(s("y_mm"), t - 1)
                    A(CT[:, t % 2, 0, 4 * b:4 * b + 4].rearrange("p a b -> p (a b)"), bank[4 + b][:, :],
                      ACT.Copy, scale=C_SCALE).then_inc(s("ct_sb"), 1)

            def logits_out(u):
                hf, t = u // TILES, u % TILES
                for q in range(2):
                    o = hf * HALF + q * 512
                    act.wait_ge(s("l_mm"), 2 * u + q + 1)
                    A(L[:, t, o:o + 512], bank[(2 * u + q) % 4][:, :], ACT.Copy, scale=1.0 / W_SCALE)\
                        .then_inc(s("l_sb"), 1)

            def exp_d(u):
                act.wait_ge(s("sD"), u + 1)
                A(Eb[:, u % 3, :], Eb[:, u % 3, :], ACT.Exp).then_inc(s("eD"), 1)

            def high_d(u):
                act.wait_ge(s("nD"), u + 1)
                if u >= 3:
                    act.wait_ge(s("xt_mm"), u - 2)
                A(Dp[:, u % 3, 0, :], Eb[:, u % 3, :], ACT.Copy, scale=C_SCALE).then_inc(s("dh_ok"), 1)

            for u in range(2 * TILES + 2):
                if u < 2 * TILES:
                    logits_out(u)
                if 1 <= u <= 2 * TILES:
                    exp_d(u - 1)
                if u >= 2:
                    high_d(u - 2)
            for m in range(-2, PAIRS_OF_SLOTS):
                if m >= 0:
                    slots_turned(m)
                if m + 2 < PAIRS_OF_SLOTS:
                    slots_tanh(2 * m + 4)
                    slots_tanh(2 * m + 5)
                if m in (0, 3):
                    exp_c(m // 3)
                if m == 2:
                    slots_high(0)
                if m == 4:
                    slots_high(1)
                if m == TURN_AT - 1:
                    weights_turned(0)
            exp_c(2)
            slots_high(2)
            slots_high(3)
            for t in range(1, TILES):
                if t + 2 < TILES:
                    exp_c(t + 2)
                weights_turned(t)
            std(0, 4)
            std(4, 5)

        @block.vector
        def _(dve):
            V = nc.vector
            ch = Chain(dve, s("dve_chain"))
            link = ch.link

            def layernorm(signal, counts, groups, k_last):
                for b0, b1 in groups:
                    for b in range(b0, b1):
                        dve.wait_ge(s(signal), counts[b])
                        w, k = (2, P) if b < 2 else (1, k_last)
                        link(V.tensor_tensor(
                            h[0:k, 2 * b:2 * b + w, :], bank[b][0:k, 0:w * D].rearrange("p (t d) -> p t d", t=w),
                            h[0:k, 2 * b:2 * b + w, :], ALU.add))
                        for t in range(2 * b, 2 * b + w):
                            m = V.bn_stats(stats[:, t, :], h[:, t, :])
                    link(m)
                    normed(2 * b0, min(2 * b1, TILES), "ln_ok")

            roots = [0]

            def normed(t0, t1, signal):
                for t in range(t0, t1):
                    m = V.bn_aggr(mv[:, t, :], stats[:, t, :])
                link(m)
                roots[0] += 1
                V.tensor_scalar(ln[:, 0, t0:t1], mv[:, t0:t1, 1], EPS, None, ALU.add).then_inc(s("var_ok"), 1)
                dve.wait_ge(s("std_ok"), roots[0])
                link(V.reciprocal(ln[:, 2, t0:t1], ln[:, 1, t0:t1]))
                newton_step(t0, t1)
                for t in range(t0, t1):
                    V.tensor_scalar(h[:, t, :], h[:, t, :], mv[:, t, 0:1], ln[:, 2, t:t + 1], ALU.subtract,
                                    ALU.mult).then_inc(s(signal), 1)

            def turned(n):
                for i, (c0, c1) in enumerate(TURNED):
                    dve.wait_ge(s("lnT_mm"), 2 * n - 1 + i)
                    V.tensor_copy(hT[:, 1, c0:c1], bank[4 + 2 * i][:, 0:c1 - c0]).then_inc(s("lnT_sb"), 1)

            high_count = [0]

            def low_rows():
                for i, (c0, c1) in enumerate(TURNED):
                    for dh in range(KD):
                        high_count[0] += 1
                        dve.wait_ge(s("xhi_ok"), high_count[0])
                        V.tensor_tensor(xlo[:, dh, c0:c1], bank[3 + 2 * i + dh][:, 0:c1 - c0], xhi[:, dh, c0:c1],
                                        ALU.subtract).then_inc(s("lnT_sb"), 1)

            def newton_step(t0, t1):
                v, y, x = ln[:, 0, t0:t1], ln[:, 2, t0:t1], ln[:, 3, t0:t1]
                link(V.tensor_tensor(x, y, y, ALU.mult))
                link(V.scalar_tensor_tensor(x, x, -0.5, v, ALU.mult, ALU.mult))
                link(V.scalar_tensor_tensor(y, x, 1.5, y, ALU.add, ALU.mult))

            def values_evac(b, im, signal, first=0):
                v = bank[first + b][64 * im:64 * im + 64, :].rearrange("p (j h a d) -> p j h a d", j=2, a=2, d=DH)
                for par in range(2):
                    to = Vbd[64 * par:64 * par + 64, 4 * b:4 * b + 4].rearrange("p (j i) h d -> p j i h d", i=2)
                    m = V.tensor_copy(to[:, :, im, :, DH * par:DH * par + DH], v[:, :, :, par, :])
                m.then_inc(s(signal), 1)

            def expand(to, src):
                return V.tensor_tensor(to, src.unsqueeze(2).broadcast_to([P, GROUP, HH, SEQ]),
                                       c["head"].unsqueeze(1).unsqueeze(3).broadcast_to([P, GROUP, HH, SEQ]),
                                       ALU.mult)

            V.memset(spare[:, :], 1.0).then_inc(s("spare_ok"), 1)
            V.memset(hT[:, :, TOK:TPAD], 0.0).then_inc(s("hT_zero"), 1)
            dve.wait_ge(s("ld_const"), 96)
            link(V.tensor_copy(relp[0:32, :], relf[:, 0, :]))
            link(V.tensor_tensor(relf[:, 1, :], relf[:, 0, :], relp[0:32, :], ALU.subtract))
            link(V.tensor_copy(relp[32:64, :], relf[:, 1, :]))
            link(V.tensor_copy(sm0[0:32, 0, 0].bitcast(BF16)[:, 0:HEADS], relf[:, 1, :]))
            link(V.tensor_tensor(relf[:, 1, :], relf[:, 1, :], sm0[0:32, 0, 0].bitcast(BF16)[:, 0:HEADS],
                                 ALU.subtract))
            V.tensor_copy(relp[64:96, :], relf[:, 1, :]).then_inc(s("relp_ok"), 1)
            dve.wait_ge(s("bias_mm"), 1)
            for hf in range(2):
                k0 = hf * (SEQ // 2)
                m = V.tensor_tensor(
                    bias0[:, :, k0:k0 + SEQ // 2],
                    bank[6 + hf][:, 0:SEQ // 2 * HEADS].rearrange("p (k h) -> p h k", h=HEADS),
                    c["cmask"][:, k0:k0 + SEQ // 2].unsqueeze(1).broadcast_to([P, HEADS, SEQ // 2]), ALU.add)
            m.then_inc(s("bias_ok"), 1)
            for i in range(3):
                dve.wait_ge(s("h_tr"), i + 1)
                w = 2 if i < 2 else 1
                V.tensor_tensor(h[:, 2 * i:2 * i + w, :],
                                bank[4 + i % 2][:, 0:w * D].rearrange("p (t d) -> p t d", t=w),
                                attn_b[:, :].unsqueeze(1).broadcast_to([P, w, D]), ALU.add).then_inc(s("h_res"), 1)
            dve.wait_ge(s("hT_mm"), 4)
            for g in range(2):
                dve.wait_ge(s("k_mm"), 2 * g + 1)
                expand(BD[:, piece(g, 0)], bank[4 + piece(g, 0)][:, 0:GT].rearrange("p (i t) -> p i t", i=GROUP))\
                    .then_inc(s("kbd_ok"), 1)
            def add0(i):
                dve.wait_ge(s("sc_mm"), i + 1)
                if i >= 3:
                    dve.wait_ge(s("p_ok"), i - 2)
                for dh in range(KD):
                    m = V.tensor_tensor(S0[:, i % 3, 8 * dh:8 * dh + 8, :],
                                        bank[2 * (i % 2) + dh][:, 0:288].rearrange("p (h k) -> p h k", h=8),
                                        bias0[:, 8 * dh:8 * dh + 8, :], ALU.add)
                m.then_inc(s("sc_free"), 1)
                dve.wait_ge(s("sc_free"), i + 1)
                V.tensor_reduce(sm0[:, i % 3, 0, :], S0[:, i % 3], AX.X, ALU.max).then_inc(s("mx_ok"), 1)

            def sum0(i):
                dve.wait_ge(s("exp_ok"), i + 1)
                link(V.tensor_reduce(sm0[:, i % 3, 1, :], S0[:, i % 3], AX.X, ALU.add))
                V.reciprocal(sm0[:, i % 3, 2, :], sm0[:, i % 3, 1, :]).then_inc(s("rs_ok"), 1)

            def out0(i):
                dve.wait_ge(s("av_mm"), i + 1)
                V.tensor_copy(oT[:, :, 2 * i * SEQ:2 * (i + 1) * SEQ],
                              bank[6 + i % 2][:, 0:4 * SEQ].rearrange("p (a b) -> p a b", a=KD)).then_inc(s("oT_ok"), 1)

            for i in range(PAIRS + 4):
                if i < PAIRS:
                    add0(i)
                if i == 1:
                    dve.wait_ge(s("zero_ok"), 4)
                    for b in range(4):
                        dve.wait_ge(s("v_mm"), b + 1)
                        values_evac(b, 1, "v_sb_d", 4)
                if 1 <= i <= PAIRS:
                    sum0(i - 1)
                if i >= 4:
                    out0(i - 4)
            layernorm("wo_mm", (2, 4, 5), ((0, 1), (1, 3)), P)
            low_rows()

            dve.wait_ge(s("route_sc"), 1)
            link(V.tensor_tensor(rsc[:, 2], rsc[:, 1], route_b[:, :].unsqueeze(1).broadcast_to([P, TILES, NEXP]),
                                 ALU.add))
            for t in range(TILES):
                m = V.max(rmax[:, t, :], rsc[:, 2, t, :])
            link(m)
            for t in range(TILES):
                m = V.max_index(ridx[:, t, :].bitcast(U32), rmax[:, t, :], rsc[:, 2, t, :])
            link(m)
            link(V.tensor_tensor(req, c["iota"].unsqueeze(1).unsqueeze(3).broadcast_to([P, TILES, NEXP, TOPK]),
                                 ridx[:, :, 0:TOPK].bitcast(U32).unsqueeze(2).broadcast_to([P, TILES, NEXP, TOPK]),
                                 ALU.is_equal))
            link(V.tensor_reduce(rsc[:, 3], req, AX.X, ALU.add))
            V.tensor_copy(maskb, rsc[:, 3]).then_inc(s("mask_ok"), 1)
            link(V.tensor_tensor(rsc[:, 4], rsc[:, 1], rsc[:, 3], ALU.mult))
            link(V.tensor_reduce(rsum[:, 0, :], rsc[:, 4], AX.X, ALU.add))
            link(V.tensor_scalar(rsum[:, 0, :], rsum[:, 0, :], 1e-12, None, ALU.max))
            link(V.reciprocal(rsum[:, 1, :], rsum[:, 0, :]))
            link(V.tensor_tensor(rsc[:, 4], rsc[:, 4], rsum[:, 1, :].unsqueeze(2).broadcast_to([P, TILES, NEXP]),
                                 ALU.mult))
            dve.wait_ge(s("pos_mm"), 1)
            link(V.tensor_scalar(rsc[:, 6], bank[7][:, 0:TILES * NEXP].rearrange("p (t e) -> p t e", t=TILES),
                                 float(CAP), None, ALU.is_lt))
            V.tensor_tensor(rsc[:, 5], rsc[:, 4], rsc[:, 6], ALU.mult).then_inc(s("g_ok"), 1)

            def product(u):
                n = CHUNKS[u % 2][1]
                dve.wait_ge(s("silu_ok"), u + 1)
                if u > GATE_LAG:
                    dve.wait_ge(s("m_ok"), u - GATE_LAG)
                V.tensor_tensor(act_p[:, u % (GATE_LAG + 1), 0:n], bank[4 + 2 * (u % 2)][:, 0:n], act_s[:, u % 2, 0:n],
                                ALU.mult).then_inc(s("p1_ok"), 1)

            def rest(u):
                n = CHUNKS[u % 2][1]
                dve.wait_ge(s("hi_ok"), u + 1)
                V.tensor_tensor(act_r[:, u % 2, 0:n], act_m[:, u % 3, 0:n], parts[:, u % PARTS, 0, 0:n],
                                ALU.subtract).then_inc(s("rest_ok"), 1)

            def low_part(u):
                n = CHUNKS[u % 2][1]
                dve.wait_ge(s("mid_ok"), u + 1)
                V.tensor_tensor(parts[:, u % PARTS, 2, 0:n], act_r[:, u % 2, 0:n], parts[:, u % PARTS, 1, 0:n],
                                ALU.subtract).then_inc(s("parts_ok"), 1)

            def split_phi(u):
                if u in range(PHI_FIRST + 1, PHI_FIRST + 17, 2):
                    q = (u - PHI_FIRST) // 2
                    k, o = eighth(q)
                    dve.wait_ge(s("phi_hi"), q + 1)
                    V.scalar_tensor_tensor(phip[:, 1, k, o], phi[:, k, o], W_SCALE, phip[:, 0, k, o], ALU.mult,
                                           ALU.subtract).then_inc(s("phi_lo"), 1)
                step = u - BIAS_FIRST
                if 0 <= step < 28:
                    step, o = step % 7, slice(step // 7 * 512, (step // 7 + 1) * 512)
                    rows = slice(*((0, 96), (0, 96), (0, 96), (32, 64), (64, 96), (64, 96), (64, 96))[step])
                    b, part = phib[rows, o], phib3[rows, o]
                    if u == BIAS_FIRST:
                        dve.wait_ge(s("ld_phib"), 16)
                    if step == 0:
                        link(V.tensor_scalar(b, b, W_SCALE / 32, None, ALU.mult))
                    elif step in (2, 5):
                        link(V.tensor_tensor(b, b, part, ALU.subtract))
                    elif step < 6:
                        link(V.tensor_copy(part, b))
                    else:
                        V.tensor_copy(part, b).then_inc(s("phib_ok"), 1)

            for u in range(UNITS + GATE_LAG + 1):
                if u < UNITS:
                    product(u)
                if u > GATE_LAG:
                    low_part(u - GATE_LAG - 1)
                if GATE_LAG <= u < UNITS + GATE_LAG:
                    rest(u - GATE_LAG)
                split_phi(u)
            layernorm("w2_used", (UNITS - 1, UNITS, UNITS), ((0, 1), (1, 3)), LAST)
            turned(2)

            swap = [i ^ 1 for i in range(32)]

            def by_image(v):
                return v.rearrange("p (i t) -> p i t", i=GROUP)

            for n in range(8):
                g, dh = n % 2, (n // 2) % 2
                dve.wait_ge(s("qk_act"), n + 1)
                if n < 4:
                    src, to = by_image(Qs[:, 1, 2 * g + dh, :]), by_image(Qs[:, 0, 2 * g + dh, :])
                else:
                    src, to = (pads[:, kind, dh, g * GROUP:(g + 1) * GROUP, 0:SEQ] for kind in (1, 0))
                if n == 4:
                    dve.wait_ge(s("zero_ok"), 6)
                swapped, turned_x = by_image(rt[:, n % 2, 0]), by_image(rt[:, n % 2, 1])
                V.tensor_tensor(turned_x, src, c["cos"].unsqueeze(1).broadcast_to([P, GROUP, SEQ]), ALU.mult)
                link(V.stream_shuffle(swapped, src, swap))
                link(V.tensor_tensor(swapped, swapped, c["sin"].unsqueeze(1).broadcast_to([P, GROUP, SEQ]), ALU.mult))
                V.tensor_tensor(to, turned_x, swapped, ALU.add).then_inc(s("rope_ok"), 1)
            dve.wait_ge(s("zero_ok"), 6)
            for j in range(4):
                dve.wait_ge(s("v1_mm"), j + 1)
                values_evac(j, 1, "v1_d", 4)

            def plain1(u):
                dve.wait_ge(s("s1_mm"), 4 * (u - 1))
                expand(BD[:, 2 * (u % 2) + 1], Qs[:, 1, u, :].rearrange("p (i t) -> p i t", i=GROUP))\
                    .then_inc(s("q1d_ok"), 1)

            def out1(st):
                u, j = st // 4, st % 4
                g, dh = u // 2, u % 2
                dve.wait_ge(s("av1_mm"), st + 1)
                link(V.reciprocal(dn1[:, st % 2, :], bank[5 + 2 * (st % 2)][:, 0:2 * SEQ]))
                o = (g * GROUP + 2 * j) * SEQ
                V.tensor_tensor(oT[:, dh, o:o + 2 * SEQ], bank[4 + 2 * (st % 2)][:, 0:2 * SEQ], dn1[:, st % 2, :],
                                ALU.mult).then_inc(s("o1_ok"), 1)

            for st in range(17):
                if st >= 1:
                    out1(st - 1)
                if st in (4, 8):
                    plain1(st // 4 + 1)
                if st in range(6, 6 + TILES):
                    if st == 6:
                        dve.wait_ge(s("ld_bo1"), 16)
                    biased = ch.mark(V.tensor_tensor(h[:, st - 6, :], h[:, st - 6, :], attn_b[:, :], ALU.add))
            ch.need(biased)
            layernorm("wo1_mm", (2, 4, 5), ((0, 1), (1, 3)), P)
            low_rows()

            def max_c(t, hf):
                V.tensor_reduce(smC[:, t, 2 * hf, :],
                                L[:, t, hf * HALF:(hf + 1) * HALF].rearrange("p (n s) -> p s n", s=SP), AX.X,
                                ALU.max).then_inc(s("pC"), 1)
                if hf:
                    dve.wait_ge(s("pC"), TILES + t + 1)
                    V.tensor_tensor(smC[:, t, 0, :], smC[:, t, 0, :], smC[:, t, 2, :], ALU.max).then_inc(s("mC"), 1)

            def sum_c(t):
                dve.wait_ge(s("eC"), t + 1)
                link(V.tensor_reduce(smC[:, t, 1, :], L[:, t, :].rearrange("p (n s) -> p s n", s=SP), AX.X,
                                     ALU.add))
                return ch.mark(V.reciprocal(smC[:, t, 1, :], smC[:, t, 1, :]))

            def norm_c(t, summed):
                ch.need(summed)
                V.tensor_tensor(L[:, t, :].rearrange("p (n s) -> p n s", s=SP),
                                L[:, t, :].rearrange("p (n s) -> p n s", s=SP),
                                smC[:, t, 1, :].unsqueeze(1).broadcast_to([P, SE, SP]),
                                ALU.mult).then_inc(s("nC"), 1)

            def max_d(u):
                hf, t = u // TILES, u % TILES
                dve.wait_ge(s("l_sb"), 2 * u + 2)
                V.tensor_reduce(smD[:, u % 2, 0, :],
                                L[:, t, hf * HALF:(hf + 1) * HALF].rearrange("p (n s) -> p n s", s=SP), AX.X,
                                ALU.max).then_inc(s("mD"), 1)

            def sum_d(u):
                dve.wait_ge(s("eD"), u + 1)
                if u >= 2:
                    dve.wait_ge(s("nD"), u - 1)
                link(V.tensor_reduce(smD[:, u % 2, 1, :], Eb[:, u % 3].rearrange("p (n s) -> p n s", s=SP), AX.X,
                                     ALU.add))
                V.reciprocal(smD[:, u % 2, 1, :], smD[:, u % 2, 1, :]).then_inc(s("rD"), 1)

            def low_d(u):
                dve.wait_ge(s("dh_ok"), u + 1)
                V.scalar_tensor_tensor(Dp[:, u % 3, 1, :], Eb[:, u % 3, :], C_SCALE, Dp[:, u % 3, 0, :], ALU.mult,
                                       ALU.subtract).then_inc(s("dl_ok"), 1)

            def slots_clip(hf):
                dve.wait_ge(s("xt_mm"), TILES * (hf + 1))
                for b in range(4):
                    V.tensor_scalar(Xs[:, 8 * hf + 2 * b:8 * hf + 2 * b + 2, :],
                                    bank[4 + b][:, :].rearrange("p (n d) -> p n d", n=2),
                                    -33000.0 * C_SCALE, 65000.0 * C_SCALE, ALU.max, ALU.min).then_inc(s("xt_sb"), 1)

            def slots_stats(n0, n1):
                dve.wait_ge(s("xt_sb"), 4 * (n0 // 8 + 1))
                for n in range(n0, n1):
                    m = V.bn_stats(stats[:, n % 8, :], Xs[:, n, :])
                return ch.mark(m)

            def slots_variance(hf, last):
                ch.need(last)
                for n in range(8):
                    m = V.bn_aggr(mv[:, n, :], stats[:, n, :])
                link(m)
                link(V.tensor_scalar(ln[:, 0, 8 * hf:8 * hf + 8], mv[:, 0:8, 1], EPS * C_SCALE ** 2, None, ALU.add))

            def slots_norm(hf):
                o = slice(8 * hf, 8 * hf + 8)
                guess = ln[:, 2, o].bitcast(I32)
                link(V.tensor_scalar(guess, ln[:, 0, o].bitcast(I32), 1, None, ALU.logical_shift_right))
                link(V.tensor_scalar(guess, guess, -1, 0x5F3759DF, ALU.mult, ALU.add))
                for _ in range(3):
                    newton_step(8 * hf, 8 * hf + 8)
                V.scalar_tensor_tensor(ln[:, 4, o], mv[:, 0:8, 0], -1.0, ln[:, 2, o], ALU.mult, ALU.mult)\
                    .then_inc(s("xln"), 1)

            def slots_out(m):
                hf = m // 4
                dve.wait_ge(s("yt_mm"), m + 1)
                if m % 4 == 0:
                    dve.wait_ge(ld_eb[hf], 64)
                b = ebr[hf][:, 2 * (m % 4):2 * (m % 4) + 2, :].rearrange("p n d -> p (n d)")
                V.tensor_tensor(b, bank[2 + m % 2][:, :], b, ALU.add).then_inc(s("yt_sb"), 1)

            for u in range(2 * TILES + 2):
                if u == TILES + 4:
                    slots_clip(0)
                if u < 2 * TILES:
                    max_d(u)
                if 1 <= u <= 2 * TILES:
                    sum_d(u - 1)
                if u >= 2:
                    low_d(u - 2)
                if u < 2 * TILES - 3:
                    max_c(u % TILES, u // TILES)
                if u == 2 * TILES:
                    last = slots_stats(0, 8)
            slots_variance(0, last)
            slots_norm(0)
            max_c(TILES - 3, 1)

            def weights_low(t):
                for b in range(4):
                    dve.wait_ge(s("ct_sb"), 4 * t + b + 1)
                    n = slice(4 * b, 4 * b + 4)
                    V.scalar_tensor_tensor(CT[:, t % 2, 1, n].rearrange("p a b -> p (a b)"), bank[4 + b][:, :],
                                           C_SCALE, CT[:, t % 2, 0, n].rearrange("p a b -> p (a b)"), ALU.mult,
                                           ALU.subtract).then_inc(s("ct_lo"), 1)

            slots_clip(1)
            slots_variance(1, slots_stats(8, 16))
            slots_norm(1)
            for m in range(PAIRS_OF_SLOTS):
                slots_out(m)
                if m == 0:
                    max_c(TILES - 2, 1)
                if m == 2:
                    max_c(TILES - 1, 1)
                if m in (1, 3):
                    summed = sum_c(m // 2)
                if m in (2, 4):
                    norm_c(m // 2 - 1, summed)
                if m == TURN_AT - 1:
                    weights_low(0)
            norm_c(2, sum_c(2))
            for t in range(TILES):
                k = tiles(t)
                if t + 1 < TILES:
                    weights_low(t + 1)
                if t + 3 < TILES:
                    norm_c(t + 3, sum_c(t + 3))
                dve.wait_ge(s("y_mm"), t + 1)
                V.scalar_tensor_tensor(h[0:k, t, :], bank[t % 2][0:k, 0:D], 1.0 / C_SCALE, h[0:k, t, :], ALU.mult,
                                       ALU.add).then_inc(s("y_sb"), 1)
                dve.wait_ge(s("y_sb"), t + 1)
                m = V.bn_stats(stats[:, t, :], h[:, t, :])
                if t == TILES - 2:
                    link(m)
                    normed(0, t + 1, "fin_ok")
            link(m)
            normed(TILES - 1, TILES, "fin_ok")

        @block.gpsimd
        def _(pool):
            G = nc.gpsimd
            pool.wait_ge(s("hT_mm"), 4)
            G.memset(pads[:, 0, :, :, SEQ:SLOT], 0.0).then_inc(s("zero_ok"), 1)
            G.memset(xTi[:, :, :, SEQ:SLOT], 0.0).then_inc(s("zero_ok"), 1)
            G.memset(Vbd[:, :, :, :], 0.0).then_inc(s("zero_ok"), 1)
            G.memset(oT[:, :, TOK:TPAD], 0.0)
            G.memset(Pb[:, :, :, :, :], 0.0).then_inc(s("zero_ok"), 1)
            for dh in range(KD):
                pool.wait_ge(s("hT_sb"), 2 * (dh + 1))
                G.tensor_copy(xTi[:, dh, :, 0:SEQ], hT[:, dh, 0:TOK].rearrange("p (i t) -> p i t", i=NIMG))\
                    .then_inc(s("xTi_ok"), 1)

            def bcast(v):
                return v.unsqueeze(2).broadcast_to([P, HEADS, SEQ])

            def norm0(i):
                pool.wait_ge(s("rs_ok"), i + 1)
                if i >= 2:
                    pool.wait_ge(s("tr_mm"), i - 1)
                G.tensor_tensor(Pb[:, i % 2].rearrange("p a b c -> p (a b) c")[:, :, 0:SEQ], S0[:, i % 3],
                                bcast(sm0[:, i % 3, 2, :]), ALU.mult).then_inc(s("p_ok"), 1)

            for i in range(PAIRS + 1):
                if i < PAIRS:
                    pool.wait_ge(s("mx_ok"), i + 1)
                    G.tensor_tensor(S0[:, i % 3], S0[:, i % 3], bcast(sm0[:, i % 3, 0, :]), ALU.subtract)\
                        .then_inc(s("sub_ok"), 1)
                if i >= 1:
                    norm0(i - 1)
            for u in range(UNITS):
                e, (t0, n) = u // 2, CHUNKS[u % 2]
                pool.wait_ge(s("p1_ok"), u + 1)
                if u >= 3:
                    pool.wait_ge(s("rest_ok"), u - 2)
                if e == 0:
                    G.tensor_copy(act_m[:, u % 3, 0:n], act_p[:, u % (GATE_LAG + 1), 0:n]).then_inc(s("m_ok"), 1)
                    continue
                pool.wait_ge(ld_g[(e - 1) % 3], 16 * ((e - 1) // 3 + 1))
                G.tensor_tensor(act_m[:, u % 3, 0:n], act_p[:, u % (GATE_LAG + 1), 0:n], gbc[:, (e - 1) % 3, t0:t0 + n],
                                ALU.mult).then_inc(s("m_ok"), 1)
            pool.wait_ge(s("w2_used"), UNITS)
            G.memset(pads[:, :, :, :, SEQ:SLOT], 0.0).then_inc(s("zero_ok"), 1)
            G.memset(xTi[:, :, :, SEQ:SLOT], 0.0)
            G.memset(Vbd[:, :, :, :], 0.0).then_inc(s("zero_ok"), 1)
            for dh in range(KD):
                pool.wait_ge(s("lnT_sb"), 8)
                G.tensor_copy(xTi[:, dh, :, 0:SEQ], hT[:, dh, 0:TOK].rearrange("p (i t) -> p i t", i=NIMG))\
                    .then_inc(s("x1i"), 1)

            def rotated1(u):
                if u >= 2:
                    pool.wait_ge(s("s1_mm"), 4 * (u - 1))
                pool.wait_ge(s("rope_ok"), (1, 3, 2, 4)[u])
                src = Qs[:, 0, u, :].rearrange("p (i t) -> p i t", i=GROUP)
                G.tensor_tensor(BD[:, 2 * (u % 2)], src.unsqueeze(2).broadcast_to([P, GROUP, HH, SEQ]),
                                c["head"].unsqueeze(1).unsqueeze(3).broadcast_to([P, GROUP, HH, SEQ]),
                                ALU.mult).then_inc(s("q1p_ok"), 1)

            rotated1(0)
            rotated1(1)
            for st in range(16):
                pool.wait_ge(s("e1_ok"), st + 1)
                v = E1[:, st % 3, 0].rearrange("p a b c -> p (a b) c")
                G.tensor_tensor(v, v, c["keep"].unsqueeze(1).broadcast_to([P, 8, SEQ]), ALU.mult)\
                    .then_inc(s("e1m_ok"), 1)
                if st % 4 == 3 and st < 8:
                    rotated1(st // 4 + 2)

            def by_expert(v):
                return v.rearrange("p (n s) -> p n s", s=SP)

            def sub_d(u):
                hf, t = u // TILES, u % TILES
                pool.wait_ge(s("mD"), u + 1)
                if u >= 3:
                    pool.wait_ge(s("dl_ok"), u - 2)
                G.tensor_tensor(by_expert(Eb[:, u % 3]), by_expert(L[:, t, hf * HALF:(hf + 1) * HALF]),
                                smD[:, u % 2, 0, :].unsqueeze(2).broadcast_to([P, HALF // SP, SP]),
                                ALU.subtract).then_inc(s("sD"), 1)

            def norm_d(u):
                pool.wait_ge(s("rD"), u + 1)
                G.tensor_tensor(by_expert(Eb[:, u % 3]), by_expert(Eb[:, u % 3]),
                                smD[:, u % 2, 1, :].unsqueeze(2).broadcast_to([P, HALF // SP, SP]),
                                ALU.mult).then_inc(s("nD"), 1)

            def sub_c(t):
                pool.wait_ge(s("mC"), t + 1)
                pool.wait_ge(s("sD"), TILES + t + 1)
                G.tensor_tensor(by_expert(L[:, t, :]), by_expert(L[:, t, :]),
                                smC[:, t, 0, :].unsqueeze(1).broadcast_to([P, SE, SP]),
                                ALU.subtract).then_inc(s("sC"), 1)

            pool.wait_ge(s("hh_ok"), 1)
            G.tensor_tensor(hp[:, :, 1, :], h[:, :, :], hp[:, :, 0, :], ALU.subtract).then_inc(s("hl_ok"), 1)
            for u in range(2 * TILES + 1):
                if u < 2 * TILES:
                    sub_d(u)
                if u >= 1:
                    norm_d(u - 1)

            def slots_low(q):
                pool.wait_ge(s("yh_ok"), q + 1)
                n = slice(4 * (q % 2), 4 * (q % 2) + 4)
                G.tensor_tensor(Yp[:, 4 * q:4 * q + 4, 1, :], ebr[q // 2][:, n, :], Yp[:, 4 * q:4 * q + 4, 0, :],
                                ALU.subtract).then_inc(s("yl_ok"), 1)

            for t in range(TILES):
                sub_c(t)
            for q in range(4):
                slots_low(q)


def vit_tower(nc, *args):
    build(nc, dict(zip(NAMES, args[:-1])), args[-1])


NAMES = ["patches", "tok_w", "tok_b", "wq0", "wk0", "wv0", "wo0", "bo0", "rel_emb", "gate_w", "route_b", "moe_w",
         "wq1", "wk1", "wv1", "wo1", "bo1", "phi_w", "phi_b", "expert_w", "expert_b", "cf", "cb"]


def constants(np):
    cf = np.zeros((P, CF_W), np.float32)
    cb = np.zeros((P, CB_W), np.float32)

    def f(n):
        return cf[:, CF[n][0]:CF[n][0] + CF[n][1]]

    def b(n):
        return cb[:, CB[n][0]:CB[n][0] + CB[n][1]]

    p = np.arange(P)
    f("ident")[:] = np.eye(P)
    f("head")[:] = (p[:, None] // DH == np.arange(HH)[None])
    q, k = p % SLOT, np.arange(SEQ)
    f("cmask")[:] = np.where((k[None] > q[:, None]), -3e38, 0.0)
    f("keep")[:] = (q[:, None] <= k[None])
    f("ones32")[:] = ((p[:, None] // SLOT == np.arange(32)[None] // DH) & (q[:, None] < SEQ))
    f("iota")[:] = np.arange(NEXP)[None]
    d = p % DH
    theta = (np.float32(10000.0) ** (np.float32(-2.0) * ((d // 2).astype(np.float32) - np.float32(1.0)) / np.float32(DH)))
    ang = (np.arange(SEQ, dtype=np.float32)[None] * theta[:, None].astype(np.float32)).astype(np.float32)
    f("cos")[:] = np.cos(ang.astype(np.float64))
    f("sin")[:] = np.sin(ang.astype(np.float64)) * np.where(d % 2 == 0, 1.0, -1.0)[:, None]
    b("before")[:] = (p[:, None] < p[None])
    b("ones")[:] = 1.0
    n = np.maximum(np.arange(SEQ + SLOT - 1) - (SEQ - 1), 0)
    exact = BUCKETS // 2
    large = exact + (np.log(np.maximum(n, 1).astype(np.float32) / exact) / np.log(np.float32(128 / exact))
                     * (BUCKETS - exact)).astype(np.int32)
    bucket = np.where(n < exact, n, np.minimum(large, BUCKETS - 1))
    for part in range(3):
        for i in range(BUCKETS):
            b("bucket")[part * BUCKETS + i] = (bucket == i)
    return cf, cb


def kernel(**inputs):
    import numpy as _np
    import concourse.bacc as _bacc
    from concourse import mybir as _mybir
    from concourse.bass_utils import run_bass_kernel_spmd as _run

    i = {n: _np.asarray(v) for n, v in inputs.items()}
    side = int(round(SEQ ** 0.5))
    px = 16

    def expert(w1, w3, w2):
        n = w1.shape[0]
        up = [w.reshape(n, KD, P, P).transpose(0, 2, 1, 3).reshape(n, P, KD * P) for w in (w1, w3)]
        return _np.concatenate(up + [w2], axis=2)

    qkv = i["L1_attn_w_qkv"].T
    q1, k1, v1 = qkv[:, 0:D], qkv[:, D:2 * D], qkv[:, 2 * D:3 * D]
    cf, cb = constants(_np)
    host = {
        "patches": i["x"].reshape(NIMG, 3, side, px, side, px).transpose(1, 3, 5, 0, 2, 4).reshape(3 * px * px, TOK),
        "tok_w": i["L0_tok_W"], "tok_b": i["L0_tok_b"].reshape(KD, P).T,
        "wq0": i["L0_attn_Wq"], "wk0": i["L0_attn_Wk"], "wv0": i["L0_attn_Wv"], "wo0": i["L0_attn_Wo"],
        "bo0": i["L0_attn_bo"], "rel_emb": i["L0_attn_rel_emb"],
        "gate_w": i["L0_ffn_gate_w"].T, "route_b": i["L0_ffn_bias"],
        "moe_w": _np.concatenate([
            expert(i["L0_ffn_sw1"].T[None], i["L0_ffn_sw3"].T[None], i["L0_ffn_sw2"].T[None]),
            expert(i["L0_ffn_W1"], i["L0_ffn_W3"], i["L0_ffn_W2"])]),
        "wq1": q1, "wk1": k1, "wv1": v1,
        "wo1": i["L1_attn_w_out"].T, "bo1": i["L1_attn_b_out"],
        "phi_w": i["L1_ffn_phi_w"].T, "phi_b": i["L1_ffn_phi_b"],
        "expert_w": i["L1_ffn_expert_w"], 
        "expert_b": i["L1_ffn_expert_b"].reshape(NPT, 4, D).transpose(1, 0, 2).reshape(4, NPT * D),
        "cf": cf, "cb": cb.astype(i["L0_ffn_gate_w"].dtype),
    }
    nc = _bacc.Bacc("TRN2", target_bir_lowering=False, num_devices=1)
    arrays, args = {}, []
    for name in NAMES:
        v = _np.ascontiguousarray(host[name])
        arrays[f"in_{name}_dram"] = v
        args.append(nc.dram_tensor(f"in_{name}_dram", v.shape, _mybir.dt.from_np(v.dtype), kind="ExternalInput").ap())
    out = nc.dram_tensor("out_0_dram", (TOK, D), _mybir.dt.float32, kind="ExternalOutput").ap()
    vit_tower(nc, *args, out)
    r = _run(nc, [arrays], core_ids=[0])
    return r.results[0]["out_0_dram"].reshape(NIMG, SEQ, D)
```
